# Optimizing a Trainium2 kernel written in Bass

```python
import numpy as np
import jax
import jax.numpy as jnp

def _softmax(x, axis=-1):
    return jax.nn.softmax(x, axis=axis)

def _gelu(x):
    return jax.nn.gelu(x, approximate=True)

def _silu(x):
    return jax.nn.silu(x)

def _sigmoid(x):
    return jax.nn.sigmoid(x)

def _layernorm(x, axis=-1, eps=1e-05):
    m = jnp.mean(x, axis=axis, keepdims=True)
    v = jnp.var(x, axis=axis, keepdims=True)
    return (x - m) / jnp.sqrt(v + eps)

def _scatter_add(tgt, idx, src, axis=0):
    return tgt.at[idx].add(src)

def _segment_sum(src, seg, n):
    return jax.ops.segment_sum(src, seg, n)
kernel_name = 'mk_decoder_postln_d1_seqx_r4_b66292'

def setup_inputs(seed: int=0):
    np.random.seed(seed)
    _w = jnp.asarray

    def _rec_inputs():
        import jax
        import jax.numpy as jnp
        _rk = jax.random.key(seed)
        x = -0.0002928 + 1 * jax.random.normal(jax.random.fold_in(_rk, 1), (8, 512, 256), jnp.float32)
        _lenS = 512 - jax.random.randint(jax.random.fold_in(_rk, 7), (8,), 0, max(1, 512 // 4) + 1, jnp.int32)
        _lenS2 = 512 - jax.random.randint(jax.random.fold_in(_rk, 8), (8,), 0, max(1, 512 // 4) + 1, jnp.int32)
        _ctx_1024P = jax.random.normal(jax.random.fold_in(_rk, 11), (8, 16, 256), jnp.float32)
        _ctx_1024c = jax.random.dirichlet(jax.random.fold_in(_rk, 511), 0.3 * jnp.ones((16,), jnp.float32), (8, 512))
        _ctx_1024t = jnp.einsum('bsk,bkd->bsd', _ctx_1024c, _ctx_1024P)
        _ctx_1024t = _ctx_1024t * jax.lax.rsqrt(jnp.mean(jnp.square(_ctx_1024t)) + 1e-12) * 0.953939
        ctx_1024 = -1.39393e-06 + 0.999914 * (_ctx_1024t + 0.3 * jax.random.normal(jax.random.fold_in(_rk, 611), (8, 512, 256), jnp.float32))
        _validS = jnp.arange(512)[None, :] < _lenS[:, None]
        _validS2 = jnp.arange(512)[None, :] < _lenS2[:, None]
        _causal = jnp.tril(jnp.ones((512, 512), dtype=bool))
        mask_Bx16xSxS2_ff0 = jnp.where(jnp.ones((8, 16, 512, 512), dtype=bool), 0.0, -1000000000.0).astype(jnp.float32)
        return (x, ctx_1024, mask_Bx16xSxS2_ff0)
    x, ctx_1024, mask_Bx16xSxS2_ff0 = _rec_inputs()

    def _L0_attn_setup():
        import jax, jax.numpy as jnp
        import numpy as np
        import math
        D_MODEL = 256
        N_HEAD = 16
        HEAD_DIM = D_MODEL // N_HEAD

        def _split_heads(t):
            B, S, _ = t.shape
            return t.reshape(B, S, N_HEAD, HEAD_DIM).transpose(0, 2, 1, 3)
        key = jax.random.key(seed)
        ks = jax.random.split(key, 9)
        B, S = (2, 512)
        x = jax.random.normal(ks[0], (B, S, D_MODEL), dtype=jnp.float32)
        w = lambda k, std: jax.random.normal(k, (D_MODEL, D_MODEL), dtype=jnp.float32) * std
        return {'x': x, 'Wq_amp': w(ks[1], 0.02), 'Wk_amp': w(ks[2], 0.02), 'Wq_phi': w(ks[3], 0.005), 'Wk_phi': w(ks[4], 0.005), 'Wv': w(ks[5], 0.02), 'Wo': w(ks[6], 0.02), 'score_log_scale': jnp.zeros((N_HEAD,), dtype=jnp.float32)}
    _L0_attn_all = _L0_attn_setup()
    _L0_attn_in = {k: v for k, v in _L0_attn_all.items() if k in ('Wq_amp', 'Wk_amp', 'Wq_phi', 'Wk_phi', 'Wv', 'Wo', 'score_log_scale')}
    del _L0_attn_all

    def _L0_xattn_setup():
        import jax, jax.numpy as jnp
        import numpy as np
        B, S, D = (2, 512, 256)
        H = 16
        DH = D // H
        LAMBDA_INIT = 0.8
        EPS = 1e-05
        SCALE = 1.0 / np.sqrt(DH)
        key = jax.random.key(seed)
        ks = jax.random.split(key, 13)
        inp = {'query': jax.random.normal(ks[0], (B, S, D), jnp.float32), 'key': jax.random.normal(ks[1], (B, S, D), jnp.float32), 'value': jax.random.normal(ks[2], (B, S, D), jnp.float32), 'attn_mask': jnp.zeros((B, H, S, S), jnp.float32), 'W_q': jax.random.normal(ks[3], (D, 2 * DH * H), jnp.float32) * 0.02, 'W_k': jax.random.normal(ks[4], (D, 2 * DH * H), jnp.float32) * 0.02, 'W_v': jax.random.normal(ks[5], (D, DH * H), jnp.float32) * 0.02, 'W_o': jax.random.normal(ks[6], (DH * H, D), jnp.float32) * 0.02, 'lambda_q1': jax.random.normal(ks[7], (H, DH), jnp.float32) * 0.1, 'lambda_k1': jax.random.normal(ks[8], (H, DH), jnp.float32) * 0.1, 'lambda_q2': jax.random.normal(ks[9], (H, DH), jnp.float32) * 0.1, 'lambda_k2': jax.random.normal(ks[10], (H, DH), jnp.float32) * 0.1, 'rms_scale': jnp.ones((DH,), jnp.float32)}
        return inp
    _L0_xattn_all = _L0_xattn_setup()
    _L0_xattn_in = {k: v for k, v in _L0_xattn_all.items() if k in ('W_q', 'W_k', 'W_v', 'W_o', 'lambda_q1', 'lambda_k1', 'lambda_q2', 'lambda_k2', 'rms_scale')}
    del _L0_xattn_all

    def _L0_ffn_setup():
        import jax, jax.numpy as jnp
        import numpy as np
        CAPACITY_RATIO = 0.75
        key = jax.random.key(seed)
        k1, k2, k3 = jax.random.split(key, 3)
        B, L, D = (4, 2048, 256)
        x = jax.random.normal(k1, (B, L, D), dtype=jnp.float32)
        w_router = jax.random.normal(k2, (D,), dtype=jnp.float32) * 0.02
        w_block = jax.random.normal(k3, (D, D), dtype=jnp.float32) * 0.02
        return {'x': x, 'w_router': w_router, 'w_block': w_block}
    _L0_ffn_all = _L0_ffn_setup()
    _L0_ffn_in = {k: v for k, v in _L0_ffn_all.items() if k in ('w_router', 'w_block')}
    del _L0_ffn_all
    return {'x': x, 'ctx_1024': ctx_1024, 'mask_Bx16xSxS2_ff0': mask_Bx16xSxS2_ff0, 'L0_attn_Wq_amp': _L0_attn_in['Wq_amp'], 'L0_attn_Wk_amp': _L0_attn_in['Wk_amp'], 'L0_attn_Wq_phi': _L0_attn_in['Wq_phi'], 'L0_attn_Wk_phi': _L0_attn_in['Wk_phi'], 'L0_attn_Wv': _L0_attn_in['Wv'], 'L0_attn_Wo': _L0_attn_in['Wo'], 'L0_attn_score_log_scale': _L0_attn_in['score_log_scale'], 'L0_xattn_W_q': _L0_xattn_in['W_q'], 'L0_xattn_W_k': _L0_xattn_in['W_k'], 'L0_xattn_W_v': _L0_xattn_in['W_v'], 'L0_xattn_W_o': _L0_xattn_in['W_o'], 'L0_xattn_lambda_q1': _L0_xattn_in['lambda_q1'], 'L0_xattn_lambda_k1': _L0_xattn_in['lambda_k1'], 'L0_xattn_lambda_q2': _L0_xattn_in['lambda_q2'], 'L0_xattn_lambda_k2': _L0_xattn_in['lambda_k2'], 'L0_xattn_rms_scale': _L0_xattn_in['rms_scale'], 'L0_ffn_w_router': _L0_ffn_in['w_router'], 'L0_ffn_w_block': _L0_ffn_in['w_block']}

def reference(x, ctx_1024, mask_Bx16xSxS2_ff0, L0_attn_Wq_amp, L0_attn_Wk_amp, L0_attn_Wq_phi, L0_attn_Wk_phi, L0_attn_Wv, L0_attn_Wo, L0_attn_score_log_scale, L0_xattn_W_q, L0_xattn_W_k, L0_xattn_W_v, L0_xattn_W_o, L0_xattn_lambda_q1, L0_xattn_lambda_k1, L0_xattn_lambda_q2, L0_xattn_lambda_k2, L0_xattn_rms_scale, L0_ffn_w_router, L0_ffn_w_block):
    import jax
    import jax.numpy as jnp

    def _L0_attn_ref(x, Wq_amp, Wk_amp, Wq_phi, Wk_phi, Wv, Wo, score_log_scale):
        import jax, jax.numpy as jnp
        import numpy as np
        import math
        D_MODEL = 256
        N_HEAD = 16
        HEAD_DIM = D_MODEL // N_HEAD

        def _split_heads(t):
            B, S, _ = t.shape
            return t.reshape(B, S, N_HEAD, HEAD_DIM).transpose(0, 2, 1, 3)
        B, S, _ = x.shape
        eps = 1e-06
        q_amp = _split_heads(jax.nn.softplus(x @ Wq_amp.T))
        k_amp = _split_heads(jax.nn.softplus(x @ Wk_amp.T))
        q_phi = _split_heads(math.pi * jnp.tanh(x @ Wq_phi.T))
        k_phi = _split_heads(math.pi * jnp.tanh(x @ Wk_phi.T))
        q_amp = q_amp / jnp.sqrt(jnp.mean(q_amp * q_amp, axis=-1, keepdims=True) + eps)
        k_amp = k_amp / jnp.sqrt(jnp.mean(k_amp * k_amp, axis=-1, keepdims=True) + eps)
        q_cos = q_amp * jnp.cos(q_phi)
        q_sin = q_amp * jnp.sin(q_phi)
        k_cos = k_amp * jnp.cos(k_phi)
        k_sin = k_amp * jnp.sin(k_phi)
        scores = (jnp.einsum('bhqd,bhkd->bhqk', q_cos, k_cos) + jnp.einsum('bhqd,bhkd->bhqk', q_sin, k_sin)) / math.sqrt(HEAD_DIM)
        scores = scores * jnp.exp(score_log_scale)[None, :, None, None]
        mask = jnp.tril(jnp.ones((S, S), dtype=bool))
        scores = jnp.where(mask[None, None], scores, -jnp.inf)
        attn = jax.nn.softmax(scores, axis=-1)
        v = _split_heads(x @ Wv.T)
        out = jnp.einsum('bhqk,bhkd->bhqd', attn, v)
        out = out.transpose(0, 2, 1, 3).reshape(B, S, D_MODEL)
        return out @ Wo.T

    def _L0_xattn_ref(query, key, value, attn_mask, W_q, W_k, W_v, W_o, lambda_q1, lambda_k1, lambda_q2, lambda_k2, rms_scale):
        import jax, jax.numpy as jnp
        import numpy as np
        B, S, D = (2, 512, 256)
        H = 16
        DH = D // H
        LAMBDA_INIT = 0.8
        EPS = 1e-05
        SCALE = 1.0 / np.sqrt(DH)
        b, s, _ = value.shape
        q = (query @ W_q).reshape(b, s, H, 2 * DH).transpose(0, 2, 1, 3)
        k = (key @ W_k).reshape(b, s, H, 2 * DH).transpose(0, 2, 1, 3)
        v = (value @ W_v).reshape(b, s, H, DH).transpose(0, 2, 1, 3)
        q1, q2 = (q[..., :DH], q[..., DH:])
        k1, k2 = (k[..., :DH], k[..., DH:])
        lam = jnp.exp(jnp.sum(lambda_q1 * lambda_k1, -1)) - jnp.exp(jnp.sum(lambda_q2 * lambda_k2, -1)) + LAMBDA_INIT
        lam = lam[None, :, None, None]
        s1 = jnp.einsum('bhqd,bhkd->bhqk', q1, k1) * SCALE + attn_mask
        s2 = jnp.einsum('bhqd,bhkd->bhqk', q2, k2) * SCALE + attn_mask
        attn = jax.nn.softmax(s1, axis=-1) - lam * jax.nn.softmax(s2, axis=-1)
        out = jnp.einsum('bhqk,bhkd->bhqd', attn, v)
        rms = jnp.sqrt(jnp.mean(out * out, axis=-1, keepdims=True) + EPS)
        out = out / rms * rms_scale
        out = out * (1.0 - LAMBDA_INIT)
        out = out.transpose(0, 2, 1, 3).reshape(b, s, H * DH)
        return out @ W_o

    def _L0_ffn_ref(x, w_router, w_block):
        import jax, jax.numpy as jnp
        import numpy as np
        CAPACITY_RATIO = 0.75
        B, L, D = x.shape
        k = max(1, int(L * CAPACITY_RATIO))
        scores = jnp.einsum('bld,d->bl', x, w_router)
        _, top_idx = jax.lax.top_k(scores, k)
        selected = jnp.take_along_axis(x, top_idx[:, :, None], axis=1)
        processed = jax.nn.gelu(jnp.einsum('bkd,de->bke', selected, w_block))
        batch_idx = jnp.arange(B)[:, None]
        out = x.at[batch_idx, top_idx].set(processed)
        return out
    x = _layernorm(x + _L0_attn_ref(x, L0_attn_Wq_amp, L0_attn_Wk_amp, L0_attn_Wq_phi, L0_attn_Wk_phi, L0_attn_Wv, L0_attn_Wo, L0_attn_score_log_scale), axis=-1)
    x = _layernorm(x + _L0_xattn_ref(x, ctx_1024, ctx_1024, mask_Bx16xSxS2_ff0, L0_xattn_W_q, L0_xattn_W_k, L0_xattn_W_v, L0_xattn_W_o, L0_xattn_lambda_q1, L0_xattn_lambda_k1, L0_xattn_lambda_q2, L0_xattn_lambda_k2, L0_xattn_rms_scale), axis=-1)
    x = _layernorm(x + _L0_ffn_ref(x, L0_ffn_w_router, L0_ffn_w_block), axis=-1)
    return x

_drawn_inputs = setup_inputs


def setup_inputs(seed=0):
    import zlib

    import numpy as np

    out = dict(_drawn_inputs(seed))
    spreads = {'L0_attn_score_log_scale': (0.0, 0.8), 'L0_xattn_rms_scale': (1.0, 0.6)}
    factors = {'L0_attn_Wq_amp': 8.0,
     'L0_attn_Wk_amp': 8.0,
     'L0_attn_Wq_phi': 8.0,
     'L0_attn_Wk_phi': 8.0,
     'L0_attn_Wv': 4.244,
     'L0_attn_Wo': 4.206,
     'L0_xattn_W_q': 2.826,
     'L0_xattn_W_k': 2.792,
     'L0_xattn_lambda_q1': 6.923,
     'L0_xattn_lambda_k1': 6.591,
     'L0_xattn_lambda_q2': 7.172,
     'L0_xattn_lambda_k2': 8.0}
    for name, (base, spread) in spreads.items():
        noise = np.random.default_rng([zlib.crc32(name.encode()), seed]).standard_normal(out[name].shape)
        drawn = base * np.exp(spread * noise) if base else spread * noise
        out[name] = jnp.asarray(drawn.astype(out[name].dtype))
    for name, factor in factors.items():
        out[name] = (out[name] * factor).astype(out[name].dtype)
    return out
```

```python
import numpy as np
from contextlib import ExitStack

import concourse.bass as bass
from concourse import mybir

P = 128
B, S, D, H = 8, 512, 256, 16
DH = D // H
TB = S // P
DC = D // P
F = 2 * DH
TERMS = P // F
VW = 32
HALF = H // 2
BANK = 512
K_SEL = int(S * 0.75)
SELF_EPS, LN_EPS, RMS_EPS = 1e-6, 1e-5, 1e-5
LAMBDA_INIT = 0.8
PI_IN = 3.1415925
GELU_C, GELU_A = 0.7978845608028654, 0.044715
FLAGS_FROM = 0.0
DEN_LO, DEN_HI = 1e-20, 1e20

QUADS1, QUADS2 = H // 4, H // 2
GROUPS1, GROUPS2 = 5, 8
G1, G2 = QUADS1 * GROUPS1, QUADS2 * GROUPS2
G = G1 + G2
SLOTS = 7
assert G % SLOTS == 0
SETS = QUADS1 + 2 * QUADS2


def self_place(r, kb):
    p, odd = divmod(r, 2)
    bank, off = [[(0, 0), (1, 0), (2, 0), (1, 384)], [(3, 0), (4, 0), (2, 256), (4, 384)]][odd][kb]
    return 5 * p + bank, off, S - kb * P


def set_of(g):
    return g // GROUPS1 if g < G1 else QUADS1 + (g - G1) // 4


MISC_FAST = (
    [u for t in range(TB) for u in ((("amp", t), ("softplus", t)), (("v1", t), ("v1_sb", t)))]
    + [(("phi", t), ("tanh", t)) for t in range(TB)]
    + [u for t in range(TB) for i in range(2) for u in (
        (("qT1", t, i), ("q1_stacked", 2 * t + i)), (("kT1", t, i), ("k1_stacked", 2 * t + i)))]
    + [(("o1T", q), ("att1", q)) for q in range(QUADS1)]
    + [(("attT1", c), ("attT1_sb", c)) for c in range(DC)]
    + [(("wo1", p), ("y1", p)) for p in range(2)]
    + [(("x1T", c), ("x1T_sb", c)) for c in range(DC)]
    + [u for t in range(TB) for u in (
        (("k2", t), ("k2_split", t)), (("v2", t), ("v2_sb", t)), (("q2", t), ("q2_split", t)),
        (("qT2", t, 0), ("q2_stacked", 2 * t)), (("kT2", t, 0), ("k2_stacked", 2 * t)),
        (("qT2", t, 1), ("q2_stacked", 2 * t + 1)), (("kT2", t, 1), ("k2_stacked", 2 * t + 1)))]
    + [(("o2T", q), ("o2_sb", q)) for q in range(QUADS2)]
    + [(("attT2", c), ("attT2_sb", c)) for c in range(DC)]
    + [(("wo2", p), ("y2", p)) for p in range(2)]
    + [(("x2T", c), ("x2T_sb", c)) for c in range(DC)]
    + [(("srow",), ("srow_sb", 0))]
    + [(("ffn", p), ("h_sb", p)) for p in range(2)]
)

PER = dict(
    xT_in=1, x_in=1, ctx_in=1, mask_in0=H // 2, mask_in1=H // 2, out_st=1,
    misc_full=len(MISC_FAST), scores=G, exps=G, causal=QUADS1 * 10, pv=SETS, oT_sb=QUADS1 + QUADS2,
    mask_seen=H,
    abs_x=TB, exp_x=TB, ln_x=TB, softplus=TB, v1_sb=TB, sq1=TB, ss1=TB, rs_ln=1, rs=1, rs_scaled=1, amp_n=TB,
    tanh=TB, sin=TB, abs_t=TB, cos=TB, w_cos=TB, w_sin=TB, hi1=TB, lo1=TB, dup1=3 * TB,
    q1_stacked=2 * TB, k1_stacked=2 * TB, den1=QUADS1, rden1=QUADS1, att1=QUADS1,
    attT1_sb=DC, y1=2, stats1=TB, aggr1=TB, ln1_ln=1, ln1_rstd=1, x1=TB, x1T_sb=DC,
    k2_hi=TB, k2_split=TB, k2_dup=2 * TB, v2_sb=TB, q2_hi=TB, q2_split=TB, q2_dup=TB,
    q2_stacked=2 * TB, k2_stacked=4 * TB, o2_sb=QUADS2, rden2=1, rden2_lam=1, o2_norm=1, o2_diff=1, o2_sq=1, o2_ms=1,
    rms_ln=1, rms_r=1, att2=1, attT2_sb=DC, y2=2, stats2=TB, aggr2=TB, ln2_ln=1, ln2_rstd=1, x2=TB, x2T_sb=DC,
    route=TB, srow_sb=1, gt=TB, eq=TB, rank=1, sel=1, keep=1, half_sel=1,
    h_sb=2, h_sq=1, h_w=1, h_u=1, h_tanh=1, h_g=1, h_gs=TB, y3=TB, stats3=TB, aggr3=TB, ln3_ln=1, ln3_rstd=1, out=TB,
    ok_lo=2, ok_cnt=2, ok_acc=2, bad_max=1, bad_acc=1,
)
MISC_FAST = [(n, (e, 2 * k + 1) if e == "k2_stacked" else (e, k)) for n, (e, k) in MISC_FAST]

NC4 = H // 4
MISC_EXACT = [
    (n, ("k2_stacked", 2 * n[1] + 1) if n[0] == "kT2" else (e[0], n[1]) if n[0] in ("qT1", "kT1", "qT2") else e)
    for n, e in MISC_FAST if n[0] not in ("o1T", "o2T") and not (n[0] in ("qT1", "kT1", "qT2", "kT2") and n[2] == 1)]
PER_EXACT = dict(
    PER, misc_full=len(MISC_EXACT), scores=0, exps=0, causal=0, pv=0, oT_sb=0, mask_in0=0, mask_in1=0, mask_seen=0,
    hi1=0, lo1=0, dup1=0, q1_stacked=TB, k1_stacked=TB, den1=0, rden1=0, att1=0, k2_hi=0, k2_dup=0, q2_hi=0, q2_dup=0,
    q2_stacked=TB, k2_stacked=2 * TB, o2_sb=0, rden2=0, rden2_lam=0, o2_norm=0, o2_diff=0, ok_lo=0, ok_cnt=0, ok_acc=0,
    bad_max=0, bad_acc=0)
ROUND = dict(
    s_scores=1, s_z=1, s_max=1, s_exp=1, s_rden=1, s_a=1, s_T=1, s_aT=1, s_pv=1, s_out=1,
    c_mask=1, c_scores=1, c_z=2, c_max=2, c_exp=2, c_rden=1, c_rlam=1, c_a0=1, c_a=1, c_T=1, c_aT=1, c_pv=1, c_out=1)
HEAD = 100
CREDITED = ("misc_full", "eq", "y1", "mask_seen", "y3", "h_g", "scores", "pv", "exps", "oT_sb", "bad_max", "ok_cnt",
            "ok_acc", "attT2_sb", "out_st", "h_sb", "srow_sb", "x2T_sb", "k2_stacked", "softplus")
DMA_EVENTS = {"xT_in", "x_in", "ctx_in", "mask_in0", "mask_in1", "out_st"}


class Mode:

    def __init__(self, misc, per, before):
        self.misc, self.per = misc, per
        self.use = {name: n for n, (name, _) in enumerate(misc)}
        self.before = {e: B * n for e, n in before.items()}


FAST = Mode(MISC_FAST, PER, {e: 0 for e in PER})
EXACT = Mode(MISC_EXACT, PER_EXACT, PER)


def build(nc, t):
    f32, f16, i32 = mybir.dt.float32, mybir.dt.float16, mybir.dt.int32
    ALU, ACT, AX = mybir.AluOpType, mybir.ActivationFunctionType, mybir.AxisListType

    with ExitStack() as ctx:
        def sb(name, shape, dt=f32):
            return ctx.enter_context(nc.sbuf_tensor(name, [P, *shape], dt))

        def ps(name, words):
            return ctx.enter_context(nc.psum_tensor(name, [P, words], f32))

        sem = {e: ctx.enter_context(nc.semaphore(e)) for e in (*PER, *ROUND, "s_k", "s_q", "c_k", "c_q", "above", "flag_sum", "flag_pe", "flag")}
        const_in, const_ok = (ctx.enter_context(nc.semaphore(n)) for n in ("const_in", "const_ok"))
        passed = ctx.enter_context(nc.semaphore("passed"))
        dve_const, act_const, pool_const = (ctx.enter_context(nc.semaphore(n)) for n in ("dve_const", "act_const", "pool_const"))

        w_amp, w_phi = sb("w_amp", [DC, 2 * D]), sb("w_phi", [DC, 2 * D])
        w_v1, w_o1 = sb("w_v1", [DC, D]), sb("w_o1", [DC, D])
        w_q2, w_k2 = sb("w_q2", [DC, 2 * D]), sb("w_k2", [DC, 2 * D])
        w_v2, w_o2, w_ffn = sb("w_v2", [DC, D]), sb("w_o2", [DC, D]), sb("w_ffn", [DC, D])
        w_route = sb("w_route", [D])
        ident, ident16 = sb("ident", [P]), sb("ident16", [P], f16)
        tie = sb("tie", [TB, S], f16)
        head_scale = sb("head_scale", [H])
        lam_sum = sb("lam_sum", [2, H])
        lam_w = sb("lam_w", [H, 2])
        rms_col = sb("rms_col", [1])
        half_mask = sb("half_mask", [2])

        xT, x_tok, ctxT = sb("xT", [DC, S]), sb("x_tok", [TB, D]), sb("ctxT", [DC, S])
        mask_t = sb("mask_t", [2, TB * S])
        work = sb("work", [3, TB, 2 * D])
        sp, tt, sn = (work[:, i] for i in range(3))
        ss, rs = sb("ss", [TB, 2 * H]), sb("rs", [TB, 2 * H])
        wk = sb("wk", [2 * H, F])
        stag = sb("stag", [2 * H, TERMS, F], f16)
        q_st, k_st = sb("q_st", [H, S], f16), sb("k_st", [2, H, S], f16)
        vals = sb("vals", [TB, H, VW])
        ex = sb("ex", [SLOTS, 2 * BANK])
        lam_in = ex[:, 0, :].rearrange("p (n d) -> p n d", d=D)
        lam_prod = ex[:, 1, 0:2 * D].rearrange("p (n d) -> p n d", d=D)
        oT = sb("oT", [2, S])
        den1, rden1 = sb("den1", [QUADS1, TB, 4]), sb("rden1", [TB, 4])
        att, att_T = sb("att", [TB, D]), sb("att_T", [DC, S])
        x1 = sb("x1", [TB, D])
        x2 = x1
        xT2 = sb("xT2", [DC, S])
        y = sb("y", [TB, D])
        st6, mv = sb("st6", [TB, 6]), sb("mv", [TB, 2])
        rstd = sb("rstd", [TB])
        o2 = work[:].rearrange("p a b c -> p (a b c)")[:, 0:TB * 2 * H * (DH + 1)].rearrange(
            "p (a h c) -> p a h c", a=TB, c=DH + 1)
        rden2, ms2 = sb("rden2", [TB, H, 2]), sb("ms2", [TB, H])
        route, cgt, ceq = sb("route", [TB]), sb("cgt", [TB]), sb("ceq", [TB])
        rank, sel, keep, hsel = sb("rank", [TB]), sb("sel", [TB]), sb("keep", [TB]), sb("hsel", [TB])
        junk = wk[:].rearrange("p h f -> p (h f)")[:, 0:S]
        mask_bad, bad, bad_b = sb("mask_bad", [H]), sb("bad", [1]), sb("bad_b", [1])
        ok_t, ok_n, ok_sum = sb("ok_t", [TB * 2 * H]), sb("ok_n", [2]), sb("ok_sum", [1])
        h_t, g_t, u_t = sp[:, 0:2, :], tt[:, 0:2, :], sn[:, 0:2, :]
        flat = lambda a: a.rearrange("p a b -> p (a b)")

        psS = [ps("psS0", 2 * BANK), ps("psS1", 2 * BANK)]
        psO = [ps("psO0", BANK), ps("psO1", BANK)]
        psM = [ps("psM0", BANK), ps("psM1", BANK)]

        path = [FAST]

        def wait(eng, b, event, k=0):
            mode = path[0]
            n, before = mode.per[event], mode.before[event]
            scale = 16 if event in DMA_EVENTS else 1
            head = HEAD if event in CREDITED else 0
            assert -HEAD < k < max(n, 1) and (k >= 0 or head or mode is EXACT), (event, k)
            assert n or k < 0, (event, k)
            eng.wait_ge(sem[event], b * (n * scale) + ((before + k + 1) * scale + head))

        def count(event):
            return path[0].per[event]

        def uses():
            return len(path[0].misc)

        def hold(eng):
            eng.sem_inc(passed, 1)

        def bank(use):
            return psM[path[0].use[use] % 2]

        def bank16(use):
            return bank(use)[:, :].bitcast(f16)

        def full(eng, b, use, back=0):
            wait(eng, b, "misc_full", path[0].use[use] - back * uses())

        def wait_round(eng, i, event, k=0):
            n, scale = ROUND[event], 16 if event == "c_mask" else 1
            eng.wait_ge(sem[event], i * (n * scale) + (k + 1) * scale)

        def rounds(eng, b, chunk_start, block_start, round_):
            hold(eng)
            with eng.Fori(0, NC4) as c:
                bc = b * NC4 + c
                chunk_start(bc, c)
                with eng.Fori(0, TB) as qb:
                    bq = bc * TB + qb
                    block_start(bq, c, qb)
                    for r in range(4):
                        round_(bq * 4 + r, c, qb, r)

        nothing = lambda *a: None

        z2 = ex[:, 0, :].rearrange("p (j k) -> p j k", j=2)
        probs, probs_T = ex[:, 1, 0:S], ex[:, 1, S:2 * S]
        q_cur, k_cur = ex[:, 2, 0:P], ex[:, 3, :].rearrange("p (j k) -> p j k", j=2)
        q32 = q_st[:].rearrange("p h s -> p (h s)").bitcast(f32)
        k32 = k_st[:].rearrange("p j h s -> p (j h s)").bitcast(f32)
        JK = NC4 * S
        neg_max, row_sum, row_scale = sb("neg_max", [2]), sb("row_sum", [2]), sb("row_scale", [2])
        ones1, flag_f, flag_i = sb("ones1", [1]), sb("flag_f", [1]), sb("flag_i", [1], i32)

        def if_needed(eng, body):
            eng.wait_ge(sem["flag"], 1)
            flag = eng.value_load(flag_i[0:1, 0:1], min_val=0, max_val=1)
            with eng.If(flag > 0):
                path[0] = EXACT
                with eng.Fori(0, B) as b:
                    body(b)
                path[0] = FAST

        block = ctx.enter_context(nc.Block())

        N_CONST = 16

        @block.sync
        def _(sp_):
            def chunks(name):
                return t[name].rearrange("(c p) n -> p c n", p=P)

            def load(dst, src):
                sp_.dma_start(dst, src).then_inc(const_in, 16)

            load(w_amp[:, :, 0:D], chunks("WqaT"))
            load(w_amp[:, :, D:], chunks("WkaT"))
            load(w_phi[:, :, 0:D], chunks("WqpT"))
            load(w_phi[:, :, D:], chunks("WkpT"))
            load(w_v1[:], chunks("WvT"))
            load(w_o1[:], chunks("WoT"))
            load(w_q2[:], chunks("xW_q"))
            load(w_k2[:], chunks("xW_k"))
            load(w_v2[:], chunks("xW_v"))
            load(w_o2[:], chunks("xW_o"))
            load(w_ffn[:], chunks("w_block"))
            load(w_route[:], t["w_router"].partition_broadcast(P))
            load(head_scale[:], t["log_scale"].partition_broadcast(P))
            load(lam_in[:], t["lam4"].partition_broadcast(P))
            load(rms_col[:], t["rms_tiled"])
            load(half_mask[:], t["half_rows"])
            def inputs(b):
                full(sp_, b, ("phi", TB - 1), 1)
                sp_.dma_start(xT[:], t["xT"][b].rearrange("(c p) s -> p c s", p=P)).then_inc(sem["xT_in"], 16)
                full(sp_, b, ("v2", TB - 1), 1)
                sp_.dma_start(ctxT[:], t["ctxT"][b].rearrange("(c p) s -> p c s", p=P)).then_inc(sem["ctx_in"], 16)
                wait(sp_, b, "y1", -1)
                sp_.dma_start(x_tok[:], t["x"][b].rearrange("(a p) d -> p a d", p=P)).then_inc(sem["x_in"], 16)

            with sp_.Fori(0, B) as b:
                inputs(b)
                for h in range(H):
                    wait(sp_, b, "mask_seen", h - 2)
                    sp_.dma_start(mask_t[:, h % 2, :], t["mask"][b, h].rearrange("(p a) k -> p (a k)", p=P)
                                  ).then_inc(sem[f"mask_in{h % 2}"], 16)

            def mask_round(b):
                def load_mask(i, c, qb, r):
                    wait_round(sp_, i, "c_z", -1)
                    sp_.dma_start(mask_t[:, 0, 0:S], t["mask"][b, c * 4 + r, bass.ds(qb * P, P), :]
                                  ).then_inc(sem["c_mask"], 16)
                rounds(sp_, b, nothing, nothing, load_mask)

            if_needed(sp_, lambda b: (inputs(b), mask_round(b)))

        @block.gpsimd
        def _(pool):
            for e in sorted(CREDITED):
                pool.sem_inc(sem[e], HEAD)
            nc.gpsimd.memset(tt[:, :, :], 1.0).then_inc(pool_const, 1)
            nc.gpsimd.memset(vals[:], 0.0).then_inc(pool_const, 1)
            pool.wait_ge(pool_const, 2)
            nc.gpsimd.memset(vals[:, :, :, DH:DH + 1], 1.0).then_inc(pool_const, 1)
            nc.gpsimd.affine_select(out=ident[:], in_=tt[:, 0, 0:P], compare_op=ALU.is_equal, fill=0.0, base=0,
                                    pattern=[[-1, P]], channel_multiplier=1).then_inc(pool_const, 1)
            for a in range(TB):
                nc.gpsimd.affine_select(out=tie[:, a, :], in_=tt[:, 0, :], compare_op=ALU.is_gt, fill=0.0, base=a * P,
                                        pattern=[[-1, S]], channel_multiplier=1).then_inc(pool_const, 1)
            pool.wait_ge(pool_const, 4)
            nc.gpsimd.tensor_copy(ident16[:], ident[:]).then_inc(pool_const, 1)
            pool.wait_ge(pool_const, 5 + TB)

            def body(b):
                for a in range(TB):
                    wait(pool, b, "softplus", a)
                    nc.gpsimd.tensor_tensor(sn[:, a, :], sp[:, a, :], sp[:, a, :], ALU.mult).then_inc(sem["sq1"], 1)
                wait(pool, b, "rs_scaled", 0)
                for a in range(TB):
                    v = sp[:, a, :].rearrange("p (g d) -> p g d", d=DH)
                    nc.gpsimd.tensor_tensor(v, v, rs[:, a, :].unsqueeze(2).broadcast_to((P, 2 * H, DH)), ALU.mult
                                            ).then_inc(sem["amp_n"], 1)
                for q in range(QUADS1 if path[0] is FAST else 0):
                    def keep_lower(group, view, n):
                        wait(pool, b, "exps", q * GROUPS1 + group)
                        hold(pool)
                        nc.gpsimd.affine_select(out=view, in_=view, compare_op=ALU.is_ge, fill=0.0, base=0,
                                                pattern=[[0, n], [1, P]], channel_multiplier=-1
                                                ).then_inc(sem["causal"], 1)
                    for pair in range(2):
                        for bk, stride, n in ((0, 0, 1), (1, 384, 2), (2, 256, 2), (3, 0, 1), (4, 384, 2)):
                            g, off = divmod(5 * pair + bk, 2)
                            tile = ex[:, (q * GROUPS1 + g) % SLOTS, off * BANK:(off + 1) * BANK]
                            if n == 1:
                                keep_lower(g, tile[:, 0:P].unsqueeze(1), 1)
                            elif stride == 256:
                                keep_lower(g, tile.rearrange("p (n c) -> p n c", n=2)[:, :, 0:P], 2)
                            else:
                                keep_lower(g, tile.rearrange("p (n c) -> p n c", n=4)[:, 0:4:3, :], 2)
                if path[0] is EXACT:
                    pool.wait_ge(sem["c_out"], b * H * TB + H * TB)
                else:
                    wait(pool, b, "o2_diff", 0)
                nc.gpsimd.tensor_tensor(y[:], att[:], att[:], ALU.mult).then_inc(sem["o2_sq"], 1)

            with pool.Fori(0, B) as b:
                body(b)
            if_needed(pool, body)

        @block.scalar
        def _(act):
            act.wait_ge(const_in, 16 * N_CONST)
            act.wait_ge(pool_const, 5 + TB)
            nc.scalar.activation(head_scale[:], head_scale[:], ACT.Exp).then_inc(act_const, 1)
            act.wait_ge(dve_const, 2)
            nc.scalar.activation(lam_sum[:], lam_sum[:], ACT.Exp).then_inc(act_const, 1)

            def rsqrt(b, out, in_, scale, eps, ready, ln_event, event):
                wait(act, b, *ready)
                nc.scalar.activation(out, in_, ACT.Ln, bias=eps, scale=scale).then_inc(sem[ln_event], 1)
                wait(act, b, ln_event)
                nc.scalar.activation(out, out, ACT.Exp, scale=-0.5).then_inc(sem[event], 1)

            def exps(b, groups, scale):
                for g in groups:
                    wait(act, b, "scores", g)
                    if g >= SLOTS:
                        wait(act, b, "pv", set_of(g - SLOTS))
                    else:
                        wait(act, b, "pv", set_of(G + g - SLOTS) - SETS)
                    nc.scalar.activation(ex[:, g % SLOTS, :], psS[g % 2][:, :], ACT.Exp, scale=scale
                                         ).then_inc(sem["exps"], 1)

            def self_exp(i, c, qb, r):
                wait_round(act, i, "s_max")
                nc.scalar.activation(z2[:, 0, :], z2[:, 0, :], ACT.Exp, bias=neg_max[:, 0:1],
                                     accum_out=row_sum[:, 0:1]).then_inc(sem["s_exp"], 1)

            def cross_exp(i, c, qb, r):
                for j in range(2):
                    wait_round(act, i, "c_max", j)
                    nc.scalar.activation(z2[:, j, :], z2[:, j, :], ACT.Exp, bias=neg_max[:, j:j + 1],
                                         accum_out=row_sum[:, j:j + 1]).then_inc(sem["c_exp"], 1)

            def body(b):
                for a in range(TB):
                    full(act, b, ("amp", a))
                    if a == 0:
                        wait(act, b, "y3", -1)
                    nc.scalar.activation(tt[:, a, :], bank(("amp", a))[:, :], ACT.Abs).then_inc(sem["abs_x"], 1)
                    wait(act, b, "abs_x", a)
                    nc.scalar.activation(tt[:, a, :], tt[:, a, :], ACT.Exp, scale=-1.0).then_inc(sem["exp_x"], 1)
                    wait(act, b, "exp_x", a)
                    nc.scalar.activation(tt[:, a, :], tt[:, a, :], ACT.Ln, bias=1.0).then_inc(sem["ln_x"], 1)
                rsqrt(b, flat(rs[:]), flat(ss[:]), 1.0 / DH, SELF_EPS, ("ss1", TB - 1), "rs_ln", "rs")
                for a in range(TB):
                    full(act, b, ("phi", a))
                    wait(act, b, "softplus", a)
                    nc.scalar.activation(tt[:, a, :], bank(("phi", a))[:, :], ACT.Tanh).then_inc(sem["tanh"], 1)
                for a in range(TB):
                    wait(act, b, "tanh", a)
                    wait(act, b, "ss1", a)
                    nc.scalar.activation(sn[:, a, :], tt[:, a, :], ACT.Sin, scale=PI_IN).then_inc(sem["sin"], 1)
                    wait(act, b, "sin", a)
                    nc.scalar.activation(tt[:, a, :], tt[:, a, :], ACT.Abs).then_inc(sem["abs_t"], 1)
                    wait(act, b, "abs_t", a)
                    nc.scalar.activation(tt[:, a, :], tt[:, a, :], ACT.Sin, scale=-float(np.pi), bias=float(np.pi / 2)
                                         ).then_inc(sem["cos"], 1)
                if path[0] is FAST:
                    exps(b, range(G1), 1.0)
                else:
                    rounds(act, b, nothing, nothing, self_exp)
                rsqrt(b, rstd[:], mv[:, :, 1], 1.0, LN_EPS, ("aggr1", TB - 1), "ln1_ln", "ln1_rstd")
                if path[0] is FAST:
                    exps(b, range(G1, G), DH ** -0.5)
                else:
                    rounds(act, b, nothing, nothing, cross_exp)
                rsqrt(b, flat(ms2[:]), flat(ms2[:]), 1.0 / DH, RMS_EPS, ("o2_ms", 0), "rms_ln", "rms_r")
                rsqrt(b, rstd[:], mv[:, :, 1], 1.0, LN_EPS, ("aggr2", TB - 1), "ln2_ln", "ln2_rstd")
                wait(act, b, "h_sb", 1)
                nc.scalar.activation(g_t, h_t, ACT.Square).then_inc(sem["h_sq"], 1)
                wait(act, b, "h_u", 0)
                nc.scalar.activation(u_t, u_t, ACT.Tanh, scale=GELU_C).then_inc(sem["h_tanh"], 1)
                rsqrt(b, rstd[:], mv[:, :, 1], 1.0, LN_EPS, ("aggr3", TB - 1), "ln3_ln", "ln3_rstd")

                wait(act, b, "out", TB - 1)
                act.dma_start(t["out"][b].rearrange("(a p) d -> p a d", p=P), y[:]).then_inc(sem["out_st"], 16)

            with act.Fori(0, B) as b:
                body(b)
            act.wait_ge(sem["out_st"], 16 * B + HEAD)

            def again(b):
                body(b)
                wait(act, b, "out_st")
            if_needed(act, again)

        @block.vector
        def _(dve):
            v = nc.vector
            dve.wait_ge(const_in, 16 * N_CONST)
            v.tensor_tensor(lam_prod[:], lam_in[:, 0:4:2, :], lam_in[:, 1:4:2, :], ALU.mult).then_inc(dve_const, 1)
            dve.wait_ge(dve_const, 1)
            v.tensor_reduce(lam_sum[:], lam_prod[:].rearrange("p a (h d) -> p a h d", d=DH), AX.X, ALU.add
                            ).then_inc(dve_const, 1)
            v.tensor_scalar(w_o2[:], w_o2[:], rms_col[:], 1.0 - LAMBDA_INIT, ALU.mult, ALU.mult
                            ).then_inc(dve_const, 1)
            v.memset(bad[:], 0.0).then_inc(dve_const, 1)
            v.memset(ok_sum[:], 0.0).then_inc(dve_const, 1)
            v.memset(lam_w[:], 1.0).then_inc(dve_const, 1)
            dve.wait_ge(act_const, 2)
            v.tensor_scalar(head_scale[:], head_scale[:], DH ** -0.5, None, ALU.mult).then_inc(dve_const, 1)
            v.tensor_tensor(lam_sum[:, 0, :], lam_sum[:, 1, :], lam_sum[:, 0, :], ALU.subtract).then_inc(dve_const, 1)
            dve.wait_ge(dve_const, 8)
            v.tensor_scalar(lam_w[:, :, 1], lam_sum[:, 0, :], LAMBDA_INIT, None, ALU.subtract).then_inc(dve_const, 1)
            dve.wait_ge(dve_const, 9)
            dve.wait_ge(pool_const, 5 + TB)

            def scan_mask(b, h):
                wait(dve, b, f"mask_in{h % 2}", h // 2)
                if h == 0:
                    wait(dve, b, "bad_max", -1)
                v.tensor_scalar(mask_t[:, h % 2, :], mask_t[:, h % 2, :], 0.0, 0.0, ALU.not_equal, ALU.max,
                                accum_out=mask_bad[:, h:h + 1]).then_inc(sem["mask_seen"], 1)

            def layer_norm_stats(b, a, src, ready, n):
                wait(dve, b, *ready)
                v.bn_stats(st6[:, a, :], src).then_inc(sem[f"stats{n}"], 1)
                wait(dve, b, f"stats{n}", a)
                hold(dve)
                v.bn_aggr(mv[:, a, :], st6[:, a, :]).then_inc(sem[f"aggr{n}"], 1)

            def normalise(b, a, dst, src, rstd_event, event):
                wait(dve, b, rstd_event)
                v.tensor_scalar(dst, src, mv[:, a, 0:1], rstd[:, a:a + 1], ALU.subtract, ALU.mult
                                ).then_inc(sem[event], 1)

            def stack(b, use, event, k, dst, scale=None):
                full(dve, b, use)
                src = bank16(use).rearrange("p (h c) -> p h c", h=HALF)
                if scale is None:
                    v.tensor_copy(dst, src).then_inc(sem[event], 1)
                else:
                    v.tensor_scalar(dst, src, scale, None, ALU.mult).then_inc(sem[event], 1)

            def evacuate_oT(b, quad):
                wait(dve, b, "pv", quad if quad < QUADS1 else QUADS1 + 2 * (quad - QUADS1) + 1)
                k = quad - 2
                name = ("o1T", k) if 0 <= k < QUADS1 else ("o2T", k - QUADS1) if k >= 0 else ("o2T", QUADS2 + k)
                full(dve, b, name, int(k < 0))
                v.tensor_copy(oT[:, quad % 2, :], psO[quad % 2][:, :]).then_inc(sem["oT_sb"], 1)

            def check_den(b, n, dens, scratch):
                if n == 0:
                    wait(dve, b, "ok_acc", -1)
                v.tensor_scalar(scratch, dens, DEN_LO, None, ALU.is_ge).then_inc(sem["ok_lo"], 1)
                wait(dve, b, "ok_lo", n)
                v.scalar_tensor_tensor(scratch, dens, DEN_HI, scratch, ALU.is_le, ALU.mult,
                                       accum_out=ok_n[:, n:n + 1]).then_inc(sem["ok_cnt"], 1)
                wait(dve, b, "ok_cnt", n)
                v.tensor_tensor(ok_sum[:], ok_sum[:], ok_n[:, n:n + 1], ALU.add).then_inc(sem["ok_acc"], 1)

            def differential(b):
                dens = o2[:, :, :, DH]
                wait(dve, b, "o2_sb", QUADS2 - 1)
                v.reciprocal(rden2[:].rearrange("p a h j -> p a (h j)"), dens).then_inc(sem["rden2"], 1)
                wait(dve, b, "rden2")
                v.tensor_tensor(rden2[:], rden2[:], lam_w[:].unsqueeze(1).broadcast_to((P, TB, H, 2)), ALU.mult
                                ).then_inc(sem["rden2_lam"], 1)
                check_den(b, 1, dens, ok_t[:].rearrange("p (a h) -> p a h", a=TB))
                wait(dve, b, "rden2_lam")
                num = o2[:, :, :, 0:DH]
                v.tensor_tensor(num, num, rden2[:].rearrange("p a h j -> p a (h j)").unsqueeze(3)
                                .broadcast_to((P, TB, 2 * H, DH)), ALU.mult).then_inc(sem["o2_norm"], 1)
                wait(dve, b, "o2_norm")
                both = o2[:].rearrange("p a (h j) c -> p a h j c", j=2)
                v.tensor_tensor(att[:].rearrange("p a (h d) -> p a h d", d=DH), both[:, :, :, 0, 0:DH], both[:, :, :, 1, 0:DH], ALU.add).then_inc(sem["o2_diff"], 1)

            def stack32(b, use, event, k0, parts):
                full(dve, b, use)
                a = use[1]
                src = bank(use).rearrange("p (c s) -> p c s", c=NC4)
                for j, part in enumerate(parts):
                    dst = part[:, 0:JK].rearrange("p (c s) -> p c s", c=NC4)[:, :, a * P:(a + 1) * P]
                    if len(parts) == 1:
                        v.tensor_copy(dst, src).then_inc(sem[event], 1)
                    else:
                        v.tensor_scalar(dst, src, half_mask[:, j:j + 1], None, ALU.mult).then_inc(sem[event], 1)

            def self_chunk(bc, c):
                wait_round(dve, bc * (4 * TB), "s_scores", -1)
                v.tensor_copy(k_cur[:, 0, :], k32[:, bass.ds(c * S, S)]).then_inc(sem["s_k"], 1)

            def cross_chunk(bc, c):
                wait_round(dve, bc * (4 * TB), "c_scores", -1)
                v.tensor_copy(k_cur[:, 0, :], k32[:, bass.ds(c * S, S)]).then_inc(sem["c_k"], 1)
                v.tensor_copy(k_cur[:, 1, :], k32[:, bass.ds(c * S + JK, S)]).then_inc(sem["c_k"], 1)

            def self_block(bq, c, qb):
                wait_round(dve, bq * 4, "s_scores", -1)
                v.tensor_copy(q_cur, q32[:, bass.ds(c * S + qb * P, P)]).then_inc(sem["s_q"], 1)

            def cross_block(bq, c, qb):
                wait_round(dve, bq * 4, "c_scores", -1)
                v.tensor_copy(q_cur, q32[:, bass.ds(c * S + qb * P, P)]).then_inc(sem["c_q"], 1)

            def round_out(i, c, qb, r, s):
                wait_round(dve, i, s + "_T")
                v.tensor_copy(probs_T, psS[0][:, BANK:2 * BANK]).then_inc(sem[s + "_aT"], 1)
                wait_round(dve, i, s + "_pv")
                v.tensor_copy(flat(att[:])[:, bass.ds(qb * D + c * (4 * DH) + r * DH, DH)], psO[0][:, 0:DH]
                              ).then_inc(sem[s + "_out"], 1)

            def self_round(i, c, qb, r):
                wait_round(dve, i, "s_scores")
                v.tensor_tensor(z2[:, 0, :], psS[0][:, 0:S], mask_t[:, 1, bass.ds(qb * S, S)], ALU.add
                                ).then_inc(sem["s_z"], 1)
                wait_round(dve, i, "s_z")
                v.tensor_reduce(neg_max[:, 0:1], z2[:, 0, :], AX.X, ALU.max, negate=True).then_inc(sem["s_max"], 1)
                wait_round(dve, i, "s_exp")
                v.reciprocal(row_scale[:, 0:1], row_sum[:, 0:1]).then_inc(sem["s_rden"], 1)
                wait_round(dve, i, "s_rden")
                v.tensor_scalar(probs, z2[:, 0, :], row_scale[:, 0:1], None, ALU.mult).then_inc(sem["s_a"], 1)
                round_out(i, c, qb, r, "s")

            def cross_round(i, c, qb, r):
                wait_round(dve, i, "c_scores")
                wait_round(dve, i, "c_mask")
                for j in range(2):
                    v.scalar_tensor_tensor(z2[:, j, :], psS[j][:, 0:S], DH ** -0.5, mask_t[:, 0, 0:S],
                                           ALU.mult, ALU.add).then_inc(sem["c_z"], 1)
                for j in range(2):
                    wait_round(dve, i, "c_z", j)
                    v.tensor_reduce(neg_max[:, j:j + 1], z2[:, j, :], AX.X, ALU.max, negate=True
                                    ).then_inc(sem["c_max"], 1)
                wait_round(dve, i, "c_exp", 1)
                v.reciprocal(row_scale[:], row_sum[:]).then_inc(sem["c_rden"], 1)
                wait_round(dve, i, "c_rden")
                v.tensor_tensor(row_scale[:], row_scale[:], flat(lam_w[:])[:, bass.ds(c * 8 + 2 * r, 2)], ALU.mult
                                ).then_inc(sem["c_rlam"], 1)
                wait_round(dve, i, "c_rlam")
                v.tensor_scalar(z2[:, 0, :], z2[:, 0, :], row_scale[:, 0:1], None, ALU.mult).then_inc(sem["c_a0"], 1)
                wait_round(dve, i, "c_a0")
                v.scalar_tensor_tensor(probs, z2[:, 1, :], row_scale[:, 1:2], z2[:, 0, :], ALU.mult, ALU.add
                                       ).then_inc(sem["c_a"], 1)
                round_out(i, c, qb, r, "c")

            def body(b):
                for a in range(TB):
                    full(dve, b, ("amp", a))
                    wait(dve, b, "ln_x", a)
                    if a == 0:
                        wait(dve, b, "h_g", -1)
                    v.scalar_tensor_tensor(sp[:, a, :], bank(("amp", a))[:, :], 0.0, tt[:, a, :], ALU.max, ALU.add
                                           ).then_inc(sem["softplus"], 1)
                    full(dve, b, ("v1", a))
                    if a == 0:
                        wait(dve, b, "pv", -1)
                    v.tensor_copy(vals[:, a, :, 0:DH], bank(("v1", a))[:, 0:D].rearrange("p (h d) -> p h d", d=DH)
                                  ).then_inc(sem["v1_sb"], 1)
                for a in range(TB):
                    wait(dve, b, "sq1", a)
                    v.tensor_reduce(ss[:, a, :], sn[:, a, :].rearrange("p (g d) -> p g d", d=DH), AX.X, ALU.add
                                    ).then_inc(sem["ss1"], 1)
                wait(dve, b, "rs")
                v.tensor_tensor(rs[:, :, 0:H], rs[:, :, 0:H], head_scale[:].unsqueeze(1).broadcast_to((P, TB, H)),
                                ALU.mult).then_inc(sem["rs_scaled"], 1)
                for a in range(TB):
                    wait(dve, b, "amp_n", a)
                    wait(dve, b, "cos", a)
                    A = sp[:, a, :].rearrange("p (g d) -> p g d", d=DH)
                    if a == 0:
                        wait(dve, b, "eq", -1)
                    elif path[0] is FAST:
                        wait(dve, b, "lo1", a - 1)
                    else:
                        full(dve, b, ("kT1", a - 1, 0))
                    v.tensor_tensor(wk[:, :, 0:DH], A, tt[:, a, :].rearrange("p (g d) -> p g d", d=DH),
                                    ALU.mult).then_inc(sem["w_cos"], 1)
                    v.tensor_tensor(wk[:, :, DH:F], A, sn[:, a, :].rearrange("p (g d) -> p g d", d=DH),
                                    ALU.mult).then_inc(sem["w_sin"], 1)
                    wait(dve, b, "w_cos", a)
                    wait(dve, b, "w_sin", a)
                    if path[0] is EXACT:
                        stack32(b, ("qT1", a, 0), "q1_stacked", a, [q32])
                        stack32(b, ("kT1", a, 0), "k1_stacked", a, [k32[:, 0:JK]])
                        continue
                    if a >= 1:
                        full(dve, b, ("kT1", a - 1, 1))
                    else:
                        full(dve, b, ("kT2", TB - 1, 1), 1)
                    s = stag
                    v.tensor_copy(s[:, :, 0, :], wk[:]).then_inc(sem["hi1"], 1)
                    wait(dve, b, "hi1", a)
                    v.tensor_tensor(s[:, :, 3, :], wk[:], s[:, :, 0, :], ALU.subtract).then_inc(sem["lo1"], 1)
                    wait(dve, b, "lo1", a)
                    v.tensor_copy(s[:, 0:H, 1:3, :], s[:, 0:H, 0:4:3, :]).then_inc(sem["dup1"], 1)
                    v.tensor_copy(s[:, H:, 1, :], s[:, H:, 3, :]).then_inc(sem["dup1"], 1)
                    v.tensor_copy(s[:, H:, 2, :], s[:, H:, 0, :]).then_inc(sem["dup1"], 1)
                    for i in range(2):
                        hs, cs = slice(i * HALF, (i + 1) * HALF), slice(a * P, (a + 1) * P)
                        if a == 0 and i == 0:
                            wait(dve, b, "scores", -1)
                        stack(b, ("qT1", a, i), "q1_stacked", 2 * a + i, q_st[:, hs, cs])
                        stack(b, ("kT1", a, i), "k1_stacked", 2 * a + i, k_st[:, 0, hs, cs])
                if path[0] is EXACT:
                    wait(dve, b, "k1_stacked", TB - 1)
                    wait(dve, b, "attT2_sb", -1)
                    rounds(dve, b, self_chunk, self_block, self_round)
                for q in range(QUADS1 if path[0] is FAST else 0):
                    evacuate_oT(b, q)
                    full(dve, b, ("o1T", q))
                    o = bank(("o1T", q)).rearrange("p (a r c) -> p a r c", a=TB, r=4)
                    if q == 0:
                        wait(dve, b, "ok_cnt", -2)
                        wait(dve, b, "attT2_sb", -1)
                    v.tensor_copy(den1[:, q], o[:, :, :, DH]).then_inc(sem["den1"], 1)
                    wait(dve, b, "den1", q)
                    v.reciprocal(rden1[:], den1[:, q]).then_inc(sem["rden1"], 1)
                    wait(dve, b, "rden1", q)
                    v.tensor_tensor(att[:, :, q * 4 * DH:(q + 1) * 4 * DH].rearrange("p a (r d) -> p a r d", d=DH),
                                    o[:, :, :, 0:DH], rden1[:].unsqueeze(3).broadcast_to((P, TB, 4, DH)), ALU.mult
                                    ).then_inc(sem["att1"], 1)
                if path[0] is FAST:
                    check_den(b, 0, den1[:].rearrange("p q a r -> p (q a r)"), ok_t[:, 0:H * TB])
                for c in range(DC):
                    full(dve, b, ("attT1", c))
                    v.tensor_copy(att_T[:, c, :], bank(("attT1", c))[:, :]).then_inc(sem["attT1_sb"], 1)
                wait(dve, b, "x_in")
                wait(dve, b, "out_st", -1)
                for p in range(2):
                    full(dve, b, ("wo1", p))
                    v.tensor_tensor(flat(y[:, 2 * p:2 * p + 2, :]), bank(("wo1", p))[:, :],
                                    flat(x_tok[:, 2 * p:2 * p + 2, :]), ALU.add).then_inc(sem["y1"], 1)
                for a in range(TB):
                    layer_norm_stats(b, a, y[:, a, :], ("y1", a // 2), 1)
                for a in range(TB):
                    normalise(b, a, x1[:, a, :], y[:, a, :], "ln1_rstd", "x1")
                for c in range(DC):
                    full(dve, b, ("x1T", c))
                    v.tensor_copy(xT2[:, c, :], bank(("x1T", c))[:, :]).then_inc(sem["x1T_sb"], 1)
                for a in range(TB if path[0] is EXACT else 0):
                    for use, part, event in ((("k2", a), slice(H, 2 * H), "k2_split"), (("q2", a), slice(0, H), "q2_split")):
                        full(dve, b, use)
                        if part.start:
                            full(dve, b, ("kT2", a - 1, 0) if a else ("kT1", TB - 1, 0))
                        v.tensor_copy(wk[:, part, :], bank(use).rearrange("p (h f) -> p h f", f=F)
                                      ).then_inc(sem[event], 1)
                        if part.start:
                            full(dve, b, ("v2", a))
                            v.tensor_copy(vals[:, a, :, 0:DH], bank(("v2", a))[:, 0:D].rearrange(
                                "p (h d) -> p h d", d=DH)).then_inc(sem["v2_sb"], 1)
                    stack32(b, ("qT2", a, 0), "q2_stacked", a, [q32])
                    stack32(b, ("kT2", a, 0), "k2_stacked", 2 * a, [k32[:, j * JK:(j + 1) * JK] for j in range(2)])
                if path[0] is EXACT:
                    wait(dve, b, "k2_stacked", 2 * TB - 1)
                    rounds(dve, b, cross_chunk, cross_block, cross_round)
                for a in range(TB if path[0] is FAST else 0):
                    s = stag
                    full(dve, b, ("k2", a))
                    full(dve, b, ("kT2", a - 1, 1) if a >= 1 else ("kT1", TB - 1, 1))
                    src = bank(("k2", a)).rearrange("p (h f) -> p h f", f=F)
                    v.tensor_copy(s[:, H:, 0, :], src).then_inc(sem["k2_hi"], 1)
                    wait(dve, b, "k2_hi", a)
                    v.tensor_tensor(s[:, H:, 3, :], src, s[:, H:, 0, :], ALU.subtract).then_inc(sem["k2_split"], 1)
                    full(dve, b, ("v2", a))
                    v.tensor_copy(vals[:, a, :, 0:DH], bank(("v2", a))[:, 0:D].rearrange("p (h d) -> p h d", d=DH)
                                  ).then_inc(sem["v2_sb"], 1)
                    wait(dve, b, "k2_split", a)
                    v.tensor_copy(s[:, H:, 1, :], s[:, H:, 3, :]).then_inc(sem["k2_dup"], 1)
                    v.tensor_copy(s[:, H:, 2, :], s[:, H:, 0, :]).then_inc(sem["k2_dup"], 1)
                    full(dve, b, ("q2", a))
                    src = bank(("q2", a)).rearrange("p (h f) -> p h f", f=F)
                    v.tensor_copy(s[:, 0:H, 0, :], src).then_inc(sem["q2_hi"], 1)
                    wait(dve, b, "q2_hi", a)
                    v.tensor_tensor(s[:, 0:H, 3, :], src, s[:, 0:H, 0, :], ALU.subtract).then_inc(sem["q2_split"], 1)
                    wait(dve, b, "q2_split", a)
                    v.tensor_copy(s[:, 0:H, 1:3, :], s[:, 0:H, 0:4:3, :]).then_inc(sem["q2_dup"], 1)
                    for i in range(2):
                        hs, cs = slice(i * HALF, (i + 1) * HALF), slice(a * P, (a + 1) * P)
                        stack(b, ("qT2", a, i), "q2_stacked", 2 * a + i, q_st[:, hs, cs])
                        for j in range(2):
                            stack(b, ("kT2", a, i), "k2_stacked", 4 * a + 2 * i + j, k_st[:, j, hs, cs],
                                  half_mask[:, j:j + 1])
                for q in range(QUADS2 if path[0] is FAST else 0):
                    scan_mask(b, 2 * q)
                    evacuate_oT(b, QUADS1 + q)
                    scan_mask(b, 2 * q + 1)
                    full(dve, b, ("o2T", q))
                    v.tensor_copy(o2[:, :, 4 * q:4 * q + 4, :],
                                  bank(("o2T", q)).rearrange("p (a r c) -> p a r c", a=TB, r=4)[:, :, :, 0:DH + 1]
                                  ).then_inc(sem["o2_sb"], 1)
                if path[0] is FAST:
                    differential(b)
                a4 = att[:].rearrange("p a (h d) -> p a h d", d=DH)
                wait(dve, b, "o2_sq")
                v.tensor_reduce(ms2[:], y[:].rearrange("p a (h d) -> p a h d", d=DH), AX.X, ALU.add
                                ).then_inc(sem["o2_ms"], 1)
                wait(dve, b, "rms_r")
                v.tensor_tensor(a4, a4, ms2[:].unsqueeze(3).broadcast_to((P, TB, H, DH)), ALU.mult
                                ).then_inc(sem["att2"], 1)
                if path[0] is FAST:
                    v.tensor_reduce(bad_b[:], mask_bad[:], AX.X, ALU.max).then_inc(sem["bad_max"], 1)
                    wait(dve, b, "bad_max")
                    v.tensor_tensor(bad[:], bad[:], bad_b[:], ALU.max).then_inc(sem["bad_acc"], 1)
                for c in range(DC):
                    full(dve, b, ("attT2", c))
                    v.tensor_copy(att_T[:, c, :], bank(("attT2", c))[:, :]).then_inc(sem["attT2_sb"], 1)
                for p in range(2):
                    full(dve, b, ("wo2", p))
                    v.tensor_tensor(flat(y[:, 2 * p:2 * p + 2, :]), bank(("wo2", p))[:, :],
                                    flat(x1[:, 2 * p:2 * p + 2, :]), ALU.add).then_inc(sem["y2"], 1)
                for a in range(TB):
                    layer_norm_stats(b, a, y[:, a, :], ("y2", a // 2), 2)
                for a in range(TB):
                    normalise(b, a, x2[:, a, :], y[:, a, :], "ln2_rstd", "x2")
                for a in range(TB):
                    wait(dve, b, "x2", a)
                    if a:
                        wait(dve, b, "route", a - 1)
                    v.scalar_tensor_tensor(junk[:, 0:D], x2[:, a, :], 1.0, w_route[:], ALU.mult, ALU.mult,
                                           accum_out=route[:, a:a + 1]).then_inc(sem["route"], 1)
                for c in range(DC):
                    full(dve, b, ("x2T", c))
                    v.tensor_copy(xT2[:, c, :], bank(("x2T", c))[:, :]).then_inc(sem["x2T_sb"], 1)
                full(dve, b, ("srow",))
                srow = att_T[:, 0, :]
                full(dve, b, ("wo2", 1))
                v.tensor_copy(srow, bank(("srow",))[:, :]).then_inc(sem["srow_sb"], 1)
                for p in range(2):
                    full(dve, b, ("ffn", p))
                    v.tensor_copy(h_t[:, p, :], bank(("ffn", p))[:, :]).then_inc(sem["h_sb"], 1)
                wait(dve, b, "srow_sb")
                for a in range(TB):
                    wait(dve, b, "route", TB - 1) if a == 0 else wait(dve, b, "eq", a - 1)
                    v.tensor_scalar(junk[:], srow, route[:, a:a + 1], 0.0, ALU.is_gt, ALU.add,
                                    accum_out=cgt[:, a:a + 1]).then_inc(sem["gt"], 1)
                    wait(dve, b, "gt", a)
                    v.scalar_tensor_tensor(junk[:], srow, route[:, a:a + 1], tie[:, a, :], ALU.is_equal, ALU.mult,
                                           accum_out=ceq[:, a:a + 1]).then_inc(sem["eq"], 1)
                wait(dve, b, "eq", TB - 1)
                v.tensor_tensor(rank[:], cgt[:], ceq[:], ALU.add).then_inc(sem["rank"], 1)
                wait(dve, b, "rank")
                v.tensor_scalar(sel[:], rank[:], float(K_SEL), None, ALU.is_lt).then_inc(sem["sel"], 1)
                wait(dve, b, "sel")
                v.tensor_scalar(keep[:], sel[:], -1.0, 2.0, ALU.mult, ALU.add).then_inc(sem["keep"], 1)
                v.tensor_scalar(hsel[:], sel[:], 0.5, None, ALU.mult).then_inc(sem["half_sel"], 1)
                wait(dve, b, "h_sq")
                v.tensor_scalar(g_t, g_t, GELU_A, 1.0, ALU.mult, ALU.add).then_inc(sem["h_w"], 1)
                wait(dve, b, "h_w")
                v.tensor_tensor(u_t, g_t, h_t, ALU.mult).then_inc(sem["h_u"], 1)
                wait(dve, b, "h_tanh")
                v.scalar_tensor_tensor(g_t, u_t, 1.0, h_t, ALU.add, ALU.mult).then_inc(sem["h_g"], 1)
                wait(dve, b, "h_g")
                wait(dve, b, "half_sel")
                wait(dve, b, "keep")
                g4 = g_t.rearrange("p c (e d) -> p (c e) d", d=D)
                for a in range(TB):
                    v.tensor_scalar(g4[:, a, :], g4[:, a, :], hsel[:, a:a + 1], None, ALU.mult).then_inc(sem["h_gs"], 1)
                    wait(dve, b, "h_gs", a)
                    v.scalar_tensor_tensor(y[:, a, :], x2[:, a, :], keep[:, a:a + 1], g4[:, a, :], ALU.mult, ALU.add
                                           ).then_inc(sem["y3"], 1)
                    layer_norm_stats(b, a, y[:, a, :], ("y3", a), 3)
                for a in range(TB):
                    normalise(b, a, y[:, a, :], y[:, a, :], "ln3_rstd", "out")

            with dve.Fori(0, B) as b:
                body(b)

            dve.wait_ge(sem["ok_acc"], HEAD + B * PER["ok_acc"])
            dve.wait_ge(sem["bad_acc"], B)
            v.tensor_scalar(ok_sum[:], ok_sum[:], float(B * TB * 3 * H), None, ALU.not_equal).then_inc(sem["flag_sum"], 1)
            v.memset(ones1[:], 1.0).then_inc(sem["flag_sum"], 1)
            dve.wait_ge(sem["flag_sum"], 2)
            v.tensor_tensor(bad[:], bad[:], ok_sum[:], ALU.add).then_inc(sem["flag_sum"], 1)
            dve.wait_ge(sem["flag_pe"], 1)
            v.tensor_scalar(flag_f[0:1, :], psO[0][0:1, 0:1], FLAGS_FROM, None, ALU.is_gt).then_inc(sem["flag_sum"], 1)
            dve.wait_ge(sem["flag_sum"], 4)
            v.tensor_copy(flag_i[0:1, :], flag_f[0:1, :]).then_inc(sem["flag"], 1)

            def again(b):
                body(b)

            dve.wait_ge(sem["flag"], 1)
            flag = dve.value_load(flag_i[0:1, 0:1], min_val=0, max_val=1)
            with dve.If(flag > 0):
                path[0] = EXACT
                above = mask_t[:, 1, :].rearrange("p (a k) -> p a k", a=TB)
                v.tensor_scalar(above, tie[:], 1.0, 1e30, ALU.subtract, ALU.mult).then_inc(sem["above"], 1)
                dve.wait_ge(sem["above"], 1)
                for a in range(TB):
                    diag = above[:, a, a * P:(a + 1) * P]
                    v.scalar_tensor_tensor(diag, ident[:], 1e30, diag, ALU.mult, ALU.add).then_inc(sem["above"], 1)
                dve.wait_ge(sem["above"], 1 + TB)
                with dve.Fori(0, B) as b:
                    body(b)
                path[0] = FAST

        @block.tensor
        def _(pe):
            mm = nc.tensor.matmul

            def claim(b, use, waited=None):
                misc = path[0].misc
                n = path[0].use[use]
                bk, prev = n % 2, n - 2
                if prev < 0:
                    prev = max(m for m in range(len(misc)) if m % 2 == bk)
                    event, k = misc[prev][1]
                    wait(pe, b, event, k - count(event))
                elif misc[prev][1][0] != waited:
                    wait(pe, b, *misc[prev][1])

            def project(b, use, lhsT, w, width, col=0, last=True):
                out = bank(use)[:, col:col + width]
                for c in range(DC):
                    i = mm(out, lhsT[:, c, :], w[:, c, 0:width], start=(c == 0), stop=(c == DC - 1))
                if last:
                    i.then_inc(sem["misc_full"], 1)

            def transpose_blocks(b, use, srcs, identity, dt=None):
                out = bank16(use) if dt is f16 else bank(use)
                for n, src in enumerate(srcs):
                    i = nc.tensor.transpose(out[:, n * P:(n + 1) * P], src, identity)
                i.then_inc(sem["misc_full"], 1)

            def token_to_feature(b, name, src):
                for c in range(DC):
                    claim(b, (name, c))
                    transpose_blocks(b, (name, c), [src[:, a, c * P:(c + 1) * P] for a in range(TB)], ident[:])

            def out_project(b, name, srcT, w, waited=None):
                for p in range(2):
                    claim(b, (name, p), waited)
                    for e in range(2):
                        a = 2 * p + e
                        project(b, (name, p), srcT[:, :, a * P:(a + 1) * P], w, D, e * D, last=(e == 1))

            def scores_ready(b, g):
                wait(pe, b, "exps", g - 2)

            def untranspose(b, use, quad):
                wait(pe, b, "oT_sb", quad)
                claim(b, use)
                transpose_blocks(b, use, [oT[:, quad % 2, a * P:(a + 1) * P] for a in range(TB)], ident[:])

            def self_scores(b, q, groups):
                blocks = [[] for _ in range(2 * GROUPS1)]
                for r in range(4):
                    for kb in range(TB):
                        bk, off, w = self_place(r, kb)
                        blocks[bk].append((r, kb, off, w))
                for g in groups:
                    n = q * GROUPS1 + g
                    scores_ready(b, n)
                    for half in range(2):
                        for r, kb, off, w in blocks[2 * g + half]:
                            h = 4 * q + r
                            i = mm(psS[n % 2][:, half * BANK + off:half * BANK + off + w],
                                   k_st[:, 0, h, kb * P:(kb + 1) * P], q_st[:, h, kb * P:S], start=True, stop=True,
                                   skip_group_check=True)
                    i.then_inc(sem["scores"], 1)

            def self_values(b, q):
                wait(pe, b, "causal", 10 * (q + 1) - 1)
                wait(pe, b, "oT_sb", q - 2)
                for kb in range(TB):
                    for r in range(4):
                        bk, off, w = self_place(r, kb)
                        g, half = divmod(bk, 2)
                        c = half * BANK + off
                        i = mm(psO[q % 2][32 * r:32 * r + VW, kb * P:S], vals[:, kb, 4 * q + r, :],
                               ex[:, (q * GROUPS1 + g) % SLOTS, c:c + w], start=(kb == 0), stop=(kb == TB - 1),
                               skip_group_check=True)
                i.then_inc(sem["pv"], 1)

            def cross_group(b, n):
                q, rest = divmod(n - G1, GROUPS2)
                pair, stream = divmod(rest, 4)
                h, j = 2 * q + stream // 2, stream % 2
                scores_ready(b, n)
                for half in range(2):
                    kb = 2 * pair + half
                    i = mm(psS[n % 2][:, half * BANK:(half + 1) * BANK], k_st[:, j, h, kb * P:(kb + 1) * P],
                           q_st[:, h, :], start=True, stop=True)
                i.then_inc(sem["scores"], 1)

            def cross_values(b, m):
                q, pair = divmod(m, 2)
                g0 = G1 + 4 * m
                wait(pe, b, "exps", g0 + 3)
                if pair == 0:
                    wait(pe, b, "oT_sb", QUADS1 + q - 2)
                for half in range(2):
                    kb = 2 * pair + half
                    for stream in range(4):
                        i = mm(psO[q % 2][32 * stream:32 * stream + VW, :], vals[:, kb, 2 * q + stream // 2, :],
                               ex[:, (g0 + stream) % SLOTS, half * BANK:(half + 1) * BANK],
                               start=(kb == 0), stop=(kb == TB - 1), skip_group_check=True)
                i.then_inc(sem["pv"], 1)

            def self_attention(b):
                self_scores(b, 0, range(GROUPS1))
                for q in range(1, QUADS1):
                    self_scores(b, q, range(2))
                    self_values(b, q - 1)
                    self_scores(b, q, range(2, 4))
                    untranspose(b, ("o1T", q - 1), q - 1)
                    self_scores(b, q, range(4, GROUPS1))
                self_values(b, QUADS1 - 1)
                untranspose(b, ("o1T", QUADS1 - 1), QUADS1 - 1)

            def cross_attention(b):
                for m in range(2 * QUADS2):
                    for stream in range(4):
                        cross_group(b, G1 + 4 * m + stream)
                        if stream == 1 and m:
                            cross_values(b, m - 1)
                    if m and m % 2 == 0:
                        untranspose(b, ("o2T", m // 2 - 1), QUADS1 + m // 2 - 1)
                cross_values(b, 2 * QUADS2 - 1)
                untranspose(b, ("o2T", QUADS2 - 1), QUADS1 + QUADS2 - 1)

            def transpose32(b, a, n):
                for name, h0 in (("qT" + n, 0), ("kT" + n, H)):
                    claim(b, (name, a, 0))
                    transpose_blocks(b, (name, a, 0), [flat(wk[:, h0 + 4 * c:h0 + 4 * c + 4, :]) for c in range(NC4)],
                                     ident[:])

            def exact_values(i, c, r, s):
                wait_round(pe, i, s + "_a")
                for kb in range(TB):
                    ins = nc.tensor.transpose(psS[0][:, BANK + kb * P:BANK + (kb + 1) * P], probs[:, kb * P:(kb + 1) * P],
                                              ident[:])
                ins.then_inc(sem[s + "_T"], 1)
                wait_round(pe, i, s + "_aT")
                for kb in range(TB):
                    ins = mm(psO[0][:, 0:DH], probs_T[:, kb * P:(kb + 1) * P],
                             vals[:].rearrange("p a h w -> p (a h w)")[:, bass.ds(c * (4 * VW) + (kb * H + r) * VW, DH)],
                             start=(kb == 0), stop=(kb == TB - 1))
                ins.then_inc(sem[s + "_pv"], 1)

            def self_round(i, c, qb, r):
                rows = slice(32 * r, 32 * r + 32)
                wait_round(pe, i, "s_out", -1)
                mm(psS[0][:, 0:S], q_cur[rows, :], k_cur[rows, 0, :], start=True, stop=True
                   ).then_inc(sem["s_scores"], 1)
                exact_values(i, c, r, "s")

            def cross_round(i, c, qb, r):
                rows = slice(32 * r, 32 * r + 32)
                wait_round(pe, i, "c_out", -1)
                for j in range(2):
                    ins = mm(psS[j][:, 0:S], q_cur[rows, :], k_cur[rows, j, :], start=True, stop=True)
                ins.then_inc(sem["c_scores"], 1)
                exact_values(i, c, r, "c")

            pe.wait_ge(const_in, 16 * N_CONST)
            pe.wait_ge(pool_const, 5 + TB)
            pe.wait_ge(dve_const, 9)

            def body(b):
                wait(pe, b, "xT_in")
                for a in range(TB):
                    ts = slice(a * P, (a + 1) * P)
                    claim(b, ("amp", a))
                    project(b, ("amp", a), xT[:, :, ts], w_amp, 2 * D)
                    claim(b, ("v1", a))
                    project(b, ("v1", a), xT[:, :, ts], w_v1, D)
                for a in range(TB):
                    claim(b, ("phi", a))
                    project(b, ("phi", a), xT[:, :, a * P:(a + 1) * P], w_phi, 2 * D)
                for a in range(TB):
                    if path[0] is EXACT:
                        wait(pe, b, "w_sin", a)
                        transpose32(b, a, "1")
                        continue
                    wait(pe, b, "dup1", 3 * a + 2)
                    s = stag
                    for i in range(2):
                        for name, h0 in (("qT1", 0), ("kT1", H)):
                            claim(b, (name, a, i))
                            transpose_blocks(b, (name, a, i),
                                             [s[:, h0 + i * HALF + h].rearrange("p t f -> p (t f)") for h in range(HALF)],
                                             ident16[:], f16)
                wait(pe, b, "k1_stacked", count("k1_stacked") - 1)
                wait(pe, b, "v1_sb", TB - 1)
                if path[0] is EXACT:
                    rounds(pe, b, nothing, lambda bq, c, qb: pe.wait_ge(sem["s_q"], bq + 1), self_round)
                else:
                    self_attention(b)
                wait(pe, b, "att1", QUADS1 - 1) if path[0] is FAST else pe.wait_ge(
                    sem["s_out"], b * H * TB + H * TB)
                token_to_feature(b, "attT1", att)
                wait(pe, b, "attT1_sb", DC - 1)
                out_project(b, "wo1", att_T, w_o1, "attT1_sb")
                wait(pe, b, "x1", TB - 1)
                token_to_feature(b, "x1T", x1)
                wait(pe, b, "ctx_in")
                wait(pe, b, "x1T_sb", DC - 1)
                for a in range(TB):
                    ts = slice(a * P, (a + 1) * P)
                    claim(b, ("k2", a))
                    project(b, ("k2", a), ctxT[:, :, ts], w_k2, 2 * D)
                    claim(b, ("v2", a))
                    project(b, ("v2", a), ctxT[:, :, ts], w_v2, D)
                    claim(b, ("q2", a))
                    project(b, ("q2", a), xT2[:, :, ts], w_q2, 2 * D)
                    if path[0] is EXACT:
                        wait(pe, b, "q2_split", a)
                        transpose32(b, a, "2")
                        continue
                    wait(pe, b, "q2_dup", a)
                    s = stag
                    for i in range(2):
                        for name, h0 in (("qT2", 0), ("kT2", H)):
                            claim(b, (name, a, i))
                            transpose_blocks(b, (name, a, i),
                                             [s[:, h0 + i * HALF + h].rearrange("p t f -> p (t f)") for h in range(HALF)],
                                             ident16[:], f16)
                wait(pe, b, "k2_stacked", count("k2_stacked") - 1)
                if path[0] is EXACT:
                    rounds(pe, b, nothing, lambda bq, c, qb: pe.wait_ge(sem["c_q"], bq + 1), cross_round)
                else:
                    cross_attention(b)
                wait(pe, b, "att2")
                token_to_feature(b, "attT2", att)
                wait(pe, b, "attT2_sb", DC - 1)
                out_project(b, "wo2", att_T, w_o2, "attT2_sb")
                wait(pe, b, "x2", TB - 1)
                token_to_feature(b, "x2T", x2)
                claim(b, ("srow",))
                wait(pe, b, "route", TB - 1)
                transpose_blocks(b, ("srow",), [route[:, a:a + 1].broadcast_to((P, P)) for a in range(TB)], ident[:])
                wait(pe, b, "x2T_sb", DC - 1)
                out_project(b, "ffn", xT2, w_ffn, "x2T_sb")

            with pe.Fori(0, B) as b:
                body(b)
            pe.wait_ge(sem["flag_sum"], 3)
            mm(psO[0][0:1, 0:1], bad[:], ones1[:], start=True, stop=True).then_inc(sem["flag_pe"], 1)
            if_needed(pe, body)


def kernel(x, ctx_1024, mask_Bx16xSxS2_ff0, L0_attn_Wq_amp, L0_attn_Wk_amp, L0_attn_Wq_phi, L0_attn_Wk_phi, L0_attn_Wv,
           L0_attn_Wo, L0_attn_score_log_scale, L0_xattn_W_q, L0_xattn_W_k, L0_xattn_W_v, L0_xattn_W_o,
           L0_xattn_lambda_q1, L0_xattn_lambda_k1, L0_xattn_lambda_q2, L0_xattn_lambda_k2, L0_xattn_rms_scale,
           L0_ffn_w_router, L0_ffn_w_block):
    import concourse.bacc as bacc
    from concourse.bass_utils import run_bass_kernel_spmd

    def tr(a):
        a = np.asarray(a)
        return np.ascontiguousarray(np.swapaxes(a, -1, -2))

    def plain(a):
        return np.ascontiguousarray(np.asarray(a))

    half_rows = np.zeros((P, 2), np.float32)
    for p in range(P):
        half_rows[p, (p % F) // DH] = 1.0
    arrays = dict(
        x=plain(x), xT=tr(x), ctxT=tr(ctx_1024), mask=plain(mask_Bx16xSxS2_ff0),
        WqaT=tr(L0_attn_Wq_amp), WkaT=tr(L0_attn_Wk_amp), WqpT=tr(L0_attn_Wq_phi), WkpT=tr(L0_attn_Wk_phi),
        WvT=tr(L0_attn_Wv), WoT=tr(L0_attn_Wo), log_scale=plain(L0_attn_score_log_scale),
        xW_q=plain(L0_xattn_W_q), xW_k=plain(L0_xattn_W_k), xW_v=plain(L0_xattn_W_v), xW_o=plain(L0_xattn_W_o),
        lam4=np.stack([np.asarray(a).reshape(-1) for a in (L0_xattn_lambda_q1, L0_xattn_lambda_k1,
                                                           L0_xattn_lambda_q2, L0_xattn_lambda_k2)]),
        rms_tiled=np.tile(np.asarray(L0_xattn_rms_scale), P // DH).reshape(P, 1),
        half_rows=half_rows, w_router=plain(L0_ffn_w_router), w_block=plain(L0_ffn_w_block))
    nc = bacc.Bacc("TRN2", target_bir_lowering=False, num_devices=1)
    tensors = {n: nc.dram_tensor(f"{n}_dram", a.shape, mybir.dt.from_np(a.dtype), kind="ExternalInput").ap()
               for n, a in arrays.items()}
    tensors["out"] = nc.dram_tensor("out_dram", (B, S, D), mybir.dt.float32, kind="ExternalOutput").ap()
    build(nc, tensors)
    r = run_bass_kernel_spmd(nc, [{f"{n}_dram": a for n, a in arrays.items()}], core_ids=[0])
    return r.results[0]["out_dram"]
```

```python
import numpy as np
from contextlib import ExitStack

import concourse.bass as bass
from concourse import mybir

P = 128
B, S, D, H = 8, 512, 256, 16
DH = D // H
TB = S // P
DC = D // P
F = 2 * DH
TERMS = P // F
VW = DH + 1
HALF = H // 2
BANK = 512
K_SEL = int(S * 0.75)
SELF_EPS, LN_EPS, RMS_EPS = 1e-6, 1e-5, 1e-5
LAMBDA_INIT = 0.8
PI_IN = 3.1415925
GELU_C, GELU_A = 0.7978845608028654, 0.044715
TABLES = dict(exp_ln=6, sin_tanh=18)
FLAGS_FROM = 0.0
DEN_LO, DEN_HI = 1e-20, 1e20

QUADS1, QUADS2 = H // 4, H // 2
GROUPS1, GROUPS2 = 5, 8
G1, G2 = QUADS1 * GROUPS1, QUADS2 * GROUPS2
G = G1 + G2
SLOTS = 7
assert G % SLOTS == 0
SETS = QUADS1 + 2 * QUADS2


def self_place(r, kb):
    p, odd = divmod(r, 2)
    bank, off = [[(0, 0), (1, 0), (2, 0), (1, 384)], [(3, 0), (4, 0), (2, 256), (4, 384)]][odd][kb]
    return 5 * p + bank, off, S - kb * P


def set_of(g):
    return g // GROUPS1 if g < G1 else QUADS1 + (g - G1) // 4



STEPS = 2 * QUADS2


def step_uses(m):
    uses = []
    if m and m % 2 == 0:
        uses += [(("o2T", m // 2 - 1), ("o2_sb", m // 2 - 1), "X")]
    if 1 <= m <= TB:
        a = m - 1
        uses += [(("qT2", 1, a), ("q2_stacked", TB + a), "X"), (("kT2", 1, a), ("k2_stacked", 2 * (TB + a) + 1), "X")]
    if m < TB:
        uses += [(("k2", 1, m), ("k2_split", TB + m), "X"), (("q2", 1, m), ("q2_split", TB + m), "X")]
    if TB <= m < 2 * TB:
        uses += [(("amp", m - TB), ("softplus", m - TB), "S"), (("v1", m - TB), ("v1_sb", m - TB), "S")]
    if m == PHI_STEP:
        uses += [(("phi", a), ("tanh", a), "S") for a in range(TB)]
    if m >= STEPS - TB:
        uses += job_uses(0, m - STEPS + TB)
    return uses


def job_uses(half, a):
    return [(("qT1", half, a), ("q1_stacked", half * TB + a), "S"), (("kT1", half, a), ("k1_stacked", half * TB + a), "S")]


PHI_STEP = 9
LOOP_USES = (
    [u for m in range(STEPS) for u in step_uses(m)]
    + [(("o2T", QUADS2 - 1), ("o2_sb", QUADS2 - 1), "X")] + job_uses(1, 0)
    + [(("o1T", 0), ("att1", 0), "S")] + [u for a in range(1, TB) for u in job_uses(1, a)]
    + [(("o1T", 1), ("att1", 1), "S")]
    + [(("attT2", c), ("attT2_sb", c), "X") for c in range(DC)]
    + [(("o1T", 2), ("att1", 2), "S")]
    + [(("wo2", p), ("y2", p), "X") for p in range(2)]
    + [(("o1T", 3), ("att1", 3), "S"), (("k2", 0, 0), ("k2_split", 0), "S")]
    + [(("attT1", c), ("attT1_sb", c), "S") for c in range(DC)]
    + [(("kT2", 0, 0), ("k2_stacked", 1), "S"), (("k2", 0, 1), ("k2_split", 1), "S")]
    + [(("wo1", p), ("y1", p), "S") for p in range(2)]
    + [(("kT2", 0, 1), ("k2_stacked", 3), "S")]
    + [(("x2T", c), ("x2T_sb", c), "X") for c in range(DC)]
    + [(("srow", p), ("srow_sb", p), "X") for p in range(2)]
    + [(("ffn", p), ("h_sb", p), "X") for p in range(2)]
    + [u for a in (2, 3) for u in ((("k2", 0, a), ("k2_split", a), "S"), (("kT2", 0, a), ("k2_stacked", 2 * a + 1), "S"))]
    + [(("x1T", c), ("x1T_sb", c), "S") for c in range(DC)]
    + [(("v2", a), ("v2_sb", a), "S") for a in range(TB)]
    + [(("q2", 0, 0), ("q2_split", 0), "S")]
    + [u for a in range(1, TB) for u in ((("q2", 0, a), ("q2_split", a), "S"), (("qT2", 0, a - 1), ("q2_stacked", a - 1), "S"))]
    + [(("qT2", 0, TB - 1), ("q2_stacked", TB - 1), "S")]
)
assert len(LOOP_USES) % 2 == 0 and {u[2] for u in LOOP_USES[-2:]} == {"S"}

PER = dict(
    xT_in=1, x_in=1, ctx_in=1, mask_in0=H, mask_in1=H, out_st=1,
    misc_full=0, scores=G, exps=G, causal=QUADS1 * 10, pv=SETS, oT_sb=QUADS1 + QUADS2, mask_seen=2 * H,
    abs_x=TB, exp_x=TB, ln_x=TB, softplus=TB, v1_sb=TB, sq1=TB, ss1=TB, rs_ln=1, rs=1, rs_scaled=1, amp_n=TB,
    tanh=TB, sin=TB, abs_t=TB, cos=TB, w_cos=TB, w_sin=TB, hi1=4 * TB, lo1=4 * TB, dup1=6 * TB,
    q1_stacked=2 * TB, k1_stacked=2 * TB, den1=QUADS1, rden1=QUADS1, att1=QUADS1,
    attT1_sb=DC, y1=2, stats1=TB, aggr1=TB, ln1_var=1, ln1_rstd=1, x1=TB, x1T_sb=DC,
    k2_hi=2 * TB, k2_split=2 * TB, k2_dup=4 * TB, v2_sb=TB, q2_hi=2 * TB, q2_split=2 * TB, q2_dup=2 * TB,
    q2_stacked=2 * TB, k2_stacked=4 * TB, o2_sb=QUADS2, rden2=1, rden2_lam=1, o2_norm=1, o2_diff=1, o2_sq=1, o2_ms=1,
    rms_ln=1, rms_r=1, att2=1, attT2_sb=DC, y2=2, stats2=TB, aggr2=TB, ln2_var=1, ln2_rstd=1, x2=TB, x2T_sb=DC,
    route=TB, srow_sb=2, gt=2 * TB - 1, eq=TB, cnt_sum=1, rank=1, sel=1, keep=1, half_sel=1,
    h_sb=2, h_sq=1, h_w=1, h_u=1, h_tanh=1, h_g=1, h_gs=TB, y3=TB, stats3=TB, aggr3=TB, ln3_var=1, ln3_rstd=1, out=TB,
    ok_lo=2, ok_cnt=2, ok_acc=2, bad_max=1, bad_acc=1, wk_cos=0, wk_sin=0,
)

NC4 = H // 4
EXACT_USES = [(use, event, "S") for use, event in (
    [u for a in range(TB) for u in ((("amp", a), ("softplus", a)), (("v1", a), ("v1_sb", a)))]
    + [(("phi", a), ("tanh", a)) for a in range(TB)]
    + [u for a in range(TB) for u in ((("qT1", 0, a), ("q1_stacked", a)), (("kT1", 0, a), ("k1_stacked", a)))]
    + [(("attT1", c), ("attT1_sb", c)) for c in range(DC)]
    + [(("wo1", p), ("y1", p)) for p in range(2)]
    + [(("x1T", c), ("x1T_sb", c)) for c in range(DC)]
    + [u for a in range(TB) for u in (
        (("k2", 0, a), ("k2_split", a)), (("v2", a), ("v2_sb", a)), (("q2", 0, a), ("q2_split", a)),
        (("qT2", 0, a), ("q2_stacked", a)), (("kT2", 0, a), ("k2_stacked", 2 * a + 1)))]
    + [(("attT2", c), ("attT2_sb", c)) for c in range(DC)]
    + [(("wo2", p), ("y2", p)) for p in range(2)]
    + [(("x2T", c), ("x2T_sb", c)) for c in range(DC)]
    + [(("srow", p), ("srow_sb", p)) for p in range(2)]
    + [(("ffn", p), ("h_sb", p)) for p in range(2)])]
assert len(EXACT_USES) % 2 == 0
PER_EXACT = dict(
    PER, scores=0, exps=0, causal=0, pv=0, oT_sb=0, mask_in0=0, mask_in1=0, mask_seen=0,
    hi1=0, lo1=0, dup1=0, q1_stacked=TB, k1_stacked=TB, den1=0, rden1=0, att1=0, k2_hi=0, k2_dup=0, q2_hi=0, q2_dup=0,
    k2_split=TB, q2_split=TB, q2_stacked=TB, k2_stacked=2 * TB, o2_sb=0, rden2=0, rden2_lam=0, o2_norm=0, o2_diff=0,
    ok_lo=0, ok_cnt=0, ok_acc=0, bad_max=0, bad_acc=0, wk_cos=TB, wk_sin=TB)
ROUND = dict(
    s_scores=1, s_z=1, s_max=1, s_exp=1, s_rden=1, s_a=1, s_T=1, s_aT=1, s_pv=1, s_out=1,
    c_mask=1, c_scores=1, c_z=2, c_max=2, c_exp=2, c_rden=1, c_rlam=1, c_a0=1, c_a=1, c_T=1, c_aT=1, c_pv=1, c_out=1)
HEAD = 100
CREDITED = ("mask_seen", "y3", "scores", "pv", "exps", "oT_sb", "bad_max", "ok_acc", "ok_cnt", "attT2_sb", "out_st",
            "tanh", "v1_sb", "x1", "k2_stacked", "v2_sb", "h_sb", "x2", "out", "eq", "k2_split")
DMA_EVENTS = {"xT_in", "x_in", "ctx_in", "mask_in0", "mask_in1", "out_st"}


class Order:

    def __init__(self, uses, kept, base, wraps):
        number, self.bank, self.claims = {}, {}, {}
        last = {} if wraps is None else {n % 2: (*u[1], u[2], wraps) for n, u in enumerate(uses[-2:])}
        for n, (use, event, side) in enumerate(uses):
            if side in kept:
                number[use] = len(number)
                self.bank[use] = n % 2
                self.claims[use] = last.get(n % 2)
                last[n % 2] = (*event, side, None)
        self.number, self.base, self.len = number, base, len(number)


FIRST = Order(LOOP_USES, "S", 0, None)
LOOP = Order(LOOP_USES, "XS", FIRST.len, "b0")
LAST = Order(LOOP_USES, "X", FIRST.len + (B - 1) * LOOP.len, "b0")
AGAIN = Order(EXACT_USES, "S", LAST.base + LAST.len, "before")


class Batch:

    def __init__(self, it, reg, off):
        self.it, self.reg, self.off = it, reg, off

    def at(self, n, const=0):
        return self.off * n + const if self.reg is None else self.reg * n + (self.off * n + const)


class Iteration:

    def __init__(self, order, reg=None, exact=False):
        self.order, self.reg, self.exact = order, reg, exact
        self.x, self.s = order is not FIRST, order is not LAST
        self.b0 = Batch(self, reg, B - 1 if order is LAST else 0)
        self.b1 = self.b0 if exact else Batch(self, reg, 0 if order is FIRST else 1)
        self.per = PER_EXACT if exact else PER


def build(nc, t):
    f32, f16, i32 = mybir.dt.float32, mybir.dt.float16, mybir.dt.int32
    ALU, ACT, AX = mybir.AluOpType, mybir.ActivationFunctionType, mybir.AxisListType

    with ExitStack() as ctx:
        def sb(name, shape, dt=f32):
            return ctx.enter_context(nc.sbuf_tensor(name, [P, *shape], dt))

        def ps(name, words):
            return ctx.enter_context(nc.psum_tensor(name, [P, words], f32))

        sem = {e: ctx.enter_context(nc.semaphore(e)) for e in (*PER, *ROUND, "s_k", "s_q", "c_k", "c_q", "above", "flag_sum", "flag_pe", "flag")}
        const_in, const_ok = (ctx.enter_context(nc.semaphore(n)) for n in ("const_in", "const_ok"))
        passed = ctx.enter_context(nc.semaphore("passed"))
        dve_const, act_const, pool_const = (ctx.enter_context(nc.semaphore(n)) for n in ("dve_const", "act_const", "pool_const"))

        w_amp, w_phi = sb("w_amp", [DC, 2 * D]), sb("w_phi", [DC, 2 * D])
        w_v1, w_o1 = sb("w_v1", [DC, D]), sb("w_o1", [DC, D])
        w_q2, w_k2 = sb("w_q2", [DC, 2 * D]), sb("w_k2", [DC, 2 * D])
        w_v2, w_o2, w_ffn = sb("w_v2", [DC, D]), sb("w_o2", [DC, D]), sb("w_ffn", [DC, D])
        w_route = sb("w_route", [D])
        ident, ident16 = sb("ident", [P]), sb("ident16", [P], f16)
        tie = sb("tie", [P], f16)
        head_scale = sb("head_scale", [H])
        lam_sum = sb("lam_sum", [2, H])
        lam_w = sb("lam_w", [H, 2])
        rms_col = sb("rms_col", [1])
        half_mask = sb("half_mask", [2])

        xT, x_tok, ctxT = sb("xT", [DC, S]), sb("x_tok", [TB, D]), sb("ctxT", [DC, S])
        mask_t = sb("mask_t", [2, 2 * S])
        work = sb("work", [3, TB, 2 * D])
        sp, tt, sn = (work[:, i] for i in range(3))
        ss, rs = sb("ss", [TB, 2 * H]), sb("rs", [TB, 2 * H])
        stag = sb("stag", [2, H, TERMS, F], f16)
        wk = stag[:].rearrange("p j h t f -> p (j h t f)").bitcast(f32)[:, 0:2 * H * F].rearrange(
            "p (h f) -> p h f", f=F)
        q_st, k_st = sb("q_st", [H, S], f16), sb("k_st", [2, H, S], f16)
        vals1, vals2 = sb("vals1", [TB, H, VW]), sb("vals2", [TB, H, VW])
        ex = sb("ex", [SLOTS, 2 * BANK])
        lam_in = ex[:, 0, :].rearrange("p (n d) -> p n d", d=D)
        lam_prod = ex[:, 1, 0:2 * D].rearrange("p (n d) -> p n d", d=D)
        oT = sb("oT", [2, S])
        den1, rden1 = sb("den1", [QUADS1, TB, 4]), sb("rden1", [TB, 4])
        att1, att2, att_T = sb("att1", [TB, D]), sb("att2", [TB, D]), sb("att_T", [DC, S])
        x1, x2 = sb("x1", [TB, D]), sb("x2", [TB, D])
        xT2 = sb("xT2", [DC, S])
        y = sb("y", [TB, D])
        st6, mv, rstd = sb("st6", [3, TB, 6]), sb("mv", [3, TB, 2]), sb("rstd", [3, TB])
        o2 = sb("o2", [TB, 2 * H, DH + 1])
        small = xT2[:].rearrange("p c s -> p (c s)")
        rden2 = small[:, 0:2 * TB * H].rearrange("p (a h j) -> p a h j", a=TB, j=2)
        ok_t = small[:, S:S + 2 * TB * H]
        ms2 = small[:, S - TB * H:S].rearrange("p (a h) -> p a h", a=TB)
        route, cgt, cge, ceq = sb("route", [TB]), sb("cgt", [TB]), sb("cge", [TB]), sb("ceq", [TB])
        rank, sel, keep, hsel = sb("rank", [TB]), sb("sel", [TB]), sb("keep", [TB]), sb("hsel", [TB])
        junk = att2[:].rearrange("p a d -> p (a d)")
        mask_bad, bad, bad_b = sb("mask_bad", [2 * H]), sb("bad", [1]), sb("bad_b", [1])
        ok_n, ok_sum = sb("ok_n", [2]), sb("ok_sum", [1])
        h_t, g_t, u_t = sp[:, 0:2, :], sp[:, 2:4, :], tt[:, 0:2, :]
        flat = lambda a: a.rearrange("p a b -> p (a b)")

        psS = [ps("psS0", 2 * BANK), ps("psS1", 2 * BANK)]
        psO = [ps("psO0", BANK), ps("psO1", BANK)]
        psM = [ps("psM0", BANK), ps("psM1", BANK)]

        def nth(b, event, k=0):
            exact, n, before = b.it.exact, b.it.per[event], 0
            if exact:
                before = B * PER[event]
            scale = 16 if event in DMA_EVENTS else 1
            head = HEAD if event in CREDITED else 0
            assert -HEAD < k < max(n, 1) and (k >= 0 or head or exact) and (n or k < 0), (event, k)
            return sem[event], b.at(n * scale, (before + k + 1) * scale + head)

        def hold(eng):
            eng.sem_inc(passed, 1)

        def bank(b, use):
            return psM[b.it.order.bank[use]]

        def bank16(b, use):
            return bank(b, use)[:, :].bitcast(f16)

        def filled(b, use):
            o = b.it.order
            n = o.base + o.number[use] + 1
            return sem["misc_full"], n if b.it.reg is None else b.it.reg * o.len + n

        def run(eng, body):
            body(Iteration(FIRST))
            with eng.Fori(0, B - 1) as i:
                body(Iteration(LOOP, i))
            body(Iteration(LAST))

        def nth_in_round(i, event, k=0):
            n, scale = ROUND[event], 16 if event == "c_mask" else 1
            return sem[event], i * (n * scale) + (k + 1) * scale

        def rounds(eng, b, chunk_start, block_start, round_):
            hold(eng)
            with eng.Fori(0, NC4) as c:
                bc = b.reg * NC4 + c
                chunk_start(bc, c)
                with eng.Fori(0, TB) as qb:
                    bq = bc * TB + qb
                    block_start(bq, c, qb)
                    for r in range(4):
                        round_(bq * 4 + r, c, qb, r)

        nothing = lambda *a: None

        above = o2[:].rearrange("p a h c -> p (a h c)")[:, 0:TB * S].rearrange("p (a k) -> p a k", a=TB)
        z2 = ex[:, 0, :].rearrange("p (j k) -> p j k", j=2)
        probs, probs_T = ex[:, 1, 0:S], ex[:, 1, S:2 * S]
        q_cur, k_cur = ex[:, 2, 0:P], ex[:, 3, :].rearrange("p (j k) -> p j k", j=2)
        q32 = q_st[:].rearrange("p h s -> p (h s)").bitcast(f32)
        k32 = k_st[:].rearrange("p j h s -> p (j h s)").bitcast(f32)
        JK = NC4 * S
        neg_max, row_sum, row_scale = sb("neg_max", [2]), sb("row_sum", [2]), sb("row_scale", [2])
        minus_half = sb("minus_half", [TB])
        ones1, flag_f, flag_i = sb("ones1", [1]), sb("flag_f", [1]), sb("flag_i", [1], i32)

        def if_needed(eng, body, first=lambda: None):
            eng.wait_ge(sem["flag"], 1)
            flag = eng.value_load(flag_i[0:1, 0:1], min_val=0, max_val=1)
            with eng.If(flag > 0):
                first()
                with eng.Fori(0, B) as i:
                    body(Iteration(AGAIN, i, exact=True))

        block = ctx.enter_context(nc.Block())

        N_CONST, POOL_CONST, DVE_CONST = 16, 7, 12

        @block.sync
        def _(sp_):
            def chunks(name):
                return t[name].rearrange("(c p) n -> p c n", p=P)

            def load(dst, src):
                sp_.dma_start(dst, src).then_inc(const_in, 16)

            load(w_amp[:, :, 0:D], chunks("WqaT"))
            load(w_amp[:, :, D:], chunks("WkaT"))
            load(w_phi[:, :, 0:D], chunks("WqpT"))
            load(w_phi[:, :, D:], chunks("WkpT"))
            load(w_v1[:], chunks("WvT"))
            load(w_o1[:], chunks("WoT"))
            load(w_q2[:], chunks("xW_q"))
            load(w_k2[:], chunks("xW_k"))
            load(w_v2[:], chunks("xW_v"))
            load(w_o2[:], chunks("xW_o"))
            load(w_ffn[:], chunks("w_block"))
            load(w_route[:], t["w_router"].partition_broadcast(P))
            load(head_scale[:], t["log_scale"].partition_broadcast(P))
            load(lam_in[:], t["lam4"].partition_broadcast(P))
            load(rms_col[:], t["rms_tiled"])
            load(half_mask[:], t["half_rows"])
            def load_x(b):
                n = b.at(1)
                sp_.wait_ge(*nth(b, "tanh", -1))
                sp_.dma_start(xT[:], t["xT"][n].rearrange("(c p) s -> p c s", p=P)).then_inc(sem["xT_in"], 16)
                sp_.wait_ge(*nth(b, "x1", -1))
                sp_.dma_start(x_tok[:], t["x"][n].rearrange("(a p) d -> p a d", p=P)).then_inc(sem["x_in"], 16)

            def load_ctx(b):
                n = b.at(1)
                sp_.wait_ge(*nth(b, "k2_split", -1))
                sp_.wait_ge(*nth(b, "v2_sb", -1))
                sp_.dma_start(ctxT[:], t["ctxT"][n].rearrange("(c p) s -> p c s", p=P)).then_inc(sem["ctx_in"], 16)

            def store(b):
                n = b.at(1)
                sp_.wait_ge(*nth(b, "out", TB - 1))
                sp_.dma_start(t["out"][n].rearrange("(a p) d -> p a d", p=P), y[:]).then_inc(sem["out_st"], 16)

            def load_mask(b, batch, n):
                rows = t["mask"][batch, n // 2].rearrange("(p a) k -> p (a k)", p=P)
                sp_.wait_ge(*nth(b, "mask_seen", n - 2))
                sp_.dma_start(mask_t[:, n % 2, :], rows[:, (n % 2) * 2 * S:(n % 2 + 1) * 2 * S]
                              ).then_inc(sem[f"mask_in{n % 2}"], 16)

            CTX_TILE = 10

            def body(it):
                if it.s:
                    load_x(it.b1)
                    if not it.x:
                        load_ctx(it.b1)
                batch = it.b0.at(1)
                for n in range(2 * H if it.x else 0):
                    if n == CTX_TILE and it.s:
                        load_ctx(it.b1)
                    load_mask(it.b0, batch, n)
                if it.x:
                    store(it.b0)

            def again(it):
                def mask_round(i, c, qb, r):
                    sp_.wait_ge(*nth_in_round(i, "c_z", -1))
                    sp_.dma_start(mask_t[:, 0, 0:S], t["mask"][it.reg, c * 4 + r, bass.ds(qb * P, P), :]
                                  ).then_inc(sem["c_mask"], 16)
                load_x(it.b1)
                load_ctx(it.b1)
                rounds(sp_, it.b1, nothing, nothing, mask_round)
                store(it.b1)
                sp_.wait_ge(*nth(it.b1, "out_st"))
                hold(sp_)

            run(sp_, body)
            sp_.wait_ge(sem["out_st"], 16 * B + HEAD)
            if_needed(sp_, again)

        @block.gpsimd
        def _(pool):
            for e in sorted(CREDITED):
                pool.sem_inc(sem[e], HEAD)
            nc.gpsimd.memset(tt[:, :, :], 1.0).then_inc(pool_const, 1)
            nc.gpsimd.memset(minus_half[:], -0.5).then_inc(pool_const, 1)
            for vals in (vals1, vals2):
                nc.gpsimd.memset(vals[:, :, :, DH:VW], 1.0).then_inc(pool_const, 1)
            pool.wait_ge(pool_const, 4)
            nc.gpsimd.affine_select(out=ident[:], in_=tt[:, 0, 0:P], compare_op=ALU.is_equal, fill=0.0, base=0,
                                    pattern=[[-1, P]], channel_multiplier=1).then_inc(pool_const, 1)
            nc.gpsimd.affine_select(out=tie[:], in_=tt[:, 0, 0:P], compare_op=ALU.is_gt, fill=0.0, base=0,
                                    pattern=[[-1, P]], channel_multiplier=1).then_inc(pool_const, 1)
            pool.wait_ge(pool_const, 6)
            nc.gpsimd.tensor_copy(ident16[:], ident[:]).then_inc(pool_const, 1)
            pool.wait_ge(pool_const, POOL_CONST)

            def rotate(b):
                pool.wait_ge(*nth(b, "rs_scaled", 0))
                for a in range(TB):
                    v = sp[:, a, :].rearrange("p (g d) -> p g d", d=DH)
                    nc.gpsimd.tensor_tensor(v, v, rs[:, a, :].unsqueeze(2).broadcast_to((P, 2 * H, DH)), ALU.mult
                                            ).then_inc(sem["amp_n"], 1)
                    pool.wait_ge(*nth(b, "amp_n", a))
                    pool.wait_ge(*nth(b, "cos", a))
                    nc.gpsimd.tensor_tensor(tt[:, a, :], tt[:, a, :], sp[:, a, :], ALU.mult).then_inc(sem["w_cos"], 1)
                    pool.wait_ge(*nth(b, "sin", a))
                    nc.gpsimd.tensor_tensor(sn[:, a, :], sn[:, a, :], sp[:, a, :], ALU.mult).then_inc(sem["w_sin"], 1)

            def causal(b, q):
                def keep_lower(group, view, n):
                    pool.wait_ge(*nth(b, "exps", q * GROUPS1 + group))
                    hold(pool)
                    nc.gpsimd.affine_select(out=view, in_=view, compare_op=ALU.is_ge, fill=0.0, base=0,
                                            pattern=[[0, n], [1, P]], channel_multiplier=-1
                                            ).then_inc(sem["causal"], 1)
                for pair in range(2):
                    for bk, stride, n in ((0, 0, 1), (1, 384, 2), (2, 256, 2), (3, 0, 1), (4, 384, 2)):
                        g, off = divmod(5 * pair + bk, 2)
                        tile = ex[:, (q * GROUPS1 + g) % SLOTS, off * BANK:(off + 1) * BANK]
                        if n == 1:
                            keep_lower(g, tile[:, 0:P].unsqueeze(1), 1)
                        elif stride == 256:
                            keep_lower(g, tile.rearrange("p (n c) -> p n c", n=2)[:, :, 0:P], 2)
                        else:
                            keep_lower(g, tile.rearrange("p (n c) -> p n c", n=4)[:, 0:4:3, :], 2)

            def squares(b):
                if not b.it.exact:
                    pool.wait_ge(*nth(b, "o2_diff", 0))
                pool.wait_ge(*nth(b, "out_st", -1))
                nc.gpsimd.tensor_tensor(y[:], att2[:], att2[:], ALU.mult).then_inc(sem["o2_sq"], 1)

            def layer_norm_rstd(b, n):
                pool.wait_ge(*nth(b, f"aggr{n}", TB - 1))
                hold(pool)
                nc.gpsimd.tensor_scalar(rstd[:, n - 1, :], mv[:, n - 1, :, 1], LN_EPS, None, ALU.add
                                        ).then_inc(sem[f"ln{n}_var"], 1)
                pool.wait_ge(*nth(b, f"ln{n}_var"))
                nc.gpsimd.tensor_tensor(rstd[:, n - 1, :], rstd[:, n - 1, :], minus_half[:], ALU.pow
                                        ).then_inc(sem[f"ln{n}_rstd"], 1)

            def square_amplitudes(b):
                for a in range(TB):
                    pool.wait_ge(*nth(b, "softplus", a))
                    nc.gpsimd.tensor_tensor(sn[:, a, :], sp[:, a, :], sp[:, a, :], ALU.mult).then_inc(sem["sq1"], 1)

            def body(it):
                if it.s:
                    square_amplitudes(it.b1)
                    rotate(it.b1)
                    causal(it.b1, 0)
                    causal(it.b1, 1)
                if it.x:
                    squares(it.b0)
                if it.s:
                    causal(it.b1, 2)
                    causal(it.b1, 3)
                if it.x:
                    layer_norm_rstd(it.b0, 2)
                if it.s:
                    layer_norm_rstd(it.b1, 1)
                if it.x:
                    layer_norm_rstd(it.b0, 3)

            def again(it):
                b = it.b1
                square_amplitudes(b)
                rotate(b)
                layer_norm_rstd(b, 1)
                pool.wait_ge(sem["c_out"], it.reg * (H * TB) + H * TB)
                squares(b)
                layer_norm_rstd(b, 2)
                layer_norm_rstd(b, 3)

            run(pool, body)

            def first_again():
                nc.gpsimd.memset(above, 0.0).then_inc(sem["above"], 1)
                pool.wait_ge(sem["above"], 1)
                for a in range(TB):
                    nc.gpsimd.affine_select(out=above[:, a, :], in_=above[:, a, :], compare_op=ALU.is_ge, fill=-1e30,
                                            base=a * P, pattern=[[-1, S]], channel_multiplier=1).then_inc(sem["above"], 1)
            if_needed(pool, again, first_again)

        @block.scalar
        def _(act):
            def table(functions):
                act.add_instruction(mybir.InstLoadActFuncSet(
                    name=nc.get_next_instruction_name(), engine=mybir.EngineType.Activation,
                    act_func_set_id=TABLES[functions]))

            act.wait_ge(const_in, 16 * N_CONST)
            act.wait_ge(pool_const, POOL_CONST)
            table("exp_ln")
            nc.scalar.activation(head_scale[:], head_scale[:], ACT.Exp).then_inc(act_const, 1)
            act.wait_ge(dve_const, 2)
            nc.scalar.activation(lam_sum[:], lam_sum[:], ACT.Exp).then_inc(act_const, 1)

            def rsqrt(b, out, in_, scale, eps, ready, ln_event, event):
                act.wait_ge(*nth(b, *ready))
                nc.scalar.activation(out, in_, ACT.Ln, bias=eps, scale=scale).then_inc(sem[ln_event], 1)
                act.wait_ge(*nth(b, ln_event))
                nc.scalar.activation(out, out, ACT.Exp, scale=-0.5).then_inc(sem[event], 1)

            def exps(b, groups, scale):
                for g in groups:
                    act.wait_ge(*nth(b, "scores", g))
                    if g >= SLOTS:
                        act.wait_ge(*nth(b, "pv", set_of(g - SLOTS)))
                    else:
                        act.wait_ge(*nth(b, "pv", set_of(G + g - SLOTS) - SETS))
                    nc.scalar.activation(ex[:, g % SLOTS, :], psS[g % 2][:, :], ACT.Exp, scale=scale
                                         ).then_inc(sem["exps"], 1)

            def self_exp(i, c, qb, r):
                act.wait_ge(*nth_in_round(i, "s_max"))
                nc.scalar.activation(z2[:, 0, :], z2[:, 0, :], ACT.Exp, bias=neg_max[:, 0:1],
                                     accum_out=row_sum[:, 0:1]).then_inc(sem["s_exp"], 1)

            def cross_exp(i, c, qb, r):
                for j in range(2):
                    act.wait_ge(*nth_in_round(i, "c_max", j))
                    nc.scalar.activation(z2[:, j, :], z2[:, j, :], ACT.Exp, bias=neg_max[:, j:j + 1],
                                         accum_out=row_sum[:, j:j + 1]).then_inc(sem["c_exp"], 1)

            def log_part(b, a):
                act.wait_ge(*filled(b, ("amp", a)))
                if a == 0:
                    act.wait_ge(*nth(b, "y3", -1 if b.it.exact else -1 - TB))
                nc.scalar.activation(tt[:, a, :], bank(b, ("amp", a))[:, :], ACT.Abs).then_inc(sem["abs_x"], 1)
                act.wait_ge(*nth(b, "abs_x", a))
                nc.scalar.activation(tt[:, a, :], tt[:, a, :], ACT.Exp, scale=-1.0).then_inc(sem["exp_x"], 1)
                act.wait_ge(*nth(b, "exp_x", a))
                nc.scalar.activation(tt[:, a, :], tt[:, a, :], ACT.Ln, bias=1.0).then_inc(sem["ln_x"], 1)

            def phases(b):
                table("sin_tanh")
                for a in range(TB):
                    act.wait_ge(*filled(b, ("phi", a)))
                    act.wait_ge(*nth(b, "softplus", a))
                    nc.scalar.activation(tt[:, a, :], bank(b, ("phi", a))[:, :], ACT.Tanh).then_inc(sem["tanh"], 1)
                for a in range(TB):
                    act.wait_ge(*nth(b, "tanh", a))
                    act.wait_ge(*nth(b, "ss1", a))
                    nc.scalar.activation(sn[:, a, :], tt[:, a, :], ACT.Sin, scale=PI_IN).then_inc(sem["sin"], 1)
                    act.wait_ge(*nth(b, "sin", a))
                    nc.scalar.activation(tt[:, a, :], tt[:, a, :], ACT.Abs).then_inc(sem["abs_t"], 1)
                    act.wait_ge(*nth(b, "abs_t", a))
                    nc.scalar.activation(tt[:, a, :], tt[:, a, :], ACT.Sin, scale=-float(np.pi), bias=float(np.pi / 2)
                                         ).then_inc(sem["cos"], 1)
                table("exp_ln")

            def amplitude_rs(b):
                rsqrt(b, flat(rs[:]), flat(ss[:]), 1.0 / DH, SELF_EPS, ("ss1", TB - 1), "rs_ln", "rs")

            def rms(b):
                rsqrt(b, flat(ms2), flat(ms2), 1.0 / DH, RMS_EPS, ("o2_ms", 0), "rms_ln", "rms_r")

            def gelu(b):
                act.wait_ge(*nth(b, "h_sb", 1))
                nc.scalar.activation(g_t, h_t, ACT.Square).then_inc(sem["h_sq"], 1)
                table("sin_tanh")
                act.wait_ge(*nth(b, "h_u", 0))
                nc.scalar.activation(u_t, u_t, ACT.Tanh, scale=GELU_C).then_inc(sem["h_tanh"], 1)
                table("exp_ln")

            def body(it):
                cross_scale = DH ** -0.5
                for m in range(STEPS):
                    g = G1 + 4 * m
                    if it.x:
                        exps(it.b0, range(g, g + 2), cross_scale)
                    if it.s and TB < m <= 2 * TB:
                        log_part(it.b1, m - TB - 1)
                    if it.x:
                        exps(it.b0, range(g + 2, g + 4), cross_scale)
                    if it.s and m == PHI_STEP:
                        phases(it.b1)
                    if it.s and m == PHI_STEP + 1:
                        amplitude_rs(it.b1)
                if it.s:
                    exps(it.b1, range(3 * GROUPS1), 1.0)
                if it.x:
                    rms(it.b0)
                if it.s:
                    exps(it.b1, range(3 * GROUPS1, G1), 1.0)
                if it.x:
                    gelu(it.b0)

            def again(it):
                b = it.b1
                for a in range(TB):
                    log_part(b, a)
                phases(b)
                amplitude_rs(b)
                rounds(act, b, nothing, nothing, self_exp)
                rounds(act, b, nothing, nothing, cross_exp)
                rms(b)
                gelu(b)

            run(act, body)
            if_needed(act, again)

        @block.vector
        def _(dve):
            v = nc.vector
            dve.wait_ge(const_in, 16 * N_CONST)
            v.tensor_tensor(lam_prod[:], lam_in[:, 0:4:2, :], lam_in[:, 1:4:2, :], ALU.mult).then_inc(dve_const, 1)
            dve.wait_ge(dve_const, 1)
            v.tensor_reduce(lam_sum[:], lam_prod[:].rearrange("p a (h d) -> p a h d", d=DH), AX.X, ALU.add
                            ).then_inc(dve_const, 1)
            v.tensor_scalar(w_o2[:], w_o2[:], rms_col[:], 1.0 - LAMBDA_INIT, ALU.mult, ALU.mult
                            ).then_inc(dve_const, 1)
            v.memset(bad[:], 0.0).then_inc(dve_const, 1)
            v.memset(ok_sum[:], 0.0).then_inc(dve_const, 1)
            v.memset(lam_w[:], 1.0).then_inc(dve_const, 1)
            v.memset(cge[:], 0.0).then_inc(dve_const, 1)
            for bank_o in psO:
                v.memset(bank_o[:, :], 0.0).then_inc(dve_const, 1)
            dve.wait_ge(act_const, 2)
            v.tensor_scalar(head_scale[:], head_scale[:], DH ** -0.5, None, ALU.mult).then_inc(dve_const, 1)
            v.tensor_tensor(lam_sum[:, 0, :], lam_sum[:, 1, :], lam_sum[:, 0, :], ALU.subtract).then_inc(dve_const, 1)
            dve.wait_ge(dve_const, DVE_CONST - 1)
            v.tensor_scalar(lam_w[:, :, 1], lam_sum[:, 0, :], LAMBDA_INIT, None, ALU.subtract).then_inc(dve_const, 1)
            dve.wait_ge(dve_const, DVE_CONST)
            dve.wait_ge(pool_const, POOL_CONST)

            def scan_mask(b, n):
                dve.wait_ge(*nth(b, f"mask_in{n % 2}", n // 2))
                if n == 0:
                    dve.wait_ge(*nth(b, "bad_max", -1))
                v.tensor_scalar(mask_t[:, n % 2, :], mask_t[:, n % 2, :], 0.0, 0.0, ALU.not_equal, ALU.max,
                                accum_out=mask_bad[:, n:n + 1]).then_inc(sem["mask_seen"], 1)

            def layer_norm_stats(b, a, src, ready, n):
                dve.wait_ge(*nth(b, *ready))
                v.bn_stats(st6[:, n - 1, a, :], src).then_inc(sem[f"stats{n}"], 1)
                dve.wait_ge(*nth(b, f"stats{n}", a))
                hold(dve)
                v.bn_aggr(mv[:, n - 1, a, :], st6[:, n - 1, a, :]).then_inc(sem[f"aggr{n}"], 1)

            def normalise(b, a, dst, src, n, event):
                dve.wait_ge(*nth(b, f"ln{n}_rstd"))
                v.tensor_scalar(dst, src, mv[:, n - 1, a, 0:1], rstd[:, n - 1, a:a + 1], ALU.subtract, ALU.mult
                                ).then_inc(sem[event], 1)

            def heads(half):
                return slice(half * HALF, (half + 1) * HALF)

            def stack(b, use, event, k, dst, scale=None):
                dve.wait_ge(*filled(b, use))
                src = bank16(b, use).rearrange("p (h c) -> p h c", h=HALF)
                if scale is None:
                    v.tensor_copy(dst, src).then_inc(sem[event], 1)
                else:
                    v.tensor_scalar(dst, src, scale, None, ALU.mult).then_inc(sem[event], 1)

            def softplus(b, a):
                dve.wait_ge(*filled(b, ("amp", a)))
                dve.wait_ge(*nth(b, "ln_x", a))
                if a == 0:
                    dve.wait_ge(*nth(b, "y3", -1 if b.it.exact else -1 - TB))
                v.scalar_tensor_tensor(sp[:, a, :], bank(b, ("amp", a))[:, :], 0.0, tt[:, a, :], ALU.max, ALU.add
                                       ).then_inc(sem["softplus"], 1)
                values(b, a, "v1", vals1)

            def values(b, a, name, vals):
                dve.wait_ge(*filled(b, (name, a)))
                v.tensor_copy(vals[:, a, :, 0:DH], bank(b, (name, a))[:, 0:D].rearrange("p (h d) -> p h d", d=DH)
                              ).then_inc(sem[name + "_sb"], 1)

            def sum_squares(b, a):
                dve.wait_ge(*nth(b, "sq1", a))
                v.tensor_reduce(ss[:, a, :], sn[:, a, :].rearrange("p (g d) -> p g d", d=DH), AX.X, ALU.add
                                ).then_inc(sem["ss1"], 1)

            def scale_rs(b):
                dve.wait_ge(*nth(b, "rs"))
                v.tensor_tensor(rs[:, :, 0:H], rs[:, :, 0:H], head_scale[:].unsqueeze(1).broadcast_to((P, TB, H)),
                                ALU.mult).then_inc(sem["rs_scaled"], 1)

            def split_self(b, half, a):
                n, s = half * TB + a, stag[:, a % 2]
                dve.wait_ge(*nth(b, "w_cos", a))
                dve.wait_ge(*nth(b, "w_sin", a))

                def parts(qk):
                    c = qk * D + half * (HALF * DH)
                    src = work[:, 1:3, a, c:c + HALF * DH].rearrange("p w (h d) -> p w h d", d=DH)
                    dst = s[:, qk * HALF:(qk + 1) * HALF].rearrange("p h t (w d) -> p t w h d", w=2)
                    return src, dst[:, 0], dst[:, 3]
                for qk in range(2):
                    src, hi, lo = parts(qk)
                    v.tensor_copy(hi, src).then_inc(sem["hi1"], 1)
                for qk in range(2):
                    src, hi, lo = parts(qk)
                    dve.wait_ge(*nth(b, "hi1", 2 * n + qk))
                    v.tensor_tensor(lo, src, hi, ALU.subtract).then_inc(sem["lo1"], 1)
                dve.wait_ge(*nth(b, "lo1", 2 * n))
                v.tensor_copy(s[:, 0:HALF, 1:3, :], s[:, 0:HALF, 0:4:3, :]).then_inc(sem["dup1"], 1)
                dve.wait_ge(*nth(b, "lo1", 2 * n + 1))
                v.tensor_copy(s[:, HALF:, 1, :], s[:, HALF:, 3, :]).then_inc(sem["dup1"], 1)
                v.tensor_copy(s[:, HALF:, 2, :], s[:, HALF:, 0, :]).then_inc(sem["dup1"], 1)

            def stack_self(b, half, a):
                cs = slice(a * P, (a + 1) * P)
                stack(b, ("qT1", half, a), "q1_stacked", half * TB + a, q_st[:, heads(half), cs])
                stack(b, ("kT1", half, a), "k1_stacked", half * TB + a, k_st[:, 0, heads(half), cs])

            def split_k2(b, half, a):
                n, s = half * TB + a, stag[:, a % 2]
                dve.wait_ge(*filled(b, ("k2", half, a)))
                src = bank(b, ("k2", half, a))[:, 0:HALF * F].rearrange("p (h f) -> p h f", f=F)
                v.tensor_copy(s[:, HALF:, 0, :], src).then_inc(sem["k2_hi"], 1)
                dve.wait_ge(*nth(b, "k2_hi", n))
                v.tensor_tensor(s[:, HALF:, 3, :], src, s[:, HALF:, 0, :], ALU.subtract).then_inc(sem["k2_split"], 1)
                dve.wait_ge(*nth(b, "k2_split", n))
                v.tensor_copy(s[:, HALF:, 1, :], s[:, HALF:, 3, :]).then_inc(sem["k2_dup"], 1)
                v.tensor_copy(s[:, HALF:, 2, :], s[:, HALF:, 0, :]).then_inc(sem["k2_dup"], 1)

            def stack_k2(b, half, a):
                for j in range(2):
                    stack(b, ("kT2", half, a), "k2_stacked", 2 * (half * TB + a) + j,
                          k_st[:, j, heads(half), a * P:(a + 1) * P], half_mask[:, j:j + 1])

            def split_q2(b, half, a):
                n, s = half * TB + a, stag[:, a % 2]
                dve.wait_ge(*filled(b, ("q2", half, a)))
                src = bank(b, ("q2", half, a))[:, 0:HALF * F].rearrange("p (h f) -> p h f", f=F)
                v.tensor_copy(s[:, 0:HALF, 0, :], src).then_inc(sem["q2_hi"], 1)
                dve.wait_ge(*nth(b, "q2_hi", n))
                v.tensor_tensor(s[:, 0:HALF, 3, :], src, s[:, 0:HALF, 0, :], ALU.subtract).then_inc(sem["q2_split"], 1)
                dve.wait_ge(*nth(b, "q2_split", n))
                v.tensor_copy(s[:, 0:HALF, 1:3, :], s[:, 0:HALF, 0:4:3, :]).then_inc(sem["q2_dup"], 1)

            def stack_q2(b, half, a):
                stack(b, ("qT2", half, a), "q2_stacked", half * TB + a, q_st[:, heads(half), a * P:(a + 1) * P])

            def evacuate_oT(b, quad):
                dve.wait_ge(*nth(b, "pv", quad if quad < QUADS1 else QUADS1 + 2 * (quad - QUADS1) + 1))
                v.tensor_copy(oT[:, quad % 2, :], psO[quad % 2][:, :]).then_inc(sem["oT_sb"], 1)

            def self_output(b, q):
                dve.wait_ge(*filled(b, ("o1T", q)))
                o = bank(b, ("o1T", q)).rearrange("p (a r c) -> p a r c", a=TB, r=4)
                if q == 0:
                    dve.wait_ge(*nth(b, "ok_cnt", -2))
                v.tensor_copy(den1[:, q], o[:, :, :, DH]).then_inc(sem["den1"], 1)
                dve.wait_ge(*nth(b, "den1", q))
                v.reciprocal(rden1[:], den1[:, q]).then_inc(sem["rden1"], 1)
                dve.wait_ge(*nth(b, "rden1", q))
                v.tensor_tensor(att1[:, :, q * 4 * DH:(q + 1) * 4 * DH].rearrange("p a (r d) -> p a r d", d=DH),
                                o[:, :, :, 0:DH], rden1[:].unsqueeze(3).broadcast_to((P, TB, 4, DH)), ALU.mult
                                ).then_inc(sem["att1"], 1)

            def cross_output(b, q):
                dve.wait_ge(*filled(b, ("o2T", q)))
                v.tensor_copy(o2[:, :, 4 * q:4 * q + 4, :],
                              bank(b, ("o2T", q)).rearrange("p (a r c) -> p a r c", a=TB, r=4)[:, :, :, 0:DH + 1]
                              ).then_inc(sem["o2_sb"], 1)

            def check_den(b, n, dens, scratch):
                if n == 0:
                    dve.wait_ge(*nth(b, "ok_acc", -1))
                v.tensor_scalar(scratch, dens, DEN_LO, None, ALU.is_ge).then_inc(sem["ok_lo"], 1)
                dve.wait_ge(*nth(b, "ok_lo", n))
                v.scalar_tensor_tensor(scratch, dens, DEN_HI, scratch, ALU.is_le, ALU.mult,
                                       accum_out=ok_n[:, n:n + 1]).then_inc(sem["ok_cnt"], 1)
                dve.wait_ge(*nth(b, "ok_cnt", n))
                v.tensor_tensor(ok_sum[:], ok_sum[:], ok_n[:, n:n + 1], ALU.add).then_inc(sem["ok_acc"], 1)

            def differential(b):
                dens = o2[:, :, :, DH]
                dve.wait_ge(*nth(b, "o2_sb", QUADS2 - 1))
                v.reciprocal(rden2.rearrange("p a h j -> p a (h j)"), dens).then_inc(sem["rden2"], 1)
                dve.wait_ge(*nth(b, "rden2"))
                v.tensor_tensor(rden2, rden2, lam_w[:].unsqueeze(1).broadcast_to((P, TB, H, 2)), ALU.mult
                                ).then_inc(sem["rden2_lam"], 1)
                check_den(b, 1, dens, ok_t.rearrange("p (a h) -> p a h", a=TB))
                dve.wait_ge(*nth(b, "rden2_lam"))
                num = o2[:, :, :, 0:DH]
                v.tensor_tensor(num, num, rden2.rearrange("p a h j -> p a (h j)").unsqueeze(3)
                                .broadcast_to((P, TB, 2 * H, DH)), ALU.mult).then_inc(sem["o2_norm"], 1)
                dve.wait_ge(*nth(b, "o2_norm"))
                both = o2[:].rearrange("p a (h j) c -> p a h j c", j=2)
                v.tensor_tensor(att2[:].rearrange("p a (h d) -> p a h d", d=DH), both[:, :, :, 0, 0:DH],
                                both[:, :, :, 1, 0:DH], ALU.add).then_inc(sem["o2_diff"], 1)

            def mean_squares(b):
                dve.wait_ge(*nth(b, "o2_sq"))
                v.tensor_reduce(ms2, y[:].rearrange("p a (h d) -> p a h d", d=DH), AX.X, ALU.add
                                ).then_inc(sem["o2_ms"], 1)

            def rms_norm(b):
                a4 = att2[:].rearrange("p a (h d) -> p a h d", d=DH)
                dve.wait_ge(*nth(b, "rms_r"))
                v.tensor_tensor(a4, a4, ms2.unsqueeze(3).broadcast_to((P, TB, H, DH)), ALU.mult
                                ).then_inc(sem["att2"], 1)

            def collect_mask(b):
                v.tensor_reduce(bad_b[:], mask_bad[:], AX.X, ALU.max).then_inc(sem["bad_max"], 1)
                dve.wait_ge(*nth(b, "bad_max"))
                v.tensor_tensor(bad[:], bad[:], bad_b[:], ALU.max).then_inc(sem["bad_acc"], 1)

            def to_sbuf(b, name, event, dst):
                for c in range(DC):
                    dve.wait_ge(*filled(b, (name, c)))
                    v.tensor_copy(dst[:, c, :], bank(b, (name, c))[:, :]).then_inc(sem[event], 1)

            def add_residual(b, name, event, dst, residual):
                for p in range(2):
                    dve.wait_ge(*filled(b, (name, p)))
                    v.tensor_tensor(flat(dst[:, 2 * p:2 * p + 2, :]), bank(b, (name, p))[:, :],
                                    flat(residual[:, 2 * p:2 * p + 2, :]), ALU.add).then_inc(sem[event], 1)

            def route_scores(b):
                for a in range(TB):
                    dve.wait_ge(*nth(b, "x2", a))
                    if a:
                        dve.wait_ge(*nth(b, "route", a - 1))
                    v.scalar_tensor_tensor(junk[:, 0:D], x2[:, a, :], 1.0, w_route[:], ALU.mult, ALU.mult,
                                           accum_out=route[:, a:a + 1]).then_inc(sem["route"], 1)

            srow = att_T[:, 0, :]

            def row_of_scores(b):
                for p in range(2):
                    dve.wait_ge(*filled(b, ("srow", p)))
                    v.tensor_copy(srow[:, p * 2 * P:(p + 1) * 2 * P], bank(b, ("srow", p))[:, 0:2 * P]
                                  ).then_inc(sem["srow_sb"], 1)

            def hidden(b):
                for p in range(2):
                    dve.wait_ge(*filled(b, ("ffn", p)))
                    v.tensor_copy(h_t[:, p, :], bank(b, ("ffn", p))[:, :]).then_inc(sem["h_sb"], 1)

            def gelu_argument(b):
                dve.wait_ge(*nth(b, "h_sq"))
                v.tensor_scalar(g_t, g_t, GELU_A, 1.0, ALU.mult, ALU.add).then_inc(sem["h_w"], 1)
                dve.wait_ge(*nth(b, "h_w"))
                v.tensor_tensor(u_t, g_t, h_t, ALU.mult).then_inc(sem["h_u"], 1)

            def rank_tokens(b):
                dve.wait_ge(*nth(b, "srow_sb", 1))
                dve.wait_ge(*nth(b, "route", TB - 1))
                for a in range(TB):
                    own, here = route[:, a:a + 1], a * P
                    if a:
                        dve.wait_ge(*nth(b, "gt", 2 * a - 2))
                        v.tensor_scalar(junk[:, 0:here], srow[:, 0:here], own, 0.0, ALU.is_ge, ALU.add,
                                        accum_out=cge[:, a:a + 1]).then_inc(sem["gt"], 1)
                    v.tensor_scalar(junk[:, here:S], srow[:, here:S], own, 0.0, ALU.is_gt, ALU.add,
                                    accum_out=cgt[:, a:a + 1]).then_inc(sem["gt"], 1)
                    if a:
                        dve.wait_ge(*nth(b, "eq", a - 1))
                    v.scalar_tensor_tensor(junk[:, S:S + P], srow[:, here:here + P], own, tie[:], ALU.is_equal, ALU.mult,
                                           accum_out=ceq[:, a:a + 1]).then_inc(sem["eq"], 1)
                dve.wait_ge(*nth(b, "gt", 2 * TB - 2))
                v.tensor_tensor(cgt[:], cgt[:], cge[:], ALU.add).then_inc(sem["cnt_sum"], 1)
                dve.wait_ge(*nth(b, "cnt_sum"))
                dve.wait_ge(*nth(b, "eq", TB - 1))
                v.tensor_tensor(rank[:], cgt[:], ceq[:], ALU.add).then_inc(sem["rank"], 1)
                dve.wait_ge(*nth(b, "rank"))
                v.tensor_scalar(sel[:], rank[:], float(K_SEL), None, ALU.is_lt).then_inc(sem["sel"], 1)
                dve.wait_ge(*nth(b, "sel"))
                v.tensor_scalar(keep[:], sel[:], -1.0, 2.0, ALU.mult, ALU.add).then_inc(sem["keep"], 1)
                v.tensor_scalar(hsel[:], sel[:], 0.5, None, ALU.mult).then_inc(sem["half_sel"], 1)

            def output(b):
                dve.wait_ge(*nth(b, "h_tanh"))
                v.scalar_tensor_tensor(g_t, u_t, 1.0, h_t, ALU.add, ALU.mult).then_inc(sem["h_g"], 1)
                dve.wait_ge(*nth(b, "h_g"))
                dve.wait_ge(*nth(b, "half_sel"))
                dve.wait_ge(*nth(b, "keep"))
                g4 = g_t.rearrange("p c (e d) -> p (c e) d", d=D)
                for a in range(TB):
                    v.tensor_scalar(g4[:, a, :], g4[:, a, :], hsel[:, a:a + 1], None, ALU.mult).then_inc(sem["h_gs"], 1)
                    dve.wait_ge(*nth(b, "h_gs", a))
                    v.scalar_tensor_tensor(y[:, a, :], x2[:, a, :], keep[:, a:a + 1], g4[:, a, :], ALU.mult, ALU.add
                                           ).then_inc(sem["y3"], 1)
                for a in range(TB):
                    layer_norm_stats(b, a, y[:, a, :], ("y3", a), 3)
                for a in range(TB):
                    normalise(b, a, y[:, a, :], y[:, a, :], 3, "out")

            def body(it):
                x, s, b0, b1 = it.x, it.s, it.b0, it.b1
                for m in range(STEPS):
                    if x and m and m % 2 == 0:
                        evacuate_oT(b0, QUADS1 + m // 2 - 1)
                    if x:
                        scan_mask(b0, 2 * m)
                    if s and TB < m <= 2 * TB:
                        softplus(b1, m - TB - 1)
                    if s and TB + 2 <= m < 2 * TB + 2:
                        sum_squares(b1, m - TB - 2)
                    if s and m == PHI_STEP + 2:
                        scale_rs(b1)
                    if s and m == STEPS - TB:
                        split_self(b1, 0, 0)
                        split_self(b1, 0, 1)
                    if s and m > STEPS - TB:
                        a = m - (STEPS - TB) - 1
                        stack_self(b1, 0, a)
                        split_self(b1, (a + 2) // TB, (a + 2) % TB)
                    if x and m and m % 2 == 0:
                        cross_output(b0, m // 2 - 1)
                    if x and 1 <= m <= TB:
                        stack_q2(b0, 1, m - 1)
                        stack_k2(b0, 1, m - 1)
                    if x and m < TB:
                        split_k2(b0, 1, m)
                        split_q2(b0, 1, m)
                    if x:
                        scan_mask(b0, 2 * m + 1)
                if s:
                    stack_self(b1, 0, TB - 1)
                if x:
                    evacuate_oT(b0, QUADS1 + QUADS2 - 1)
                    cross_output(b0, QUADS2 - 1)
                if s:
                    split_self(b1, 1, 1)
                    stack_self(b1, 1, 0)
                    split_self(b1, 1, 2)
                if x:
                    differential(b0)
                    collect_mask(b0)
                if s:
                    evacuate_oT(b1, 0)
                    self_output(b1, 0)
                    stack_self(b1, 1, 1)
                    split_self(b1, 1, 3)
                    stack_self(b1, 1, 2)
                    stack_self(b1, 1, 3)
                    evacuate_oT(b1, 1)
                    self_output(b1, 1)
                if x:
                    mean_squares(b0)
                    rms_norm(b0)
                    to_sbuf(b0, "attT2", "attT2_sb", att_T)
                if s:
                    evacuate_oT(b1, 2)
                    self_output(b1, 2)
                if x:
                    add_residual(b0, "wo2", "y2", y, x1)
                    for a in range(TB):
                        layer_norm_stats(b0, a, y[:, a, :], ("y2", a // 2), 2)
                if s:
                    evacuate_oT(b1, 3)
                    self_output(b1, 3)
                    split_k2(b1, 0, 0)
                    to_sbuf(b1, "attT1", "attT1_sb", att_T)
                    check_den(b1, 0, den1[:].rearrange("p q a r -> p (q a r)"), ok_t[:, 0:H * TB])
                if x:
                    for a in range(TB):
                        normalise(b0, a, x2[:, a, :], y[:, a, :], 2, "x2")
                if s:
                    stack_k2(b1, 0, 0)
                    split_k2(b1, 0, 1)
                if x:
                    route_scores(b0)
                if s:
                    dve.wait_ge(*nth(b1, "x_in"))
                    add_residual(b1, "wo1", "y1", x_tok, x_tok)
                    for a in range(TB):
                        layer_norm_stats(b1, a, x_tok[:, a, :], ("y1", a // 2), 1)
                    stack_k2(b1, 0, 1)
                if x:
                    to_sbuf(b0, "x2T", "x2T_sb", xT2)
                    row_of_scores(b0)
                    hidden(b0)
                if s:
                    for a in range(TB):
                        normalise(b1, a, x1[:, a, :], x_tok[:, a, :], 1, "x1")
                    split_k2(b1, 0, 2)
                    stack_k2(b1, 0, 2)
                    split_k2(b1, 0, 3)
                if x:
                    gelu_argument(b0)
                if s:
                    stack_k2(b1, 0, 3)
                    to_sbuf(b1, "x1T", "x1T_sb", xT2)
                    for a in range(TB):
                        values(b1, a, "v2", vals2)
                    split_q2(b1, 0, 0)
                    for a in range(1, TB):
                        split_q2(b1, 0, a)
                        stack_q2(b1, 0, a - 1)
                    stack_q2(b1, 0, TB - 1)
                if x:
                    rank_tokens(b0)
                    output(b0)

            run(dve, body)

            dve.wait_ge(sem["ok_acc"], HEAD + B * PER["ok_acc"])
            dve.wait_ge(sem["bad_acc"], B)
            v.tensor_scalar(ok_sum[:], ok_sum[:], float(B * TB * 3 * H), None, ALU.not_equal).then_inc(sem["flag_sum"], 1)
            v.memset(ones1[:], 1.0).then_inc(sem["flag_sum"], 1)
            dve.wait_ge(sem["flag_sum"], 2)
            v.tensor_tensor(bad[:], bad[:], ok_sum[:], ALU.add).then_inc(sem["flag_sum"], 1)
            dve.wait_ge(sem["flag_pe"], 1)
            v.tensor_scalar(flag_f[0:1, :], psO[0][0:1, 0:1], FLAGS_FROM, None, ALU.is_gt).then_inc(sem["flag_sum"], 1)
            dve.wait_ge(sem["flag_sum"], 4)
            v.tensor_copy(flag_i[0:1, :], flag_f[0:1, :]).then_inc(sem["flag"], 1)

            def stack32(b, use, event, k0, parts):
                dve.wait_ge(*filled(b, use))
                a = use[2]
                src = bank(b, use).rearrange("p (c s) -> p c s", c=NC4)
                for j, part in enumerate(parts):
                    dst = part[:, 0:JK].rearrange("p (c s) -> p c s", c=NC4)[:, :, a * P:(a + 1) * P]
                    if len(parts) == 1:
                        v.tensor_copy(dst, src).then_inc(sem[event], 1)
                    else:
                        v.tensor_scalar(dst, src, half_mask[:, j:j + 1], None, ALU.mult).then_inc(sem[event], 1)

            def self_chunk(bc, c):
                dve.wait_ge(*nth_in_round(bc * (4 * TB), "s_scores", -1))
                v.tensor_copy(k_cur[:, 0, :], k32[:, bass.ds(c * S, S)]).then_inc(sem["s_k"], 1)

            def cross_chunk(bc, c):
                dve.wait_ge(*nth_in_round(bc * (4 * TB), "c_scores", -1))
                v.tensor_copy(k_cur[:, 0, :], k32[:, bass.ds(c * S, S)]).then_inc(sem["c_k"], 1)
                v.tensor_copy(k_cur[:, 1, :], k32[:, bass.ds(c * S + JK, S)]).then_inc(sem["c_k"], 1)

            def self_block(bq, c, qb):
                dve.wait_ge(*nth_in_round(bq * 4, "s_scores", -1))
                v.tensor_copy(q_cur, q32[:, bass.ds(c * S + qb * P, P)]).then_inc(sem["s_q"], 1)

            def cross_block(bq, c, qb):
                dve.wait_ge(*nth_in_round(bq * 4, "c_scores", -1))
                v.tensor_copy(q_cur, q32[:, bass.ds(c * S + qb * P, P)]).then_inc(sem["c_q"], 1)

            def round_out(i, c, qb, r, s, att):
                dve.wait_ge(*nth_in_round(i, s + "_T"))
                v.tensor_copy(probs_T, psS[0][:, BANK:2 * BANK]).then_inc(sem[s + "_aT"], 1)
                dve.wait_ge(*nth_in_round(i, s + "_pv"))
                v.tensor_copy(flat(att[:])[:, bass.ds(qb * D + c * (4 * DH) + r * DH, DH)], psO[0][:, 0:DH]
                              ).then_inc(sem[s + "_out"], 1)

            def self_round(i, c, qb, r):
                dve.wait_ge(*nth_in_round(i, "s_scores"))
                v.tensor_tensor(z2[:, 0, :], psS[0][:, 0:S], flat(above)[:, bass.ds(qb * S, S)], ALU.add
                                ).then_inc(sem["s_z"], 1)
                dve.wait_ge(*nth_in_round(i, "s_z"))
                v.tensor_reduce(neg_max[:, 0:1], z2[:, 0, :], AX.X, ALU.max, negate=True).then_inc(sem["s_max"], 1)
                dve.wait_ge(*nth_in_round(i, "s_exp"))
                v.reciprocal(row_scale[:, 0:1], row_sum[:, 0:1]).then_inc(sem["s_rden"], 1)
                dve.wait_ge(*nth_in_round(i, "s_rden"))
                v.tensor_scalar(probs, z2[:, 0, :], row_scale[:, 0:1], None, ALU.mult).then_inc(sem["s_a"], 1)
                round_out(i, c, qb, r, "s", att1)

            def cross_round(i, c, qb, r):
                dve.wait_ge(*nth_in_round(i, "c_scores"))
                dve.wait_ge(*nth_in_round(i, "c_mask"))
                for j in range(2):
                    v.scalar_tensor_tensor(z2[:, j, :], psS[j][:, 0:S], DH ** -0.5, mask_t[:, 0, 0:S],
                                           ALU.mult, ALU.add).then_inc(sem["c_z"], 1)
                for j in range(2):
                    dve.wait_ge(*nth_in_round(i, "c_z", j))
                    v.tensor_reduce(neg_max[:, j:j + 1], z2[:, j, :], AX.X, ALU.max, negate=True
                                    ).then_inc(sem["c_max"], 1)
                dve.wait_ge(*nth_in_round(i, "c_exp", 1))
                v.reciprocal(row_scale[:], row_sum[:]).then_inc(sem["c_rden"], 1)
                dve.wait_ge(*nth_in_round(i, "c_rden"))
                v.tensor_tensor(row_scale[:], row_scale[:], flat(lam_w[:])[:, bass.ds(c * 8 + 2 * r, 2)], ALU.mult
                                ).then_inc(sem["c_rlam"], 1)
                dve.wait_ge(*nth_in_round(i, "c_rlam"))
                v.tensor_scalar(z2[:, 0, :], z2[:, 0, :], row_scale[:, 0:1], None, ALU.mult).then_inc(sem["c_a0"], 1)
                dve.wait_ge(*nth_in_round(i, "c_a0"))
                v.scalar_tensor_tensor(probs, z2[:, 1, :], row_scale[:, 1:2], z2[:, 0, :], ALU.mult, ALU.add
                                       ).then_inc(sem["c_a"], 1)
                round_out(i, c, qb, r, "c", att2)

            def again(it):
                b = it.b1
                for a in range(TB):
                    softplus(b, a)
                for a in range(TB):
                    sum_squares(b, a)
                scale_rs(b)
                for a in range(TB):
                    dve.wait_ge(*nth(b, "w_sin", a))
                    for w, event, cols in ((tt, "wk_cos", slice(0, DH)), (sn, "wk_sin", slice(DH, F))):
                        v.tensor_copy(wk[:, :, cols], w[:, a, :].rearrange("p (g d) -> p g d", d=DH)
                                      ).then_inc(sem[event], 1)
                    stack32(b, ("qT1", 0, a), "q1_stacked", a, [q32])
                    stack32(b, ("kT1", 0, a), "k1_stacked", a, [k32[:, 0:JK]])
                dve.wait_ge(*nth(b, "k1_stacked", TB - 1))
                rounds(dve, b, self_chunk, self_block, self_round)
                to_sbuf(b, "attT1", "attT1_sb", att_T)
                dve.wait_ge(*nth(b, "x_in"))
                add_residual(b, "wo1", "y1", x_tok, x_tok)
                for a in range(TB):
                    layer_norm_stats(b, a, x_tok[:, a, :], ("y1", a // 2), 1)
                for a in range(TB):
                    normalise(b, a, x1[:, a, :], x_tok[:, a, :], 1, "x1")
                to_sbuf(b, "x1T", "x1T_sb", xT2)
                for a in range(TB):
                    for use, part, event in ((("k2", 0, a), slice(H, 2 * H), "k2_split"),
                                             (("q2", 0, a), slice(0, H), "q2_split")):
                        dve.wait_ge(*filled(b, use))
                        v.tensor_copy(wk[:, part, :], bank(b, use).rearrange("p (h f) -> p h f", f=F)
                                      ).then_inc(sem[event], 1)
                        if part.start:
                            values(b, a, "v2", vals2)
                    stack32(b, ("qT2", 0, a), "q2_stacked", a, [q32])
                    stack32(b, ("kT2", 0, a), "k2_stacked", 2 * a, [k32[:, j * JK:(j + 1) * JK] for j in range(2)])
                dve.wait_ge(*nth(b, "k2_stacked", 2 * TB - 1))
                rounds(dve, b, cross_chunk, cross_block, cross_round)
                mean_squares(b)
                rms_norm(b)
                to_sbuf(b, "attT2", "attT2_sb", att_T)
                add_residual(b, "wo2", "y2", y, x1)
                for a in range(TB):
                    layer_norm_stats(b, a, y[:, a, :], ("y2", a // 2), 2)
                for a in range(TB):
                    normalise(b, a, x2[:, a, :], y[:, a, :], 2, "x2")
                route_scores(b)
                to_sbuf(b, "x2T", "x2T_sb", xT2)
                row_of_scores(b)
                hidden(b)
                gelu_argument(b)
                rank_tokens(b)
                output(b)

            if_needed(dve, again, lambda: dve.wait_ge(sem["above"], 1 + TB))

        @block.tensor
        def _(pe):
            mm = nc.tensor.matmul

            def claim(b, use, waited=None):
                it = b.it
                last = it.order.claims[use]
                if last is None:
                    return
                event, k, side, crossing = last
                if crossing == "b0":
                    pe.wait_ge(*nth(it.b0, event, k))
                elif crossing == "before":
                    pe.wait_ge(*nth(b, event, k - it.per[event]))
                elif event != waited:
                    pe.wait_ge(*nth(it.b1 if side == "S" else it.b0, event, k))

            def project(b, use, lhsT, w, width, col=0, last=True, w0=0):
                out = bank(b, use)[:, col:col + width]
                for c in range(DC):
                    i = mm(out, lhsT[:, c, :], w[:, c, w0:w0 + width], start=(c == 0), stop=(c == DC - 1))
                if last:
                    i.then_inc(sem["misc_full"], 1)

            def project_block(b, use, srcT, a, w, width, w0=0):
                claim(b, use)
                project(b, use, srcT[:, :, a * P:(a + 1) * P], w, width, w0=w0)

            def transpose_blocks(b, use, srcs, identity, dt=None):
                out = bank16(b, use) if dt is f16 else bank(b, use)
                for n, src in enumerate(srcs):
                    i = nc.tensor.transpose(out[:, n * P:(n + 1) * P], src, identity)
                i.then_inc(sem["misc_full"], 1)

            def token_to_feature(b, name, src):
                for c in range(DC):
                    claim(b, (name, c))
                    transpose_blocks(b, (name, c), [src[:, a, c * P:(c + 1) * P] for a in range(TB)], ident[:])

            def out_project(b, name, srcT, w, waited):
                pe.wait_ge(*nth(b, waited, DC - 1))
                for p in range(2):
                    claim(b, (name, p), waited)
                    for e in range(2):
                        a = 2 * p + e
                        project(b, (name, p), srcT[:, :, a * P:(a + 1) * P], w, D, e * D, last=(e == 1))

            def amplitudes_and_values(b, a):
                if a == 0:
                    pe.wait_ge(*nth(b, "xT_in"))
                project_block(b, ("amp", a), xT, a, w_amp, 2 * D)
                project_block(b, ("v1", a), xT, a, w_v1, D)

            def phases(b):
                for a in range(TB):
                    project_block(b, ("phi", a), xT, a, w_phi, 2 * D)

            def staged(b, name, half, a, kind):
                claim(b, (name, half, a))
                transpose_blocks(b, (name, half, a),
                                 [stag[:, a % 2, kind * HALF + h].rearrange("p t f -> p (t f)") for h in range(HALF)],
                                 ident16[:], f16)

            def self_job(b, half, a):
                pe.wait_ge(*nth(b, "dup1", 3 * (half * TB + a) + 2))
                staged(b, "qT1", half, a, 0)
                staged(b, "kT1", half, a, 1)

            def q2_job(b, half, a):
                pe.wait_ge(*nth(b, "q2_dup", half * TB + a))
                staged(b, "qT2", half, a, 0)

            def k2_job(b, half, a):
                pe.wait_ge(*nth(b, "k2_dup", 2 * (half * TB + a) + 1))
                staged(b, "kT2", half, a, 1)

            def project_k2(b, half, a):
                if half == 0 and a == 0:
                    pe.wait_ge(*nth(b, "ctx_in"))
                project_block(b, ("k2", half, a), ctxT, a, w_k2, D, w0=half * D)

            def project_q2(b, half, a):
                project_block(b, ("q2", half, a), xT2, a, w_q2, D, w0=half * D)

            def scores_ready(b, g):
                pe.wait_ge(*nth(b, "exps", g - 2))

            def untranspose(b, use, quad):
                pe.wait_ge(*nth(b, "oT_sb", quad))
                claim(b, use)
                transpose_blocks(b, use, [oT[:, quad % 2, a * P:(a + 1) * P] for a in range(TB)], ident[:])

            def self_scores(b, q, groups):
                blocks = [[] for _ in range(2 * GROUPS1)]
                for r in range(4):
                    for kb in range(TB):
                        bk, off, w = self_place(r, kb)
                        blocks[bk].append((r, kb, off, w))
                for g in groups:
                    n = q * GROUPS1 + g
                    if g == 0 and q % 2 == 0:
                        half = q // 2
                        pe.wait_ge(*nth(b, "q1_stacked", half * TB + TB - 1))
                        pe.wait_ge(*nth(b, "k1_stacked", half * TB + TB - 1))
                    scores_ready(b, n)
                    for half in range(2):
                        for r, kb, off, w in blocks[2 * g + half]:
                            h = 4 * q + r
                            i = mm(psS[n % 2][:, half * BANK + off:half * BANK + off + w],
                                   k_st[:, 0, h, kb * P:(kb + 1) * P], q_st[:, h, kb * P:S], start=True, stop=True,
                                   skip_group_check=True)
                    i.then_inc(sem["scores"], 1)

            def self_values(b, q):
                pe.wait_ge(*nth(b, "causal", 10 * (q + 1) - 1))
                pe.wait_ge(*nth(b, "oT_sb", q - 2))
                if q == 0:
                    pe.wait_ge(*nth(b, "v1_sb", TB - 1))
                for kb in range(TB):
                    for r in range(4):
                        bk, off, w = self_place(r, kb)
                        g, half = divmod(bk, 2)
                        c = half * BANK + off
                        i = mm(psO[q % 2][32 * r:32 * r + VW, kb * P:S], vals1[:, kb, 4 * q + r, :],
                               ex[:, (q * GROUPS1 + g) % SLOTS, c:c + w], start=(kb == 0), stop=(kb == TB - 1),
                               skip_group_check=True)
                i.then_inc(sem["pv"], 1)

            def cross_group(b, n):
                q, rest = divmod(n - G1, GROUPS2)
                pair, stream = divmod(rest, 4)
                h, j = 2 * q + stream // 2, stream % 2
                if rest == 0 and q % (QUADS2 // 2) == 0:
                    half = q // (QUADS2 // 2)
                    pe.wait_ge(*nth(b, "q2_stacked", half * TB + TB - 1))
                    pe.wait_ge(*nth(b, "k2_stacked", 2 * (half * TB + TB) - 1))
                scores_ready(b, n)
                for half in range(2):
                    kb = 2 * pair + half
                    i = mm(psS[n % 2][:, half * BANK:(half + 1) * BANK], k_st[:, j, h, kb * P:(kb + 1) * P],
                           q_st[:, h, :], start=True, stop=True)
                i.then_inc(sem["scores"], 1)

            def cross_values(b, m):
                q, pair = divmod(m, 2)
                g0 = G1 + 4 * m
                pe.wait_ge(*nth(b, "exps", g0 + 3))
                if pair == 0:
                    pe.wait_ge(*nth(b, "oT_sb", QUADS1 + q - 2))
                if m == 0:
                    pe.wait_ge(*nth(b, "v2_sb", TB - 1))
                for half in range(2):
                    kb = 2 * pair + half
                    for stream in range(4):
                        i = mm(psO[q % 2][32 * stream:32 * stream + VW, :], vals2[:, kb, 2 * q + stream // 2, :],
                               ex[:, (g0 + stream) % SLOTS, half * BANK:(half + 1) * BANK],
                               start=(kb == 0), stop=(kb == TB - 1), skip_group_check=True)
                i.then_inc(sem["pv"], 1)

            def score_row(b):
                for p in range(2):
                    claim(b, ("srow", p))
                    if p == 0:
                        pe.wait_ge(*nth(b, "route", TB - 1))
                    transpose_blocks(b, ("srow", p), [route[:, a:a + 1].broadcast_to((P, P))
                                                      for a in range(2 * p, 2 * p + 2)], ident[:])

            pe.wait_ge(const_in, 16 * N_CONST)
            pe.wait_ge(pool_const, POOL_CONST)
            pe.wait_ge(dve_const, DVE_CONST)

            def body(it):
                x, s, b0, b1 = it.x, it.s, it.b0, it.b1
                for m in range(STEPS):
                    for stream in range(4 if x else 0):
                        cross_group(b0, G1 + 4 * m + stream)
                        if stream == 1 and m:
                            cross_values(b0, m - 1)
                    if x and m and m % 2 == 0:
                        untranspose(b0, ("o2T", m // 2 - 1), QUADS1 + m // 2 - 1)
                    if x and 1 <= m <= TB:
                        q2_job(b0, 1, m - 1)
                        k2_job(b0, 1, m - 1)
                    if x and m < TB:
                        project_k2(b0, 1, m)
                        project_q2(b0, 1, m)
                    if s and TB <= m < 2 * TB:
                        amplitudes_and_values(b1, m - TB)
                    if s and m == PHI_STEP:
                        phases(b1)
                    if s and m >= STEPS - TB:
                        self_job(b1, 0, m - STEPS + TB)
                if s:
                    self_scores(b1, 0, range(2))
                if x:
                    cross_values(b0, STEPS - 1)
                if s:
                    self_scores(b1, 0, range(2, GROUPS1))
                if x:
                    untranspose(b0, ("o2T", QUADS2 - 1), QUADS1 + QUADS2 - 1)
                if s:
                    self_job(b1, 1, 0)
                    self_scores(b1, 1, range(2))
                    self_values(b1, 0)
                    self_scores(b1, 1, range(2, 4))
                    untranspose(b1, ("o1T", 0), 0)
                    self_scores(b1, 1, range(4, GROUPS1))
                    for a in range(1, TB):
                        self_job(b1, 1, a)
                    self_scores(b1, 2, range(2))
                    self_values(b1, 1)
                    self_scores(b1, 2, range(2, 4))
                    untranspose(b1, ("o1T", 1), 1)
                    self_scores(b1, 2, range(4, GROUPS1))
                if x:
                    pe.wait_ge(*nth(b0, "att2"))
                    token_to_feature(b0, "attT2", att2)
                if s:
                    self_scores(b1, 3, range(2))
                    self_values(b1, 2)
                    self_scores(b1, 3, range(2, 4))
                    untranspose(b1, ("o1T", 2), 2)
                    self_scores(b1, 3, range(4, GROUPS1))
                if x:
                    out_project(b0, "wo2", att_T, w_o2, "attT2_sb")
                if s:
                    self_values(b1, 3)
                    untranspose(b1, ("o1T", 3), 3)
                    project_k2(b1, 0, 0)
                    pe.wait_ge(*nth(b1, "att1", QUADS1 - 1))
                    token_to_feature(b1, "attT1", att1)
                    k2_job(b1, 0, 0)
                    project_k2(b1, 0, 1)
                    out_project(b1, "wo1", att_T, w_o1, "attT1_sb")
                    k2_job(b1, 0, 1)
                if x:
                    pe.wait_ge(*nth(b0, "x2", TB - 1))
                    token_to_feature(b0, "x2T", x2)
                    score_row(b0)
                    out_project(b0, "ffn", xT2, w_ffn, "x2T_sb")
                if s:
                    for a in range(2, TB):
                        project_k2(b1, 0, a)
                        k2_job(b1, 0, a)
                    pe.wait_ge(*nth(b1, "x1", TB - 1))
                    token_to_feature(b1, "x1T", x1)
                    for a in range(TB):
                        project_block(b1, ("v2", a), ctxT, a, w_v2, D)
                    pe.wait_ge(*nth(b1, "x1T_sb", DC - 1))
                    project_q2(b1, 0, 0)
                    for a in range(1, TB):
                        project_q2(b1, 0, a)
                        q2_job(b1, 0, a - 1)
                    q2_job(b1, 0, TB - 1)

            run(pe, body)
            pe.wait_ge(sem["flag_sum"], 3)
            mm(psO[0][0:1, 0:1], bad[:], ones1[:], start=True, stop=True).then_inc(sem["flag_pe"], 1)

            def transpose32(b, a, n):
                for name, h0 in (("qT" + n, 0), ("kT" + n, H)):
                    claim(b, (name, 0, a))
                    transpose_blocks(b, (name, 0, a), [flat(wk[:, h0 + 4 * c:h0 + 4 * c + 4, :]) for c in range(NC4)],
                                     ident[:])

            def exact_values(i, c, r, s, vals):
                pe.wait_ge(*nth_in_round(i, s + "_a"))
                for kb in range(TB):
                    ins = nc.tensor.transpose(psS[0][:, BANK + kb * P:BANK + (kb + 1) * P], probs[:, kb * P:(kb + 1) * P],
                                              ident[:])
                ins.then_inc(sem[s + "_T"], 1)
                pe.wait_ge(*nth_in_round(i, s + "_aT"))
                for kb in range(TB):
                    ins = mm(psO[0][:, 0:DH], probs_T[:, kb * P:(kb + 1) * P],
                             vals[:].rearrange("p a h w -> p (a h w)")[:, bass.ds(c * (4 * VW) + (kb * H + r) * VW, DH)],
                             start=(kb == 0), stop=(kb == TB - 1))
                ins.then_inc(sem[s + "_pv"], 1)

            def self_round(i, c, qb, r):
                rows = slice(32 * r, 32 * r + 32)
                pe.wait_ge(*nth_in_round(i, "s_out", -1))
                mm(psS[0][:, 0:S], q_cur[rows, :], k_cur[rows, 0, :], start=True, stop=True
                   ).then_inc(sem["s_scores"], 1)
                exact_values(i, c, r, "s", vals1)

            def cross_round(i, c, qb, r):
                rows = slice(32 * r, 32 * r + 32)
                pe.wait_ge(*nth_in_round(i, "c_out", -1))
                for j in range(2):
                    ins = mm(psS[j][:, 0:S], q_cur[rows, :], k_cur[rows, j, :], start=True, stop=True)
                ins.then_inc(sem["c_scores"], 1)
                exact_values(i, c, r, "c", vals2)

            def again(it):
                b = it.b1
                for a in range(TB):
                    amplitudes_and_values(b, a)
                phases(b)
                for a in range(TB):
                    pe.wait_ge(*nth(b, "wk_cos", a))
                    pe.wait_ge(*nth(b, "wk_sin", a))
                    transpose32(b, a, "1")
                pe.wait_ge(*nth(b, "k1_stacked", TB - 1))
                pe.wait_ge(*nth(b, "v1_sb", TB - 1))
                rounds(pe, b, nothing, lambda bq, c, qb: pe.wait_ge(sem["s_q"], bq + 1), self_round)
                pe.wait_ge(sem["s_out"], b.reg * (H * TB) + H * TB)
                token_to_feature(b, "attT1", att1)
                out_project(b, "wo1", att_T, w_o1, "attT1_sb")
                pe.wait_ge(*nth(b, "x1", TB - 1))
                token_to_feature(b, "x1T", x1)
                pe.wait_ge(*nth(b, "ctx_in"))
                for a in range(TB):
                    project_block(b, ("k2", 0, a), ctxT, a, w_k2, 2 * D)
                    project_block(b, ("v2", a), ctxT, a, w_v2, D)
                    project_block(b, ("q2", 0, a), xT2, a, w_q2, 2 * D)
                    pe.wait_ge(*nth(b, "q2_split", a))
                    transpose32(b, a, "2")
                pe.wait_ge(*nth(b, "k2_stacked", 2 * TB - 1))
                rounds(pe, b, nothing, lambda bq, c, qb: pe.wait_ge(sem["c_q"], bq + 1), cross_round)
                pe.wait_ge(*nth(b, "att2"))
                token_to_feature(b, "attT2", att2)
                out_project(b, "wo2", att_T, w_o2, "attT2_sb")
                pe.wait_ge(*nth(b, "x2", TB - 1))
                token_to_feature(b, "x2T", x2)
                score_row(b)
                out_project(b, "ffn", xT2, w_ffn, "x2T_sb")

            if_needed(pe, again)


def kernel(x, ctx_1024, mask_Bx16xSxS2_ff0, L0_attn_Wq_amp, L0_attn_Wk_amp, L0_attn_Wq_phi, L0_attn_Wk_phi, L0_attn_Wv,
           L0_attn_Wo, L0_attn_score_log_scale, L0_xattn_W_q, L0_xattn_W_k, L0_xattn_W_v, L0_xattn_W_o,
           L0_xattn_lambda_q1, L0_xattn_lambda_k1, L0_xattn_lambda_q2, L0_xattn_lambda_k2, L0_xattn_rms_scale,
           L0_ffn_w_router, L0_ffn_w_block):
    import concourse.bacc as bacc
    from concourse.bass_utils import run_bass_kernel_spmd

    def tr(a):
        a = np.asarray(a)
        return np.ascontiguousarray(np.swapaxes(a, -1, -2))

    def plain(a):
        return np.ascontiguousarray(np.asarray(a))

    half_rows = np.zeros((P, 2), np.float32)
    for p in range(P):
        half_rows[p, (p % F) // DH] = 1.0
    arrays = dict(
        x=plain(x), xT=tr(x), ctxT=tr(ctx_1024), mask=plain(mask_Bx16xSxS2_ff0),
        WqaT=tr(L0_attn_Wq_amp), WkaT=tr(L0_attn_Wk_amp), WqpT=tr(L0_attn_Wq_phi), WkpT=tr(L0_attn_Wk_phi),
        WvT=tr(L0_attn_Wv), WoT=tr(L0_attn_Wo), log_scale=plain(L0_attn_score_log_scale),
        xW_q=plain(L0_xattn_W_q), xW_k=plain(L0_xattn_W_k), xW_v=plain(L0_xattn_W_v), xW_o=plain(L0_xattn_W_o),
        lam4=np.stack([np.asarray(a).reshape(-1) for a in (L0_xattn_lambda_q1, L0_xattn_lambda_k1,
                                                           L0_xattn_lambda_q2, L0_xattn_lambda_k2)]),
        rms_tiled=np.tile(np.asarray(L0_xattn_rms_scale), P // DH).reshape(P, 1),
        half_rows=half_rows, w_router=plain(L0_ffn_w_router), w_block=plain(L0_ffn_w_block))
    nc = bacc.Bacc("TRN2", target_bir_lowering=False, num_devices=1)
    tensors = {n: nc.dram_tensor(f"{n}_dram", a.shape, mybir.dt.from_np(a.dtype), kind="ExternalInput").ap()
               for n, a in arrays.items()}
    tensors["out"] = nc.dram_tensor("out_dram", (B, S, D), mybir.dt.float32, kind="ExternalOutput").ap()
    build(nc, tensors)
    r = run_bass_kernel_spmd(nc, [{f"{n}_dram": a for n, a in arrays.items()}], core_ids=[0])
    return r.results[0]["out_dram"]
```

```python
import numpy as np
from contextlib import ExitStack

import concourse.bass as bass
from concourse import mybir

P = 128
B, S, D, H = 8, 512, 256, 16
DH = D // H
TB = S // P
DC = D // P
F = 2 * DH
TERMS = P // F
VW = DH + 1
HALF = H // 2
BANK = 512
K_SEL = int(S * 0.75)
SELF_EPS, LN_EPS, RMS_EPS = 1e-6, 1e-5, 1e-5
LAMBDA_INIT = 0.8
PI_IN = 3.1415925
GELU_C, GELU_A = 0.7978845608028654, 0.044715
TABLES = dict(exp_ln=6, sin_tanh=18)
FLAGS_FROM = 0.0
DEN_LO, DEN_HI = 1e-20, 1e20

QUADS1, QUADS2 = H // 4, H // 2
GROUPS1, GROUPS2 = 5, 8
G1, G2 = QUADS1 * GROUPS1, QUADS2 * GROUPS2
G = G1 + G2
SLOTS = 7
assert G % SLOTS == 0
SETS = QUADS1 + 2 * QUADS2


def self_place(r, kb):
    p, odd = divmod(r, 2)
    bank, off = [[(0, 0), (1, 0), (2, 0), (1, 384)], [(3, 0), (4, 0), (2, 256), (4, 384)]][odd][kb]
    return 5 * p + bank, off, S - kb * P


def set_of(g):
    return g // GROUPS1 if g < G1 else QUADS1 + (g - G1) // 4


STEPS = 2 * QUADS2
CUT = TB
AMP_STEP = CUT
PHI_STEP = AMP_STEP + 1
TRIG_STEP = PHI_STEP + TB
MASK_LATE = 2 * (STEPS - CUT)
JOB_STEP = STEPS - TB


def late_uses(m):
    uses = []
    if m % 2:
        uses += [(("o2T", (m - 3) // 2), ("o2_sb", (m - 3) // 2), "X")]
    if AMP_STEP <= m < AMP_STEP + TB:
        uses += [(("amp", m - AMP_STEP), ("softplus", m - AMP_STEP), "S")]
    if PHI_STEP <= m < PHI_STEP + TB:
        uses += [(("phi", m - PHI_STEP), ("phi_sb", m - PHI_STEP), "S")]
    if m == TRIG_STEP + 1:
        uses += [(("v1", a), ("v1_sb", a), "S") for a in range(TB)]
    if m >= JOB_STEP:
        uses += job_uses(0, m - JOB_STEP)
    return uses


def job_uses(half, a):
    return [(("qT1", half, a), ("q1_stacked", half * TB + a), "S"), (("kT1", half, a), ("k1_stacked", half * TB + a), "S")]


def early_uses(m):
    uses = []
    if m == 3:
        uses += [(("o2T", 0), ("o2_sb", 0), "S")]
    if m:
        uses += [(("qT2", 1, m - 1), ("q2_stacked", TB + m - 1), "S")]
    uses += [(("k2", 1, m), ("k2_split", TB + m), "S")]
    if m:
        uses += [(("kT2", 1, m - 1), ("k2_stacked", 2 * (TB + m - 1) + 1), "S")]
    uses += [(("q2", 1, m), ("q2_split", TB + m), "S")]
    if m == 0:
        uses += [(("x2T", c), ("x2T_sb", c), "X") for c in range(DC)]
    if m == 1:
        uses += [(("srow", p), ("srow_sb", p), "X") for p in range(2)] + [(("ffn", 0), ("h_sb", 0), "X")]
    if m == 2:
        uses += [(("ffn", 1), ("h_sb", 1), "X")]
    return uses


def k2_use(a):
    return ("k2", 0, a), ("k2_split", a), "S"


def kT2_use(a):
    return ("kT2", 0, a), ("k2_stacked", 2 * a + 1), "S"


def q2_use(a):
    return ("q2", 0, a), ("q2_split", a), "S"


def qT2_use(a):
    return ("qT2", 0, a), ("q2_stacked", a), "S"


LOOP_USES = (
    [u for m in range(CUT, STEPS) for u in late_uses(m)]
    + [(("o2T", QUADS2 - 1), ("o2_sb", QUADS2 - 1), "X")] + job_uses(1, 0)
    + [(("o1T", 0), ("att1", 0), "S")] + [u for a in range(1, TB) for u in job_uses(1, a)]
    + [(("o1T", q), ("att1", q), "S") for q in (1, 2)]
    + [(("attT2", c), ("attT2_sb", c), "X") for c in range(DC)]
    + [(("o1T", 3), ("att1", 3), "S"), (("v2", 0), ("v2_sb", 0), "S")]
    + [(("attT1", c), ("attT1_sb", c), "S") for c in range(DC)] + [(("v2", 1), ("v2_sb", 1), "S")]
    + [(("wo1", p), ("y1", p), "S") for p in range(2)]
    + [(("wo2", p), ("y2", p), "X") for p in range(2)] + [k2_use(0)]
    + [(("x1T", c), ("x1T_sb", c), "S") for c in range(DC)]
    + [kT2_use(0), q2_use(0), q2_use(1), qT2_use(0), qT2_use(1), q2_use(2), k2_use(1),
       q2_use(3), qT2_use(2), k2_use(2), kT2_use(1), qT2_use(3), k2_use(3), kT2_use(2), kT2_use(3)]
    + [(("v2", a), ("v2_sb", a), "S") for a in (2, 3)]
    + [u for m in range(CUT) for u in early_uses(m)]
    + [(("qT2", 1, TB - 1), ("q2_stacked", 2 * TB - 1), "S"), (("kT2", 1, TB - 1), ("k2_stacked", 4 * TB - 1), "S")]
)
assert len(LOOP_USES) % 2 == 0 and {u[2] for u in LOOP_USES[-2:]} == {"S"}

PER = dict(
    xT_in=1, x_in=1, ctx_in=1, mask_in0=H, mask_in1=H, out_st=1,
    misc_full=0, scores=G, exps=G, causal=QUADS1 * 10, pv=SETS, oT_sb=QUADS1 + QUADS2, mask_seen=2 * H,
    abs_x=TB, exp_x=TB, ln_x=TB, softplus=TB, v1_sb=TB, sq1=TB, ss1=TB, rs_ln=1, rs=1, rs_scaled=1, amp_n=TB,
    phi_sb=TB, tanh=2, sin=2, abs_t=2, cos=2, w_cos=TB, w_sin=TB, hi1=4 * TB, lo1=4 * TB, dup1=6 * TB,
    q1_stacked=2 * TB, k1_stacked=2 * TB, den1=QUADS1, rden1=QUADS1, att1=QUADS1,
    attT1_sb=DC, y1=2, stats1=TB, aggr1=TB, ln1_var=1, ln1_rstd=1, x1=TB, x1T_sb=DC,
    k2_hi=2 * TB, k2_split=2 * TB, k2_dup=4 * TB, v2_sb=TB, q2_hi=2 * TB, q2_split=2 * TB, q2_dup=2 * TB,
    q2_stacked=2 * TB, k2_stacked=4 * TB, o2_sb=QUADS2, rden2=1, rden2_lam=1, o2_norm=1, o2_diff=1, o2_sq=1, o2_ms=1,
    rms_ln=1, rms_r=1, att2=1, attT2_sb=DC, y2=2, stats2=TB, aggr2=TB, ln2_var=1, ln2_rstd=1, x2=TB, x2T_sb=DC,
    route=TB, srow_sb=2, gt=2 * TB - 1, eq=TB, cnt_sum=1, rank=1, sel=1, keep=1, half_sel=1,
    h_sb=2, h_sq=1, h_w=1, h_u=1, h_tanh=1, h_g=1, h_gs=TB, y3=TB, stats3=TB, aggr3=TB, ln3_var=1, ln3_rstd=1, out=TB,
    ok_lo=2, ok_cnt=2, ok_acc=2, bad_max=1, bad_acc=1, wk_cos=0, wk_sin=0,
)

NC4 = H // 4
EXACT_USES = [(use, event, "S") for use, event in (
    [u for a in range(TB) for u in ((("amp", a), ("softplus", a)), (("v1", a), ("v1_sb", a)))]
    + [(("phi", a), ("phi_sb", a)) for a in range(TB)]
    + [u for a in range(TB) for u in ((("qT1", 0, a), ("q1_stacked", a)), (("kT1", 0, a), ("k1_stacked", a)))]
    + [(("attT1", c), ("attT1_sb", c)) for c in range(DC)]
    + [(("wo1", p), ("y1", p)) for p in range(2)]
    + [(("x1T", c), ("x1T_sb", c)) for c in range(DC)]
    + [u for a in range(TB) for u in (
        (("k2", 0, a), ("k2_split", a)), (("v2", a), ("v2_sb", a)), (("q2", 0, a), ("q2_split", a)),
        (("qT2", 0, a), ("q2_stacked", a)), (("kT2", 0, a), ("k2_stacked", 2 * a + 1)))]
    + [(("attT2", c), ("attT2_sb", c)) for c in range(DC)]
    + [(("wo2", p), ("y2", p)) for p in range(2)]
    + [(("x2T", c), ("x2T_sb", c)) for c in range(DC)]
    + [(("srow", p), ("srow_sb", p)) for p in range(2)]
    + [(("ffn", p), ("h_sb", p)) for p in range(2)])]
assert len(EXACT_USES) % 2 == 0
PER_EXACT = dict(
    PER, scores=0, exps=0, causal=0, pv=0, oT_sb=0, mask_in0=0, mask_in1=0, mask_seen=0,
    hi1=0, lo1=0, dup1=0, q1_stacked=TB, k1_stacked=TB, den1=0, rden1=0, att1=0, k2_hi=0, k2_dup=0, q2_hi=0, q2_dup=0,
    k2_split=TB, q2_split=TB, q2_stacked=TB, k2_stacked=2 * TB, o2_sb=0, rden2=0, rden2_lam=0, o2_norm=0, o2_diff=0,
    ok_lo=0, ok_cnt=0, ok_acc=0, bad_max=0, bad_acc=0, wk_cos=TB, wk_sin=TB)
ROUND = dict(
    s_scores=1, s_z=1, s_max=1, s_exp=1, s_rden=1, s_a=1, s_T=1, s_aT=1, s_pv=1, s_out=1,
    c_mask=1, c_scores=1, c_z=2, c_max=2, c_exp=2, c_rden=1, c_rlam=1, c_a0=1, c_a=1, c_T=1, c_aT=1, c_pv=1, c_out=1)
HEAD = 100
CREDITED = ("mask_seen", "y3", "scores", "pv", "exps", "oT_sb", "bad_max", "ok_acc", "ok_cnt", "attT2_sb",
            "phi_sb", "v1_sb", "x1", "k2_stacked", "v2_sb", "h_sb", "x2", "out", "eq", "k2_split")
DMA_EVENTS = {"xT_in", "x_in", "ctx_in", "mask_in0", "mask_in1", "out_st"}


class Order:

    def __init__(self, uses, kept, base, wraps):
        number, self.bank, self.claims = {}, {}, {}
        last = {} if wraps is None else {n % 2: (*u[1], u[2], wraps) for n, u in enumerate(uses[-2:])}
        for n, (use, event, side) in enumerate(uses):
            if side in kept:
                number[use] = len(number)
                self.bank[use] = n % 2
                self.claims[use] = last.get(n % 2)
                last[n % 2] = (*event, side, None)
        self.number, self.base, self.len = number, base, len(number)


FIRST = Order(LOOP_USES, "S", 0, None)
LOOP = Order(LOOP_USES, "XS", FIRST.len, "b0")
LAST = Order(LOOP_USES, "X", FIRST.len + (B - 1) * LOOP.len, "b0")
AGAIN = Order(EXACT_USES, "S", LAST.base + LAST.len, "before")


class Batch:

    def __init__(self, it, reg, off):
        self.it, self.reg, self.off = it, reg, off

    def at(self, n, const=0):
        return self.off * n + const if self.reg is None else self.reg * n + (self.off * n + const)


class Iteration:

    def __init__(self, order, reg=None, exact=False):
        self.order, self.reg, self.exact = order, reg, exact
        self.x, self.s = order is not FIRST, order is not LAST
        self.b0 = Batch(self, reg, B - 1 if order is LAST else 0)
        self.b1 = self.b0 if exact else Batch(self, reg, 0 if order is FIRST else 1)
        self.per = PER_EXACT if exact else PER


def build(nc, t):
    f32, f16, i32 = mybir.dt.float32, mybir.dt.float16, mybir.dt.int32
    ALU, ACT, AX = mybir.AluOpType, mybir.ActivationFunctionType, mybir.AxisListType

    with ExitStack() as ctx:
        def sb(name, shape, dt=f32):
            return ctx.enter_context(nc.sbuf_tensor(name, [P, *shape], dt))

        def ps(name, words):
            return ctx.enter_context(nc.psum_tensor(name, [P, words], f32))

        sem = {e: ctx.enter_context(nc.semaphore(e)) for e in (*PER, *ROUND, "s_k", "s_q", "c_k", "c_q", "above", "flag_sum", "flag_pe", "flag")}
        const_in, const_ok = (ctx.enter_context(nc.semaphore(n)) for n in ("const_in", "const_ok"))
        passed = ctx.enter_context(nc.semaphore("passed"))
        dve_const, act_const, pool_const = (ctx.enter_context(nc.semaphore(n)) for n in ("dve_const", "act_const", "pool_const"))

        w_amp, w_phi = sb("w_amp", [DC, 2 * D]), sb("w_phi", [DC, 2 * D])
        w_v1, w_o1 = sb("w_v1", [DC, D]), sb("w_o1", [DC, D])
        w_q2, w_k2 = sb("w_q2", [DC, 2 * D]), sb("w_k2", [DC, 2 * D])
        w_v2, w_o2, w_ffn = sb("w_v2", [DC, D]), sb("w_o2", [DC, D]), sb("w_ffn", [DC, D])
        w_route = sb("w_route", [D])
        ident, ident16 = sb("ident", [P]), sb("ident16", [P], f16)
        tie = sb("tie", [P], f16)
        head_scale = sb("head_scale", [H])
        lam_sum = sb("lam_sum", [2, H])
        lam_w = sb("lam_w", [H, 2])
        rms_col = sb("rms_col", [1])
        half_mask = sb("half_mask", [2])

        xT, x_tok, ctxT = sb("xT", [DC, S]), sb("x_tok", [TB, D]), sb("ctxT", [DC, S])
        mask_t = sb("mask_t", [2, 2 * S])
        work = sb("work", [3, TB, 2 * D])
        sp, tt, sn = (work[:, i] for i in range(3))
        ss, rs = sb("ss", [TB, 2 * H]), sb("rs", [TB, 2 * H])
        stag = sb("stag", [2, H, TERMS, F], f16)
        wk = stag[:].rearrange("p j h t f -> p (j h t f)").bitcast(f32)[:, 0:2 * H * F].rearrange(
            "p (h f) -> p h f", f=F)
        q_st, k_st = sb("q_st", [H, S], f16), sb("k_st", [2, H, S], f16)
        vals1, vals2 = sb("vals1", [TB, H, VW]), sb("vals2", [TB, H, VW])
        ex = sb("ex", [SLOTS, 2 * BANK])
        lam_in = ex[:, 0, :].rearrange("p (n d) -> p n d", d=D)
        lam_prod = ex[:, 1, 0:2 * D].rearrange("p (n d) -> p n d", d=D)
        oT = sb("oT", [2, S])
        den1, rden1 = sb("den1", [QUADS1, TB, 4]), sb("rden1", [TB, 4])
        att1, att2, att_T = sb("att1", [TB, D]), sb("att2", [TB, D]), sb("att_T", [DC, S])
        x1, x2 = sb("x1", [TB, D]), sb("x2", [TB, D])
        xT2 = sb("xT2", [DC, S])
        y = sb("y", [TB, D])
        st6, mv, rstd = sb("st6", [3, TB, 6]), sb("mv", [3, TB, 2]), sb("rstd", [3, TB])
        o2 = sb("o2", [TB, 2 * H, DH + 1])
        small = xT2[:].rearrange("p c s -> p (c s)")
        rden2 = small[:, 0:2 * TB * H].rearrange("p (a h j) -> p a h j", a=TB, j=2)
        ok_t = small[:, S:S + 2 * TB * H]
        ms2 = small[:, S - TB * H:S].rearrange("p (a h) -> p a h", a=TB)
        route, cgt, cge, ceq = sb("route", [TB]), sb("cgt", [TB]), sb("cge", [TB]), sb("ceq", [TB])
        rank, sel, keep, hsel = sb("rank", [TB]), sb("sel", [TB]), sb("keep", [TB]), sb("hsel", [TB])
        junk = att2[:].rearrange("p a d -> p (a d)")
        mask_bad, bad, bad_b = sb("mask_bad", [2 * H]), sb("bad", [1]), sb("bad_b", [1])
        ok_n, ok_sum = sb("ok_n", [2]), sb("ok_sum", [1])
        h_t, g_t, u_t = sp[:, 0:2, :], sp[:, 2:4, :], tt[:, 0:2, :]
        flat = lambda a: a.rearrange("p a b -> p (a b)")

        psS = [ps("psS0", 2 * BANK), ps("psS1", 2 * BANK)]
        psO = [ps("psO0", BANK), ps("psO1", BANK)]
        psM = [ps("psM0", BANK), ps("psM1", BANK)]

        def nth(b, event, k=0):
            exact, n, before = b.it.exact, b.it.per[event], 0
            if exact:
                before = B * PER[event]
            scale = 16 if event in DMA_EVENTS else 1
            head = HEAD if event in CREDITED else 0
            assert -HEAD < k < max(n, 1) and (k >= -1 or head or exact) and (n or k < 0), (event, k)
            return sem[event], b.at(n * scale, (before + k + 1) * scale + head)

        def hold(eng):
            eng.sem_inc(passed, 1)

        def bank(b, use):
            return psM[b.it.order.bank[use]]

        def bank16(b, use):
            return bank(b, use)[:, :].bitcast(f16)

        def filled(b, use):
            o = b.it.order
            n = o.base + o.number[use] + 1
            return sem["misc_full"], n if b.it.reg is None else b.it.reg * o.len + n

        def run(eng, body):
            body(Iteration(FIRST))
            with eng.Fori(0, B - 1) as i:
                body(Iteration(LOOP, i))
            body(Iteration(LAST))

        def nth_in_round(i, event, k=0):
            n, scale = ROUND[event], 16 if event == "c_mask" else 1
            return sem[event], i * (n * scale) + (k + 1) * scale

        def rounds(eng, b, chunk_start, block_start, round_):
            hold(eng)
            with eng.Fori(0, NC4) as c:
                bc = b.reg * NC4 + c
                chunk_start(bc, c)
                with eng.Fori(0, TB) as qb:
                    bq = bc * TB + qb
                    block_start(bq, c, qb)
                    for r in range(4):
                        round_(bq * 4 + r, c, qb, r)

        nothing = lambda *a: None

        above = o2[:].rearrange("p a h c -> p (a h c)")[:, 0:TB * S].rearrange("p (a k) -> p a k", a=TB)
        z2 = ex[:, 0, :].rearrange("p (j k) -> p j k", j=2)
        probs, probs_T = ex[:, 1, 0:S], ex[:, 1, S:2 * S]
        q_cur, k_cur = ex[:, 2, 0:P], ex[:, 3, :].rearrange("p (j k) -> p j k", j=2)
        q32 = q_st[:].rearrange("p h s -> p (h s)").bitcast(f32)
        k32 = k_st[:].rearrange("p j h s -> p (j h s)").bitcast(f32)
        JK = NC4 * S
        neg_max, row_sum, row_scale = sb("neg_max", [2]), sb("row_sum", [2]), sb("row_scale", [2])
        minus_half = sb("minus_half", [TB])
        ones1, flag_f, flag_i = sb("ones1", [1]), sb("flag_f", [1]), sb("flag_i", [1], i32)

        def if_needed(eng, body, first=lambda: None):
            eng.wait_ge(sem["flag"], 1)
            flag = eng.value_load(flag_i[0:1, 0:1], min_val=0, max_val=1)
            with eng.If(flag > 0):
                first()
                with eng.Fori(0, B) as i:
                    body(Iteration(AGAIN, i, exact=True))

        block = ctx.enter_context(nc.Block())

        N_CONST, POOL_CONST, DVE_CONST = 16, 7, 12

        @block.sync
        def _(sp_):
            def chunks(name):
                return t[name].rearrange("(c p) n -> p c n", p=P)

            def load(dst, src):
                sp_.dma_start(dst, src).then_inc(const_in, 16)

            load(w_amp[:, :, 0:D], chunks("WqaT"))
            load(w_amp[:, :, D:], chunks("WkaT"))
            load(w_phi[:, :, 0:D], chunks("WqpT"))
            load(w_phi[:, :, D:], chunks("WkpT"))
            load(w_v1[:], chunks("WvT"))
            load(w_o1[:], chunks("WoT"))
            load(w_q2[:], chunks("xW_q"))
            load(w_k2[:], chunks("xW_k"))
            load(w_v2[:], chunks("xW_v"))
            load(w_o2[:], chunks("xW_o"))
            load(w_ffn[:], chunks("w_block"))
            load(w_route[:], t["w_router"].partition_broadcast(P))
            load(head_scale[:], t["log_scale"].partition_broadcast(P))
            load(lam_in[:], t["lam4"].partition_broadcast(P))
            load(rms_col[:], t["rms_tiled"])
            load(half_mask[:], t["half_rows"])
            def load_x(b):
                n = b.at(1)
                sp_.wait_ge(*nth(b, "phi_sb", -1))
                sp_.wait_ge(*nth(b, "v1_sb", -1))
                sp_.dma_start(xT[:], t["xT"][n].rearrange("(c p) s -> p c s", p=P)).then_inc(sem["xT_in"], 16)
                sp_.wait_ge(*nth(b, "x1", -1))
                sp_.dma_start(x_tok[:], t["x"][n].rearrange("(a p) d -> p a d", p=P)).then_inc(sem["x_in"], 16)

            def load_ctx(b):
                n = b.at(1)
                sp_.wait_ge(*nth(b, "k2_split", -1))
                sp_.wait_ge(*nth(b, "v2_sb", -1))
                sp_.dma_start(ctxT[:], t["ctxT"][n].rearrange("(c p) s -> p c s", p=P)).then_inc(sem["ctx_in"], 16)

            def load_mask(b, batch, n):
                rows = t["mask"][batch, n // 2].rearrange("(p a) k -> p (a k)", p=P)
                sp_.wait_ge(*nth(b, "mask_seen", n - 2))
                sp_.dma_start(mask_t[:, n % 2, :], rows[:, (n % 2) * 2 * S:(n % 2 + 1) * 2 * S]
                              ).then_inc(sem[f"mask_in{n % 2}"], 16)

            def body(it):
                if it.s:
                    load_x(it.b1)
                    load_ctx(it.b1)
                for n in range(2 * H if it.x else 0):
                    load_mask(it.b0, it.b0.at(1), n)

            def again(it):
                def mask_round(i, c, qb, r):
                    sp_.wait_ge(*nth_in_round(i, "c_z", -1))
                    sp_.dma_start(mask_t[:, 0, 0:S], t["mask"][it.reg, c * 4 + r, bass.ds(qb * P, P), :]
                                  ).then_inc(sem["c_mask"], 16)
                load_x(it.b1)
                load_ctx(it.b1)
                rounds(sp_, it.b1, nothing, nothing, mask_round)

            run(sp_, body)
            if_needed(sp_, again)

        @block.gpsimd
        def _(pool):
            for e in sorted(CREDITED):
                pool.sem_inc(sem[e], HEAD)
            nc.gpsimd.memset(tt[:, :, :], 1.0).then_inc(pool_const, 1)
            nc.gpsimd.memset(minus_half[:], -0.5).then_inc(pool_const, 1)
            for vals in (vals1, vals2):
                nc.gpsimd.memset(vals[:, :, :, DH:VW], 1.0).then_inc(pool_const, 1)
            pool.wait_ge(pool_const, 4)
            nc.gpsimd.affine_select(out=ident[:], in_=tt[:, 0, 0:P], compare_op=ALU.is_equal, fill=0.0, base=0,
                                    pattern=[[-1, P]], channel_multiplier=1).then_inc(pool_const, 1)
            nc.gpsimd.affine_select(out=tie[:], in_=tt[:, 0, 0:P], compare_op=ALU.is_gt, fill=0.0, base=0,
                                    pattern=[[-1, P]], channel_multiplier=1).then_inc(pool_const, 1)
            pool.wait_ge(pool_const, 6)
            nc.gpsimd.tensor_copy(ident16[:], ident[:]).then_inc(pool_const, 1)
            pool.wait_ge(pool_const, POOL_CONST)

            def rotate(b):
                pool.wait_ge(*nth(b, "rs_scaled", 0))
                for a in range(TB):
                    v = sp[:, a, :].rearrange("p (g d) -> p g d", d=DH)
                    nc.gpsimd.tensor_tensor(v, v, rs[:, a, :].unsqueeze(2).broadcast_to((P, 2 * H, DH)), ALU.mult
                                            ).then_inc(sem["amp_n"], 1)
                for a in range(TB):
                    pool.wait_ge(*nth(b, "amp_n", a))
                    pool.wait_ge(*nth(b, "cos", a // 2))
                    nc.gpsimd.tensor_tensor(tt[:, a, :], tt[:, a, :], sp[:, a, :], ALU.mult).then_inc(sem["w_cos"], 1)
                    pool.wait_ge(*nth(b, "sin", a // 2))
                    nc.gpsimd.tensor_tensor(sn[:, a, :], sn[:, a, :], sp[:, a, :], ALU.mult).then_inc(sem["w_sin"], 1)

            def causal(b, q):
                def keep_lower(group, view, n):
                    pool.wait_ge(*nth(b, "exps", q * GROUPS1 + group))
                    hold(pool)
                    nc.gpsimd.affine_select(out=view, in_=view, compare_op=ALU.is_ge, fill=0.0, base=0,
                                            pattern=[[0, n], [1, P]], channel_multiplier=-1
                                            ).then_inc(sem["causal"], 1)
                for pair in range(2):
                    for bk, stride, n in ((0, 0, 1), (1, 384, 2), (2, 256, 2), (3, 0, 1), (4, 384, 2)):
                        g, off = divmod(5 * pair + bk, 2)
                        tile = ex[:, (q * GROUPS1 + g) % SLOTS, off * BANK:(off + 1) * BANK]
                        if n == 1:
                            keep_lower(g, tile[:, 0:P].unsqueeze(1), 1)
                        elif stride == 256:
                            keep_lower(g, tile.rearrange("p (n c) -> p n c", n=2)[:, :, 0:P], 2)
                        else:
                            keep_lower(g, tile.rearrange("p (n c) -> p n c", n=4)[:, 0:4:3, :], 2)

            def squares(b):
                if not b.it.exact:
                    pool.wait_ge(*nth(b, "o2_diff", 0))
                pool.wait_ge(*nth(b, "out_st", -1))
                nc.gpsimd.tensor_tensor(y[:], att2[:], att2[:], ALU.mult).then_inc(sem["o2_sq"], 1)

            def layer_norm_rstd(b, n):
                pool.wait_ge(*nth(b, f"aggr{n}", TB - 1))
                hold(pool)
                nc.gpsimd.tensor_scalar(rstd[:, n - 1, :], mv[:, n - 1, :, 1], LN_EPS, None, ALU.add
                                        ).then_inc(sem[f"ln{n}_var"], 1)
                pool.wait_ge(*nth(b, f"ln{n}_var"))
                nc.gpsimd.tensor_tensor(rstd[:, n - 1, :], rstd[:, n - 1, :], minus_half[:], ALU.pow
                                        ).then_inc(sem[f"ln{n}_rstd"], 1)

            def normalise(b, dst, n, event):
                for a in range(TB):
                    pool.wait_ge(*nth(b, f"ln{n}_rstd"))
                    hold(pool)
                    nc.gpsimd.tensor_scalar(dst[:, a, :], y[:, a, :], mv[:, n - 1, a, 0:1], rstd[:, n - 1, a:a + 1],
                                            ALU.subtract, ALU.mult).then_inc(sem[event], 1)

            def store(b):
                n = b.at(1)
                pool.wait_ge(*nth(b, "out", TB - 1))
                pool.dma_start(t["out"][n].rearrange("(a p) d -> p a d", p=P), y[:]).then_inc(sem["out_st"], 16)

            def square_amplitudes(b):
                for a in range(TB):
                    pool.wait_ge(*nth(b, "softplus", a))
                    nc.gpsimd.tensor_tensor(sn[:, a, :], sp[:, a, :], sp[:, a, :], ALU.mult).then_inc(sem["sq1"], 1)

            def body(it):
                if it.s:
                    square_amplitudes(it.b1)
                    rotate(it.b1)
                    causal(it.b1, 0)
                    causal(it.b1, 1)
                if it.x:
                    squares(it.b0)
                if it.s:
                    causal(it.b1, 2)
                    causal(it.b1, 3)
                if it.x:
                    layer_norm_rstd(it.b0, 2)
                    normalise(it.b0, x2, 2, "x2")
                    layer_norm_rstd(it.b0, 3)
                    normalise(it.b0, y, 3, "out")
                    store(it.b0)

            def again(it):
                b = it.b1
                square_amplitudes(b)
                rotate(b)
                pool.wait_ge(sem["c_out"], it.reg * (H * TB) + H * TB)
                squares(b)
                layer_norm_rstd(b, 2)
                normalise(b, x2, 2, "x2")
                layer_norm_rstd(b, 3)
                normalise(b, y, 3, "out")
                store(b)
                pool.wait_ge(*nth(b, "out_st"))
                hold(pool)

            run(pool, body)
            pool.wait_ge(sem["out_st"], 16 * B)

            def first_again():
                nc.gpsimd.memset(above, 0.0).then_inc(sem["above"], 1)
                pool.wait_ge(sem["above"], 1)
                for a in range(TB):
                    nc.gpsimd.affine_select(out=above[:, a, :], in_=above[:, a, :], compare_op=ALU.is_ge, fill=-1e30,
                                            base=a * P, pattern=[[-1, S]], channel_multiplier=1).then_inc(sem["above"], 1)
            if_needed(pool, again, first_again)

        @block.scalar
        def _(act):
            def table(functions):
                act.add_instruction(mybir.InstLoadActFuncSet(
                    name=nc.get_next_instruction_name(), engine=mybir.EngineType.Activation,
                    act_func_set_id=TABLES[functions]))

            act.wait_ge(const_in, 16 * N_CONST)
            act.wait_ge(pool_const, POOL_CONST)
            table("exp_ln")
            nc.scalar.activation(head_scale[:], head_scale[:], ACT.Exp).then_inc(act_const, 1)
            act.wait_ge(dve_const, 2)
            nc.scalar.activation(lam_sum[:], lam_sum[:], ACT.Exp).then_inc(act_const, 1)

            def rsqrt(b, out, in_, scale, eps, ready, ln_event, event):
                act.wait_ge(*nth(b, *ready))
                nc.scalar.activation(out, in_, ACT.Ln, bias=eps, scale=scale).then_inc(sem[ln_event], 1)
                act.wait_ge(*nth(b, ln_event))
                nc.scalar.activation(out, out, ACT.Exp, scale=-0.5).then_inc(sem[event], 1)

            def exps(b, groups, scale):
                for g in groups:
                    act.wait_ge(*nth(b, "scores", g))
                    if g >= SLOTS:
                        act.wait_ge(*nth(b, "pv", set_of(g - SLOTS)))
                    else:
                        act.wait_ge(*nth(b, "pv", set_of(G + g - SLOTS) - SETS))
                    nc.scalar.activation(ex[:, g % SLOTS, :], psS[g % 2][:, :], ACT.Exp, scale=scale
                                         ).then_inc(sem["exps"], 1)

            def self_exp(i, c, qb, r):
                act.wait_ge(*nth_in_round(i, "s_max"))
                nc.scalar.activation(z2[:, 0, :], z2[:, 0, :], ACT.Exp, bias=neg_max[:, 0:1],
                                     accum_out=row_sum[:, 0:1]).then_inc(sem["s_exp"], 1)

            def cross_exp(i, c, qb, r):
                for j in range(2):
                    act.wait_ge(*nth_in_round(i, "c_max", j))
                    nc.scalar.activation(z2[:, j, :], z2[:, j, :], ACT.Exp, bias=neg_max[:, j:j + 1],
                                         accum_out=row_sum[:, j:j + 1]).then_inc(sem["c_exp"], 1)

            def log_part(b, a):
                act.wait_ge(*filled(b, ("amp", a)))
                if a == 0:
                    act.wait_ge(*nth(b, "y3", -1 if b.it.exact else -1 - TB))
                nc.scalar.activation(tt[:, a, :], bank(b, ("amp", a))[:, :], ACT.Abs).then_inc(sem["abs_x"], 1)
                act.wait_ge(*nth(b, "abs_x", a))
                nc.scalar.activation(tt[:, a, :], tt[:, a, :], ACT.Exp, scale=-1.0).then_inc(sem["exp_x"], 1)
                act.wait_ge(*nth(b, "exp_x", a))
                nc.scalar.activation(tt[:, a, :], tt[:, a, :], ACT.Ln, bias=1.0).then_inc(sem["ln_x"], 1)

            def phases(b):
                table("sin_tanh")
                halves = [slice(0, 2), slice(2, TB)]
                for i, h in enumerate(halves):
                    act.wait_ge(*nth(b, "phi_sb", 2 * i + 1))
                    nc.scalar.activation(tt[:, h, :], tt[:, h, :], ACT.Tanh).then_inc(sem["tanh"], 1)
                for i, h in enumerate(halves):
                    act.wait_ge(*nth(b, "tanh", i))
                    act.wait_ge(*nth(b, "ss1", 2 * i + 1))
                    nc.scalar.activation(sn[:, h, :], tt[:, h, :], ACT.Sin, scale=PI_IN).then_inc(sem["sin"], 1)
                    act.wait_ge(*nth(b, "sin", i))
                    nc.scalar.activation(tt[:, h, :], tt[:, h, :], ACT.Abs).then_inc(sem["abs_t"], 1)
                    act.wait_ge(*nth(b, "abs_t", i))
                    nc.scalar.activation(tt[:, h, :], tt[:, h, :], ACT.Sin, scale=-float(np.pi), bias=float(np.pi / 2)
                                         ).then_inc(sem["cos"], 1)
                table("exp_ln")

            def amplitude_rs(b):
                rsqrt(b, flat(rs[:]), flat(ss[:]), 1.0 / DH, SELF_EPS, ("ss1", TB - 1), "rs_ln", "rs")

            def layer_norm1_rstd(b):
                rsqrt(b, rstd[:, 0, :], mv[:, 0, :, 1], 1.0, LN_EPS, ("aggr1", TB - 1), "ln1_var", "ln1_rstd")

            def rms(b):
                rsqrt(b, flat(ms2), flat(ms2), 1.0 / DH, RMS_EPS, ("o2_ms", 0), "rms_ln", "rms_r")

            def gelu_square(b):
                act.wait_ge(*nth(b, "h_sb", 1))
                nc.scalar.activation(g_t, h_t, ACT.Square).then_inc(sem["h_sq"], 1)

            def gelu_tanh(b):
                table("sin_tanh")
                act.wait_ge(*nth(b, "h_u", 0))
                nc.scalar.activation(u_t, u_t, ACT.Tanh, scale=GELU_C).then_inc(sem["h_tanh"], 1)
                table("exp_ln")

            def to_sbuf(b, name, event, dst):
                for c in range(DC):
                    act.wait_ge(*filled(b, (name, c)))
                    nc.scalar.activation(dst[:, c, :], bank(b, (name, c))[:, :], ACT.Copy).then_inc(sem[event], 1)

            def cross_values(b, a):
                act.wait_ge(*filled(b, ("v2", a)))
                nc.scalar.activation(vals2[:, a, :, 0:DH], bank(b, ("v2", a))[:, 0:D].rearrange(
                    "p (h d) -> p h d", d=DH), ACT.Copy).then_inc(sem["v2_sb"], 1)

            def stack_k1(b, a):
                act.wait_ge(*filled(b, ("kT1", 1, a)))
                nc.scalar.activation(k_st[:, 0, HALF:H, a * P:(a + 1) * P], bank16(b, ("kT1", 1, a)).rearrange(
                    "p (h c) -> p h c", h=HALF), ACT.Copy).then_inc(sem["k1_stacked"], 1)

            def stack_k2(b, half, a):
                act.wait_ge(*filled(b, ("kT2", half, a)))
                src = bank16(b, ("kT2", half, a)).rearrange("p (h c) -> p h c", h=HALF)
                for j in range(2):
                    nc.scalar.activation(k_st[:, j, half * HALF:(half + 1) * HALF, a * P:(a + 1) * P], src, ACT.Copy,
                                         scale=half_mask[:, j:j + 1]).then_inc(sem["k2_stacked"], 1)

            def stack_q2(b, a):
                act.wait_ge(*filled(b, ("qT2", 0, a)))
                src = bank16(b, ("qT2", 0, a)).rearrange("p (h c) -> p h c", h=HALF)
                nc.scalar.activation(q_st[:, 0:HALF, a * P:(a + 1) * P], src, ACT.Copy).then_inc(sem["q2_stacked"], 1)

            def body(it):
                x, s, b0, b1 = it.x, it.s, it.b0, it.b1
                cross_scale = DH ** -0.5
                for m in range(CUT, STEPS):
                    g = G1 + 4 * m
                    if x:
                        exps(b0, range(g, g + 2), cross_scale)
                    if s and AMP_STEP <= m < AMP_STEP + TB:
                        log_part(b1, m - AMP_STEP)
                    if x:
                        exps(b0, range(g + 2, g + 4), cross_scale)
                    if s and m == TRIG_STEP - 1:
                        amplitude_rs(b1)
                    if s and m == TRIG_STEP:
                        phases(b1)
                if s:
                    exps(b1, range(GROUPS1), 1.0)
                    stack_k1(b1, 0)
                    exps(b1, range(GROUPS1, 2 * GROUPS1), 1.0)
                    for a in range(1, TB):
                        stack_k1(b1, a)
                    exps(b1, range(2 * GROUPS1, 3 * GROUPS1), 1.0)
                if x:
                    rms(b0)
                if s:
                    exps(b1, range(3 * GROUPS1, G1), 1.0)
                if x:
                    to_sbuf(b0, "attT2", "attT2_sb", xT2)
                if s:
                    cross_values(b1, 0)
                    to_sbuf(b1, "attT1", "attT1_sb", att_T)
                    cross_values(b1, 1)
                    layer_norm1_rstd(b1)
                    to_sbuf(b1, "x1T", "x1T_sb", xT2)
                    stack_k2(b1, 0, 0)
                    stack_q2(b1, 0)
                    stack_q2(b1, 1)
                    stack_q2(b1, 2)
                    stack_k2(b1, 0, 1)
                    stack_q2(b1, 3)
                    stack_k2(b1, 0, 2)
                    stack_k2(b1, 0, 3)
                    cross_values(b1, 2)
                    cross_values(b1, 3)
                for m in range(CUT):
                    if s:
                        exps(b1, range(G1 + 4 * m, G1 + 4 * m + 4), cross_scale)
                        if m:
                            stack_k2(b1, 1, m - 1)
                    if x and m == 2:
                        gelu_square(b0)
                if s:
                    stack_k2(b1, 1, TB - 1)
                if x:
                    gelu_tanh(b0)

            def again(it):
                b = it.b1
                for a in range(TB):
                    log_part(b, a)
                phases(b)
                amplitude_rs(b)
                rounds(act, b, nothing, nothing, self_exp)
                to_sbuf(b, "attT1", "attT1_sb", att_T)
                layer_norm1_rstd(b)
                to_sbuf(b, "x1T", "x1T_sb", xT2)
                for a in range(TB):
                    cross_values(b, a)
                rounds(act, b, nothing, nothing, cross_exp)
                rms(b)
                to_sbuf(b, "attT2", "attT2_sb", xT2)
                gelu_square(b)
                gelu_tanh(b)

            run(act, body)
            if_needed(act, again)

        @block.vector
        def _(dve):
            v = nc.vector
            dve.wait_ge(const_in, 16 * N_CONST)
            v.tensor_tensor(lam_prod[:], lam_in[:, 0:4:2, :], lam_in[:, 1:4:2, :], ALU.mult).then_inc(dve_const, 1)
            dve.wait_ge(dve_const, 1)
            v.tensor_reduce(lam_sum[:], lam_prod[:].rearrange("p a (h d) -> p a h d", d=DH), AX.X, ALU.add
                            ).then_inc(dve_const, 1)
            v.tensor_scalar(w_o2[:], w_o2[:], rms_col[:], 1.0 - LAMBDA_INIT, ALU.mult, ALU.mult
                            ).then_inc(dve_const, 1)
            v.memset(bad[:], 0.0).then_inc(dve_const, 1)
            v.memset(ok_sum[:], 0.0).then_inc(dve_const, 1)
            v.memset(lam_w[:], 1.0).then_inc(dve_const, 1)
            v.memset(cge[:], 0.0).then_inc(dve_const, 1)
            for bank_o in psO:
                v.memset(bank_o[:, :], 0.0).then_inc(dve_const, 1)
            dve.wait_ge(act_const, 2)
            v.tensor_scalar(head_scale[:], head_scale[:], DH ** -0.5, None, ALU.mult).then_inc(dve_const, 1)
            v.tensor_tensor(lam_sum[:, 0, :], lam_sum[:, 1, :], lam_sum[:, 0, :], ALU.subtract).then_inc(dve_const, 1)
            dve.wait_ge(dve_const, DVE_CONST - 1)
            v.tensor_scalar(lam_w[:, :, 1], lam_sum[:, 0, :], LAMBDA_INIT, None, ALU.subtract).then_inc(dve_const, 1)
            dve.wait_ge(dve_const, DVE_CONST)
            dve.wait_ge(pool_const, POOL_CONST)

            def scan_mask(b, n):
                dve.wait_ge(*nth(b, f"mask_in{n % 2}", n // 2))
                if n == 0:
                    dve.wait_ge(*nth(b, "bad_max", -1))
                v.tensor_scalar(mask_t[:, n % 2, :], mask_t[:, n % 2, :], 0.0, 0.0, ALU.not_equal, ALU.max,
                                accum_out=mask_bad[:, n:n + 1]).then_inc(sem["mask_seen"], 1)

            def layer_norm_stats(b, src, ready, n, blocks=range(TB)):
                for a in blocks:
                    dve.wait_ge(*nth(b, *ready[a]))
                    v.bn_stats(st6[:, n - 1, a, :], src[:, a, :]).then_inc(sem[f"stats{n}"], 1)
                for a in blocks:
                    dve.wait_ge(*nth(b, f"stats{n}", a))
                    hold(dve)
                    v.bn_aggr(mv[:, n - 1, a, :], st6[:, n - 1, a, :]).then_inc(sem[f"aggr{n}"], 1)

            def normalise(b, a, dst, src, n, event):
                dve.wait_ge(*nth(b, f"ln{n}_rstd"))
                v.tensor_scalar(dst, src, mv[:, n - 1, a, 0:1], rstd[:, n - 1, a:a + 1], ALU.subtract, ALU.mult
                                ).then_inc(sem[event], 1)

            def heads(half):
                return slice(half * HALF, (half + 1) * HALF)

            def stack(b, use, event, k, dst, scale=None):
                dve.wait_ge(*filled(b, use))
                src = bank16(b, use).rearrange("p (h c) -> p h c", h=HALF)
                if scale is None:
                    v.tensor_copy(dst, src).then_inc(sem[event], 1)
                else:
                    v.tensor_scalar(dst, src, scale, None, ALU.mult).then_inc(sem[event], 1)

            def softplus(b, a):
                dve.wait_ge(*filled(b, ("amp", a)))
                dve.wait_ge(*nth(b, "ln_x", a))
                if a == 0:
                    dve.wait_ge(*nth(b, "y3", -1 if b.it.exact else -1 - TB))
                v.scalar_tensor_tensor(sp[:, a, :], bank(b, ("amp", a))[:, :], 0.0, tt[:, a, :], ALU.max, ALU.add
                                       ).then_inc(sem["softplus"], 1)

            def phase_arguments(b, a):
                dve.wait_ge(*filled(b, ("phi", a)))
                dve.wait_ge(*nth(b, "softplus", a))
                v.tensor_copy(tt[:, a, :], bank(b, ("phi", a))[:, :]).then_inc(sem["phi_sb"], 1)

            def self_attention_values(b, a):
                dve.wait_ge(*filled(b, ("v1", a)))
                v.tensor_copy(vals1[:, a, :, 0:DH], bank(b, ("v1", a))[:, 0:D].rearrange("p (h d) -> p h d", d=DH)
                              ).then_inc(sem["v1_sb"], 1)

            def sum_squares(b, a):
                dve.wait_ge(*nth(b, "sq1", a))
                v.tensor_reduce(ss[:, a, :], sn[:, a, :].rearrange("p (g d) -> p g d", d=DH), AX.X, ALU.add
                                ).then_inc(sem["ss1"], 1)

            def scale_rs(b):
                dve.wait_ge(*nth(b, "rs"))
                v.tensor_tensor(rs[:, :, 0:H], rs[:, :, 0:H], head_scale[:].unsqueeze(1).broadcast_to((P, TB, H)),
                                ALU.mult).then_inc(sem["rs_scaled"], 1)

            def split_self(b, half, a):
                n, s = half * TB + a, stag[:, a % 2]
                dve.wait_ge(*nth(b, "w_cos", a))
                dve.wait_ge(*nth(b, "w_sin", a))
                if half == 1 and a >= 2:
                    dve.wait_ge(*filled(b, ("kT1", 1, a - 2)))

                def parts(qk):
                    c = qk * D + half * (HALF * DH)
                    src = work[:, 1:3, a, c:c + HALF * DH].rearrange("p w (h d) -> p w h d", d=DH)
                    dst = s[:, qk * HALF:(qk + 1) * HALF].rearrange("p h t (w d) -> p t w h d", w=2)
                    return src, dst[:, 0], dst[:, 3]
                for qk in range(2):
                    src, hi, lo = parts(qk)
                    v.tensor_copy(hi, src).then_inc(sem["hi1"], 1)
                for qk in range(2):
                    src, hi, lo = parts(qk)
                    dve.wait_ge(*nth(b, "hi1", 2 * n + qk))
                    v.tensor_tensor(lo, src, hi, ALU.subtract).then_inc(sem["lo1"], 1)
                dve.wait_ge(*nth(b, "lo1", 2 * n))
                v.tensor_copy(s[:, 0:HALF, 1:3, :], s[:, 0:HALF, 0:4:3, :]).then_inc(sem["dup1"], 1)
                dve.wait_ge(*nth(b, "lo1", 2 * n + 1))
                v.tensor_copy(s[:, HALF:, 1, :], s[:, HALF:, 3, :]).then_inc(sem["dup1"], 1)
                v.tensor_copy(s[:, HALF:, 2, :], s[:, HALF:, 0, :]).then_inc(sem["dup1"], 1)

            def stack_self(b, half, a):
                cs = slice(a * P, (a + 1) * P)
                stack(b, ("qT1", half, a), "q1_stacked", half * TB + a, q_st[:, heads(half), cs])
                if half == 0:
                    stack(b, ("kT1", half, a), "k1_stacked", half * TB + a, k_st[:, 0, heads(half), cs])

            def split_k2(b, half, a):
                n, s = half * TB + a, stag[:, a % 2]
                dve.wait_ge(*filled(b, ("k2", half, a)))
                src = bank(b, ("k2", half, a))[:, 0:HALF * F].rearrange("p (h f) -> p h f", f=F)
                v.tensor_copy(s[:, HALF:, 0, :], src).then_inc(sem["k2_hi"], 1)
                dve.wait_ge(*nth(b, "k2_hi", n))
                v.tensor_tensor(s[:, HALF:, 3, :], src, s[:, HALF:, 0, :], ALU.subtract).then_inc(sem["k2_split"], 1)
                dve.wait_ge(*nth(b, "k2_split", n))
                v.tensor_copy(s[:, HALF:, 1, :], s[:, HALF:, 3, :]).then_inc(sem["k2_dup"], 1)
                v.tensor_copy(s[:, HALF:, 2, :], s[:, HALF:, 0, :]).then_inc(sem["k2_dup"], 1)

            def split_q2(b, half, a):
                n, s = half * TB + a, stag[:, a % 2]
                dve.wait_ge(*filled(b, ("q2", half, a)))
                src = bank(b, ("q2", half, a))[:, 0:HALF * F].rearrange("p (h f) -> p h f", f=F)
                v.tensor_copy(s[:, 0:HALF, 0, :], src).then_inc(sem["q2_hi"], 1)
                dve.wait_ge(*nth(b, "q2_hi", n))
                v.tensor_tensor(s[:, 0:HALF, 3, :], src, s[:, 0:HALF, 0, :], ALU.subtract).then_inc(sem["q2_split"], 1)
                dve.wait_ge(*nth(b, "q2_split", n))
                v.tensor_copy(s[:, 0:HALF, 1:3, :], s[:, 0:HALF, 0:4:3, :]).then_inc(sem["q2_dup"], 1)

            def stack_q2(b, half, a):
                stack(b, ("qT2", half, a), "q2_stacked", half * TB + a, q_st[:, heads(half), a * P:(a + 1) * P])

            def evacuate_oT(b, quad):
                dve.wait_ge(*nth(b, "pv", quad if quad < QUADS1 else QUADS1 + 2 * (quad - QUADS1) + 1))
                v.tensor_copy(oT[:, quad % 2, :], psO[quad % 2][:, :]).then_inc(sem["oT_sb"], 1)

            def self_output(b, q):
                dve.wait_ge(*filled(b, ("o1T", q)))
                o = bank(b, ("o1T", q)).rearrange("p (a r c) -> p a r c", a=TB, r=4)
                if q == 0:
                    dve.wait_ge(*nth(b, "ok_cnt", -2))
                v.tensor_copy(den1[:, q], o[:, :, :, DH]).then_inc(sem["den1"], 1)
                dve.wait_ge(*nth(b, "den1", q))
                v.reciprocal(rden1[:], den1[:, q]).then_inc(sem["rden1"], 1)
                dve.wait_ge(*nth(b, "rden1", q))
                v.tensor_tensor(att1[:, :, q * 4 * DH:(q + 1) * 4 * DH].rearrange("p a (r d) -> p a r d", d=DH),
                                o[:, :, :, 0:DH], rden1[:].unsqueeze(3).broadcast_to((P, TB, 4, DH)), ALU.mult
                                ).then_inc(sem["att1"], 1)

            def cross_output(b, q):
                dve.wait_ge(*filled(b, ("o2T", q)))
                v.tensor_copy(o2[:, :, 4 * q:4 * q + 4, :],
                              bank(b, ("o2T", q)).rearrange("p (a r c) -> p a r c", a=TB, r=4)[:, :, :, 0:DH + 1]
                              ).then_inc(sem["o2_sb"], 1)

            def check_den(b, n, dens, scratch):
                if n == 0:
                    dve.wait_ge(*nth(b, "ok_acc", -1))
                v.tensor_scalar(scratch, dens, DEN_LO, None, ALU.is_ge).then_inc(sem["ok_lo"], 1)
                dve.wait_ge(*nth(b, "ok_lo", n))
                v.scalar_tensor_tensor(scratch, dens, DEN_HI, scratch, ALU.is_le, ALU.mult,
                                       accum_out=ok_n[:, n:n + 1]).then_inc(sem["ok_cnt"], 1)
                dve.wait_ge(*nth(b, "ok_cnt", n))
                v.tensor_tensor(ok_sum[:], ok_sum[:], ok_n[:, n:n + 1], ALU.add).then_inc(sem["ok_acc"], 1)

            def differential(b):
                dens = o2[:, :, :, DH]
                dve.wait_ge(*nth(b, "o2_sb", QUADS2 - 1))
                v.reciprocal(rden2.rearrange("p a h j -> p a (h j)"), dens).then_inc(sem["rden2"], 1)
                dve.wait_ge(*nth(b, "rden2"))
                v.tensor_tensor(rden2, rden2, lam_w[:].unsqueeze(1).broadcast_to((P, TB, H, 2)), ALU.mult
                                ).then_inc(sem["rden2_lam"], 1)
                check_den(b, 1, dens, ok_t.rearrange("p (a h) -> p a h", a=TB))
                dve.wait_ge(*nth(b, "rden2_lam"))
                num = o2[:, :, :, 0:DH]
                v.tensor_tensor(num, num, rden2.rearrange("p a h j -> p a (h j)").unsqueeze(3)
                                .broadcast_to((P, TB, 2 * H, DH)), ALU.mult).then_inc(sem["o2_norm"], 1)
                dve.wait_ge(*nth(b, "o2_norm"))
                both = o2[:].rearrange("p a (h j) c -> p a h j c", j=2)
                v.tensor_tensor(att2[:].rearrange("p a (h d) -> p a h d", d=DH), both[:, :, :, 0, 0:DH],
                                both[:, :, :, 1, 0:DH], ALU.add).then_inc(sem["o2_diff"], 1)

            def mean_squares(b):
                dve.wait_ge(*nth(b, "o2_sq"))
                v.tensor_reduce(ms2, y[:].rearrange("p a (h d) -> p a h d", d=DH), AX.X, ALU.add
                                ).then_inc(sem["o2_ms"], 1)

            def rms_norm(b):
                a4 = att2[:].rearrange("p a (h d) -> p a h d", d=DH)
                dve.wait_ge(*nth(b, "rms_r"))
                v.tensor_tensor(a4, a4, ms2.unsqueeze(3).broadcast_to((P, TB, H, DH)), ALU.mult
                                ).then_inc(sem["att2"], 1)

            def collect_mask(b):
                dve.wait_ge(*nth(b, "mask_seen", 2 * H - 1))
                v.tensor_reduce(bad_b[:], mask_bad[:], AX.X, ALU.max).then_inc(sem["bad_max"], 1)
                dve.wait_ge(*nth(b, "bad_max"))
                v.tensor_tensor(bad[:], bad[:], bad_b[:], ALU.max).then_inc(sem["bad_acc"], 1)

            def to_sbuf(b, name, event, dst):
                for c in range(DC):
                    dve.wait_ge(*filled(b, (name, c)))
                    v.tensor_copy(dst[:, c, :], bank(b, (name, c))[:, :]).then_inc(sem[event], 1)

            def add_residual(b, name, event, dst, residual):
                for p in range(2):
                    dve.wait_ge(*filled(b, (name, p)))
                    v.tensor_tensor(flat(dst[:, 2 * p:2 * p + 2, :]), bank(b, (name, p))[:, :],
                                    flat(residual[:, 2 * p:2 * p + 2, :]), ALU.add).then_inc(sem[event], 1)

            def route_scores(b):
                for a in range(TB):
                    dve.wait_ge(*nth(b, "x2", a))
                    if a:
                        dve.wait_ge(*nth(b, "route", a - 1))
                    v.scalar_tensor_tensor(junk[:, 0:D], x2[:, a, :], 1.0, w_route[:], ALU.mult, ALU.mult,
                                           accum_out=route[:, a:a + 1]).then_inc(sem["route"], 1)

            srow = flat(att1[:])[:, 0:S]

            def row_of_scores(b):
                for p in range(2):
                    dve.wait_ge(*filled(b, ("srow", p)))
                    v.tensor_copy(srow[:, p * 2 * P:(p + 1) * 2 * P], bank(b, ("srow", p))[:, 0:2 * P]
                                  ).then_inc(sem["srow_sb"], 1)

            def hidden(b, p):
                dve.wait_ge(*filled(b, ("ffn", p)))
                v.tensor_copy(h_t[:, p, :], bank(b, ("ffn", p))[:, :]).then_inc(sem["h_sb"], 1)

            def gelu_argument(b):
                dve.wait_ge(*nth(b, "h_sq"))
                v.tensor_scalar(g_t, g_t, GELU_A, 1.0, ALU.mult, ALU.add).then_inc(sem["h_w"], 1)
                dve.wait_ge(*nth(b, "h_w"))
                v.tensor_tensor(u_t, g_t, h_t, ALU.mult).then_inc(sem["h_u"], 1)

            def rank_tokens(b, blocks):
                if 0 in blocks:
                    dve.wait_ge(*nth(b, "srow_sb", 1))
                    dve.wait_ge(*nth(b, "route", TB - 1))
                for a in blocks:
                    own, here = route[:, a:a + 1], a * P
                    if a:
                        dve.wait_ge(*nth(b, "gt", 2 * a - 2))
                        v.tensor_scalar(junk[:, 0:here], srow[:, 0:here], own, 0.0, ALU.is_ge, ALU.add,
                                        accum_out=cge[:, a:a + 1]).then_inc(sem["gt"], 1)
                    v.tensor_scalar(junk[:, here:S], srow[:, here:S], own, 0.0, ALU.is_gt, ALU.add,
                                    accum_out=cgt[:, a:a + 1]).then_inc(sem["gt"], 1)
                    if a:
                        dve.wait_ge(*nth(b, "eq", a - 1))
                    v.scalar_tensor_tensor(junk[:, S:S + P], srow[:, here:here + P], own, tie[:], ALU.is_equal, ALU.mult,
                                           accum_out=ceq[:, a:a + 1]).then_inc(sem["eq"], 1)

            def select(b):
                dve.wait_ge(*nth(b, "gt", 2 * TB - 2))
                v.tensor_tensor(cgt[:], cgt[:], cge[:], ALU.add).then_inc(sem["cnt_sum"], 1)
                dve.wait_ge(*nth(b, "cnt_sum"))
                dve.wait_ge(*nth(b, "eq", TB - 1))
                v.tensor_tensor(rank[:], cgt[:], ceq[:], ALU.add).then_inc(sem["rank"], 1)
                dve.wait_ge(*nth(b, "rank"))
                v.tensor_scalar(sel[:], rank[:], float(K_SEL), None, ALU.is_lt).then_inc(sem["sel"], 1)
                dve.wait_ge(*nth(b, "sel"))
                v.tensor_scalar(keep[:], sel[:], -1.0, 2.0, ALU.mult, ALU.add).then_inc(sem["keep"], 1)
                v.tensor_scalar(hsel[:], sel[:], 0.5, None, ALU.mult).then_inc(sem["half_sel"], 1)

            def output(b):
                dve.wait_ge(*nth(b, "h_tanh"))
                v.scalar_tensor_tensor(g_t, u_t, 1.0, h_t, ALU.add, ALU.mult).then_inc(sem["h_g"], 1)
                dve.wait_ge(*nth(b, "h_g"))
                dve.wait_ge(*nth(b, "half_sel"))
                dve.wait_ge(*nth(b, "keep"))
                g4 = g_t.rearrange("p c (e d) -> p (c e) d", d=D)
                for a in range(TB):
                    v.tensor_scalar(g4[:, a, :], g4[:, a, :], hsel[:, a:a + 1], None, ALU.mult).then_inc(sem["h_gs"], 1)
                    dve.wait_ge(*nth(b, "h_gs", a))
                    v.scalar_tensor_tensor(y[:, a, :], x2[:, a, :], keep[:, a:a + 1], g4[:, a, :], ALU.mult, ALU.add
                                           ).then_inc(sem["y3"], 1)
                layer_norm_stats(b, y, [("y3", a) for a in range(TB)], 3)

            def body(it):
                x, s, b0, b1 = it.x, it.s, it.b0, it.b1
                for m in range(CUT, STEPS):
                    if s and m > JOB_STEP:
                        stack_self(b1, 0, m - JOB_STEP - 1)
                    if x and m % 2:
                        cross_output(b0, (m - 3) // 2)
                    if x:
                        scan_mask(b0, 2 * (m - CUT))
                    if s and AMP_STEP <= m < AMP_STEP + TB:
                        softplus(b1, m - AMP_STEP)
                    if s and AMP_STEP < m <= AMP_STEP + TB:
                        sum_squares(b1, m - AMP_STEP - 1)
                    if s and m == TRIG_STEP:
                        scale_rs(b1)
                    if s and m == TRIG_STEP + 1:
                        for a in range(TB):
                            self_attention_values(b1, a)
                    if s and m == JOB_STEP:
                        split_self(b1, 0, 1)
                    if s and m > JOB_STEP:
                        a = m - JOB_STEP + 1
                        split_self(b1, a // TB, a % TB)
                    if x and m % 2 == 0:
                        evacuate_oT(b0, QUADS1 + m // 2 - 1)
                    if s and PHI_STEP <= m < PHI_STEP + TB:
                        phase_arguments(b1, m - PHI_STEP)
                    if x:
                        scan_mask(b0, 2 * (m - CUT) + 1)
                    if s and m == JOB_STEP - 1:
                        split_self(b1, 0, 0)
                if s:
                    stack_self(b1, 0, TB - 1)
                if x:
                    evacuate_oT(b0, QUADS1 + QUADS2 - 1)
                    scan_mask(b0, MASK_LATE)
                    cross_output(b0, QUADS2 - 1)
                if s:
                    split_self(b1, 1, 1)
                    stack_self(b1, 1, 0)
                    split_self(b1, 1, 2)
                    evacuate_oT(b1, 0)
                    self_output(b1, 0)
                    stack_self(b1, 1, 1)
                    split_self(b1, 1, 3)
                    stack_self(b1, 1, 2)
                    stack_self(b1, 1, 3)
                if x:
                    differential(b0)
                    scan_mask(b0, MASK_LATE + 1)
                if s:
                    evacuate_oT(b1, 1)
                    self_output(b1, 1)
                if x:
                    mean_squares(b0)
                    scan_mask(b0, MASK_LATE + 2)
                    scan_mask(b0, MASK_LATE + 3)
                if s:
                    evacuate_oT(b1, 2)
                    self_output(b1, 2)
                if x:
                    rms_norm(b0)
                    scan_mask(b0, MASK_LATE + 4)
                if s:
                    evacuate_oT(b1, 3)
                    self_output(b1, 3)
                    check_den(b1, 0, den1[:].rearrange("p q a r -> p (q a r)"), junk[:, 0:TB * H])
                if x:
                    scan_mask(b0, MASK_LATE + 5)
                if s:
                    dve.wait_ge(*nth(b1, "x_in"))
                    add_residual(b1, "wo1", "y1", x_tok, x_tok)
                    layer_norm_stats(b1, x_tok, [("y1", a // 2) for a in range(TB)], 1)
                if x:
                    add_residual(b0, "wo2", "y2", y, x1)
                    dve.wait_ge(*nth(b0, "y2", 1))
                if s:
                    for a in range(TB):
                        normalise(b1, a, x1[:, a, :], x_tok[:, a, :], 1, "x1")
                    split_k2(b1, 0, 0)
                if x:
                    layer_norm_stats(b0, y, [("y2", a // 2) for a in range(TB)], 2)
                if s:
                    split_q2(b1, 0, 0)
                    split_q2(b1, 0, 1)
                    split_q2(b1, 0, 2)
                    split_k2(b1, 0, 1)
                    split_q2(b1, 0, 3)
                    split_k2(b1, 0, 2)
                    split_k2(b1, 0, 3)
                if x:
                    scan_mask(b0, MASK_LATE + 6)
                    scan_mask(b0, MASK_LATE + 7)
                    collect_mask(b0)
                    route_scores(b0)
                for m in range(CUT):
                    if s:
                        if m == 3:
                            cross_output(b1, 0)
                        if m:
                            stack_q2(b1, 1, m - 1)
                        split_k2(b1, 1, m)
                    if x and m == 3:
                        gelu_argument(b0)
                    if s:
                        split_q2(b1, 1, m)
                    if x and m == 0:
                        to_sbuf(b0, "x2T", "x2T_sb", att_T)
                    if x and m == 1:
                        row_of_scores(b0)
                        hidden(b0, 0)
                    if s and m == 2:
                        evacuate_oT(b1, QUADS1)
                    if x and m == 1:
                        rank_tokens(b0, range(0, 1))
                    if x and m == 2:
                        hidden(b0, 1)
                        rank_tokens(b0, range(1, 2))
                    if x and m == 3:
                        rank_tokens(b0, range(2, TB))
                if s:
                    stack_q2(b1, 1, TB - 1)
                if x:
                    select(b0)
                    output(b0)

            run(dve, body)

            dve.wait_ge(sem["ok_acc"], HEAD + B * PER["ok_acc"])
            dve.wait_ge(sem["bad_acc"], B)
            v.tensor_scalar(ok_sum[:], ok_sum[:], float(B * TB * 3 * H), None, ALU.not_equal).then_inc(sem["flag_sum"], 1)
            v.memset(ones1[:], 1.0).then_inc(sem["flag_sum"], 1)
            dve.wait_ge(sem["flag_sum"], 2)
            v.tensor_tensor(bad[:], bad[:], ok_sum[:], ALU.add).then_inc(sem["flag_sum"], 1)
            dve.wait_ge(sem["flag_pe"], 1)
            v.tensor_scalar(flag_f[0:1, :], psO[0][0:1, 0:1], FLAGS_FROM, None, ALU.is_gt).then_inc(sem["flag_sum"], 1)
            dve.wait_ge(sem["flag_sum"], 4)
            v.tensor_copy(flag_i[0:1, :], flag_f[0:1, :]).then_inc(sem["flag"], 1)

            def stack32(b, use, event, k0, parts):
                dve.wait_ge(*filled(b, use))
                a = use[2]
                src = bank(b, use).rearrange("p (c s) -> p c s", c=NC4)
                for j, part in enumerate(parts):
                    dst = part[:, 0:JK].rearrange("p (c s) -> p c s", c=NC4)[:, :, a * P:(a + 1) * P]
                    if len(parts) == 1:
                        v.tensor_copy(dst, src).then_inc(sem[event], 1)
                    else:
                        v.tensor_scalar(dst, src, half_mask[:, j:j + 1], None, ALU.mult).then_inc(sem[event], 1)

            def self_chunk(bc, c):
                dve.wait_ge(*nth_in_round(bc * (4 * TB), "s_scores", -1))
                v.tensor_copy(k_cur[:, 0, :], k32[:, bass.ds(c * S, S)]).then_inc(sem["s_k"], 1)

            def cross_chunk(bc, c):
                dve.wait_ge(*nth_in_round(bc * (4 * TB), "c_scores", -1))
                v.tensor_copy(k_cur[:, 0, :], k32[:, bass.ds(c * S, S)]).then_inc(sem["c_k"], 1)
                v.tensor_copy(k_cur[:, 1, :], k32[:, bass.ds(c * S + JK, S)]).then_inc(sem["c_k"], 1)

            def self_block(bq, c, qb):
                dve.wait_ge(*nth_in_round(bq * 4, "s_scores", -1))
                v.tensor_copy(q_cur, q32[:, bass.ds(c * S + qb * P, P)]).then_inc(sem["s_q"], 1)

            def cross_block(bq, c, qb):
                dve.wait_ge(*nth_in_round(bq * 4, "c_scores", -1))
                v.tensor_copy(q_cur, q32[:, bass.ds(c * S + qb * P, P)]).then_inc(sem["c_q"], 1)

            def round_out(i, c, qb, r, s, att):
                dve.wait_ge(*nth_in_round(i, s + "_T"))
                v.tensor_copy(probs_T, psS[0][:, BANK:2 * BANK]).then_inc(sem[s + "_aT"], 1)
                dve.wait_ge(*nth_in_round(i, s + "_pv"))
                v.tensor_copy(flat(att[:])[:, bass.ds(qb * D + c * (4 * DH) + r * DH, DH)], psO[0][:, 0:DH]
                              ).then_inc(sem[s + "_out"], 1)

            def self_round(i, c, qb, r):
                dve.wait_ge(*nth_in_round(i, "s_scores"))
                v.tensor_tensor(z2[:, 0, :], psS[0][:, 0:S], flat(above)[:, bass.ds(qb * S, S)], ALU.add
                                ).then_inc(sem["s_z"], 1)
                dve.wait_ge(*nth_in_round(i, "s_z"))
                v.tensor_reduce(neg_max[:, 0:1], z2[:, 0, :], AX.X, ALU.max, negate=True).then_inc(sem["s_max"], 1)
                dve.wait_ge(*nth_in_round(i, "s_exp"))
                v.reciprocal(row_scale[:, 0:1], row_sum[:, 0:1]).then_inc(sem["s_rden"], 1)
                dve.wait_ge(*nth_in_round(i, "s_rden"))
                v.tensor_scalar(probs, z2[:, 0, :], row_scale[:, 0:1], None, ALU.mult).then_inc(sem["s_a"], 1)
                round_out(i, c, qb, r, "s", att1)

            def cross_round(i, c, qb, r):
                dve.wait_ge(*nth_in_round(i, "c_scores"))
                dve.wait_ge(*nth_in_round(i, "c_mask"))
                for j in range(2):
                    v.scalar_tensor_tensor(z2[:, j, :], psS[j][:, 0:S], DH ** -0.5, mask_t[:, 0, 0:S],
                                           ALU.mult, ALU.add).then_inc(sem["c_z"], 1)
                for j in range(2):
                    dve.wait_ge(*nth_in_round(i, "c_z", j))
                    v.tensor_reduce(neg_max[:, j:j + 1], z2[:, j, :], AX.X, ALU.max, negate=True
                                    ).then_inc(sem["c_max"], 1)
                dve.wait_ge(*nth_in_round(i, "c_exp", 1))
                v.reciprocal(row_scale[:], row_sum[:]).then_inc(sem["c_rden"], 1)
                dve.wait_ge(*nth_in_round(i, "c_rden"))
                v.tensor_tensor(row_scale[:], row_scale[:], flat(lam_w[:])[:, bass.ds(c * 8 + 2 * r, 2)], ALU.mult
                                ).then_inc(sem["c_rlam"], 1)
                dve.wait_ge(*nth_in_round(i, "c_rlam"))
                v.tensor_scalar(z2[:, 0, :], z2[:, 0, :], row_scale[:, 0:1], None, ALU.mult).then_inc(sem["c_a0"], 1)
                dve.wait_ge(*nth_in_round(i, "c_a0"))
                v.scalar_tensor_tensor(probs, z2[:, 1, :], row_scale[:, 1:2], z2[:, 0, :], ALU.mult, ALU.add
                                       ).then_inc(sem["c_a"], 1)
                round_out(i, c, qb, r, "c", att2)

            def again(it):
                b = it.b1
                for a in range(TB):
                    softplus(b, a)
                    self_attention_values(b, a)
                for a in range(TB):
                    phase_arguments(b, a)
                    sum_squares(b, a)
                scale_rs(b)
                for a in range(TB):
                    dve.wait_ge(*nth(b, "w_sin", a))
                    for w, event, cols in ((tt, "wk_cos", slice(0, DH)), (sn, "wk_sin", slice(DH, F))):
                        v.tensor_copy(wk[:, :, cols], w[:, a, :].rearrange("p (g d) -> p g d", d=DH)
                                      ).then_inc(sem[event], 1)
                    stack32(b, ("qT1", 0, a), "q1_stacked", a, [q32])
                    stack32(b, ("kT1", 0, a), "k1_stacked", a, [k32[:, 0:JK]])
                dve.wait_ge(*nth(b, "k1_stacked", TB - 1))
                rounds(dve, b, self_chunk, self_block, self_round)
                dve.wait_ge(*nth(b, "x_in"))
                add_residual(b, "wo1", "y1", x_tok, x_tok)
                layer_norm_stats(b, x_tok, [("y1", a // 2) for a in range(TB)], 1)
                for a in range(TB):
                    normalise(b, a, x1[:, a, :], x_tok[:, a, :], 1, "x1")
                for a in range(TB):
                    for use, part, event in ((("k2", 0, a), slice(H, 2 * H), "k2_split"),
                                             (("q2", 0, a), slice(0, H), "q2_split")):
                        dve.wait_ge(*filled(b, use))
                        v.tensor_copy(wk[:, part, :], bank(b, use).rearrange("p (h f) -> p h f", f=F)
                                      ).then_inc(sem[event], 1)
                    stack32(b, ("qT2", 0, a), "q2_stacked", a, [q32])
                    stack32(b, ("kT2", 0, a), "k2_stacked", 2 * a, [k32[:, j * JK:(j + 1) * JK] for j in range(2)])
                dve.wait_ge(*nth(b, "k2_stacked", 2 * TB - 1))
                rounds(dve, b, cross_chunk, cross_block, cross_round)
                mean_squares(b)
                rms_norm(b)
                add_residual(b, "wo2", "y2", y, x1)
                layer_norm_stats(b, y, [("y2", a // 2) for a in range(TB)], 2)
                route_scores(b)
                to_sbuf(b, "x2T", "x2T_sb", att_T)
                row_of_scores(b)
                hidden(b, 0)
                hidden(b, 1)
                gelu_argument(b)
                rank_tokens(b, range(TB))
                select(b)
                output(b)

            if_needed(dve, again, lambda: dve.wait_ge(sem["above"], 1 + TB))

        @block.tensor
        def _(pe):
            mm = nc.tensor.matmul

            def claim(b, use, waited=None):
                it = b.it
                last = it.order.claims[use]
                if last is None:
                    return
                event, k, side, crossing = last
                if crossing == "b0":
                    pe.wait_ge(*nth(it.b0, event, k))
                elif crossing == "before":
                    pe.wait_ge(*nth(b, event, k - it.per[event]))
                elif event != waited:
                    pe.wait_ge(*nth(it.b1 if side == "S" else it.b0, event, k))

            def project(b, use, lhsT, w, width, col=0, last=True, w0=0):
                out = bank(b, use)[:, col:col + width]
                for c in range(DC):
                    i = mm(out, lhsT[:, c, :], w[:, c, w0:w0 + width], start=(c == 0), stop=(c == DC - 1))
                if last:
                    i.then_inc(sem["misc_full"], 1)

            def project_block(b, use, srcT, a, w, width, w0=0, waited=None):
                claim(b, use, waited)
                project(b, use, srcT[:, :, a * P:(a + 1) * P], w, width, w0=w0)

            def transpose_blocks(b, use, srcs, identity, dt=None):
                out = bank16(b, use) if dt is f16 else bank(b, use)
                for n, src in enumerate(srcs):
                    i = nc.tensor.transpose(out[:, n * P:(n + 1) * P], src, identity)
                i.then_inc(sem["misc_full"], 1)

            def token_to_feature(b, name, src, waited=None):
                for c in range(DC):
                    claim(b, (name, c), waited)
                    transpose_blocks(b, (name, c), [src[:, a, c * P:(c + 1) * P] for a in range(TB)], ident[:])

            def out_project(b, name, srcT, w, waited):
                pe.wait_ge(*nth(b, waited, DC - 1))
                for p in range(2):
                    claim(b, (name, p), waited)
                    for e in range(2):
                        a = 2 * p + e
                        project(b, (name, p), srcT[:, :, a * P:(a + 1) * P], w, D, e * D, last=(e == 1))

            def feed_forward(b, a):
                if a == 0:
                    pe.wait_ge(*nth(b, "x2T_sb", DC - 1))
                if a % 2 == 0:
                    claim(b, ("ffn", a // 2), "x2T_sb")
                project(b, ("ffn", a // 2), att_T[:, :, a * P:(a + 1) * P], w_ffn, D, a % 2 * D, last=(a % 2 == 1))

            def amplitudes(b, a):
                if a == 0:
                    pe.wait_ge(*nth(b, "xT_in"))
                project_block(b, ("amp", a), xT, a, w_amp, 2 * D)

            def self_attention_values(b, a):
                project_block(b, ("v1", a), xT, a, w_v1, D)

            def phases(b, a):
                project_block(b, ("phi", a), xT, a, w_phi, 2 * D)

            def staged(b, name, half, a, kind):
                claim(b, (name, half, a))
                transpose_blocks(b, (name, half, a),
                                 [stag[:, a % 2, kind * HALF + h].rearrange("p t f -> p (t f)") for h in range(HALF)],
                                 ident16[:], f16)

            def self_job(b, half, a, kinds=(0, 1)):
                if 0 in kinds:
                    pe.wait_ge(*nth(b, "dup1", 3 * (half * TB + a)))
                    staged(b, "qT1", half, a, 0)
                if 1 in kinds:
                    pe.wait_ge(*nth(b, "dup1", 3 * (half * TB + a) + 2))
                    staged(b, "kT1", half, a, 1)

            def q2_job(b, half, a):
                pe.wait_ge(*nth(b, "q2_dup", half * TB + a))
                staged(b, "qT2", half, a, 0)

            def k2_job(b, half, a):
                pe.wait_ge(*nth(b, "k2_dup", 2 * (half * TB + a) + 1))
                staged(b, "kT2", half, a, 1)

            def project_k2(b, half, a):
                project_block(b, ("k2", half, a), ctxT, a, w_k2, D, w0=half * D)

            def project_q2(b, half, a, waited=None):
                project_block(b, ("q2", half, a), xT2, a, w_q2, D, half * D, waited)

            def cross_attention_values(b, a):
                project_block(b, ("v2", a), ctxT, a, w_v2, D)

            def scores_ready(b, g):
                pe.wait_ge(*nth(b, "exps", g - 2))

            def untranspose(b, use, quad):
                pe.wait_ge(*nth(b, "oT_sb", quad))
                claim(b, use)
                transpose_blocks(b, use, [oT[:, quad % 2, a * P:(a + 1) * P] for a in range(TB)], ident[:])

            def self_scores(b, q, groups):
                blocks = [[] for _ in range(2 * GROUPS1)]
                for r in range(4):
                    for kb in range(TB):
                        bk, off, w = self_place(r, kb)
                        blocks[bk].append((r, kb, off, w))
                for g in groups:
                    n = q * GROUPS1 + g
                    if g == 0 and q % 2 == 0:
                        half = q // 2
                        pe.wait_ge(*nth(b, "q1_stacked", half * TB + TB - 1))
                        pe.wait_ge(*nth(b, "k1_stacked", half * TB + TB - 1))
                    scores_ready(b, n)
                    for half in range(2):
                        for r, kb, off, w in blocks[2 * g + half]:
                            h = 4 * q + r
                            i = mm(psS[n % 2][:, half * BANK + off:half * BANK + off + w],
                                   k_st[:, 0, h, kb * P:(kb + 1) * P], q_st[:, h, kb * P:S], start=True, stop=True,
                                   skip_group_check=True)
                    i.then_inc(sem["scores"], 1)

            def self_values(b, q):
                pe.wait_ge(*nth(b, "causal", 10 * (q + 1) - 1))
                pe.wait_ge(*nth(b, "oT_sb", q - 2))
                if q == 0:
                    pe.wait_ge(*nth(b, "v1_sb", TB - 1))
                for kb in range(TB):
                    for r in range(4):
                        bk, off, w = self_place(r, kb)
                        g, half = divmod(bk, 2)
                        c = half * BANK + off
                        i = mm(psO[q % 2][32 * r:32 * r + VW, kb * P:S], vals1[:, kb, 4 * q + r, :],
                               ex[:, (q * GROUPS1 + g) % SLOTS, c:c + w], start=(kb == 0), stop=(kb == TB - 1),
                               skip_group_check=True)
                i.then_inc(sem["pv"], 1)

            def cross_group(b, n):
                q, rest = divmod(n - G1, GROUPS2)
                pair, stream = divmod(rest, 4)
                h, j = 2 * q + stream // 2, stream % 2
                if q % (QUADS2 // 2) == 0 and stream == 0:
                    half = q // (QUADS2 // 2)
                    if pair == 0:
                        pe.wait_ge(*nth(b, "q2_stacked", half * TB + TB - 1))
                    pe.wait_ge(*nth(b, "k2_stacked", 2 * (half * TB + 2 * pair + 2) - 1))
                scores_ready(b, n)
                for half in range(2):
                    kb = 2 * pair + half
                    i = mm(psS[n % 2][:, half * BANK:(half + 1) * BANK], k_st[:, j, h, kb * P:(kb + 1) * P],
                           q_st[:, h, :], start=True, stop=True)
                i.then_inc(sem["scores"], 1)

            def cross_values(b, m, half):
                q, pair = divmod(m, 2)
                g0 = G1 + 4 * m
                if half == 0:
                    pe.wait_ge(*nth(b, "exps", g0 + 3))
                    if pair == 0:
                        pe.wait_ge(*nth(b, "oT_sb", QUADS1 + q - 2))
                    if m == 0:
                        pe.wait_ge(*nth(b, "v2_sb", TB - 1))
                kb = 2 * pair + half
                for stream in range(4):
                    i = mm(psO[q % 2][32 * stream:32 * stream + VW, :], vals2[:, kb, 2 * q + stream // 2, :],
                           ex[:, (g0 + stream) % SLOTS, half * BANK:(half + 1) * BANK],
                           start=(kb == 0), stop=(kb == TB - 1), skip_group_check=True)
                if half == 1:
                    i.then_inc(sem["pv"], 1)

            def cross_step(b, m, between=nothing, after=nothing):
                g = G1 + 4 * m
                if b is not None:
                    cross_group(b, g)
                between()
                if b is not None:
                    cross_group(b, g + 1)
                    if m:
                        cross_values(b, m - 1, 0)
                    cross_group(b, g + 2)
                    if m:
                        cross_values(b, m - 1, 1)
                    cross_group(b, g + 3)
                after()

            def score_row(b):
                for p in range(2):
                    claim(b, ("srow", p))
                    if p == 0:
                        pe.wait_ge(*nth(b, "route", TB - 1))
                    transpose_blocks(b, ("srow", p), [route[:, a:a + 1].broadcast_to((P, P))
                                                      for a in range(2 * p, 2 * p + 2)], ident[:])

            pe.wait_ge(const_in, 16 * N_CONST)
            pe.wait_ge(pool_const, POOL_CONST)
            pe.wait_ge(dve_const, DVE_CONST)

            def body(it):
                x, s, b0, b1 = it.x, it.s, it.b0, it.b1
                for m in range(CUT, STEPS):
                    def between():
                        if x and m % 2:
                            q = (m - 3) // 2
                            untranspose(b0, ("o2T", q), QUADS1 + q)
                        if s and AMP_STEP <= m < AMP_STEP + TB:
                            amplitudes(b1, m - AMP_STEP)
                        if s and m == TRIG_STEP + 1:
                            for a in range(TB):
                                self_attention_values(b1, a)
                        if s and m >= JOB_STEP:
                            self_job(b1, 0, m - JOB_STEP, (0,))

                    def after():
                        if s and PHI_STEP <= m < PHI_STEP + TB:
                            phases(b1, m - PHI_STEP)
                        if s and m >= JOB_STEP:
                            self_job(b1, 0, m - JOB_STEP, (1,))
                    cross_step(b0 if x else None, m, between, after)
                if s:
                    self_scores(b1, 0, range(2))
                if x:
                    cross_values(b0, STEPS - 1, 0)
                    cross_values(b0, STEPS - 1, 1)
                if s:
                    self_scores(b1, 0, range(2, GROUPS1))
                if x:
                    untranspose(b0, ("o2T", QUADS2 - 1), QUADS1 + QUADS2 - 1)
                if s:
                    self_job(b1, 1, 0)
                    self_scores(b1, 1, range(2))
                    self_values(b1, 0)
                    self_scores(b1, 1, range(2, 4))
                    untranspose(b1, ("o1T", 0), 0)
                    self_scores(b1, 1, range(4, GROUPS1))
                    for a in range(1, TB):
                        self_job(b1, 1, a)
                    self_scores(b1, 2, range(2))
                    self_values(b1, 1)
                    self_scores(b1, 2, range(2, 4))
                    untranspose(b1, ("o1T", 1), 1)
                    self_scores(b1, 2, range(4, GROUPS1))
                    self_scores(b1, 3, range(2))
                    self_values(b1, 2)
                    self_scores(b1, 3, range(2, 4))
                    untranspose(b1, ("o1T", 2), 2)
                    self_scores(b1, 3, range(4, GROUPS1))
                if x:
                    pe.wait_ge(*nth(b0, "att2"))
                    token_to_feature(b0, "attT2", att2)
                if s:
                    self_values(b1, 3)
                    untranspose(b1, ("o1T", 3), 3)
                    pe.wait_ge(*nth(b1, "ctx_in"))
                    cross_attention_values(b1, 0)
                    pe.wait_ge(*nth(b1, "att1", QUADS1 - 1))
                    token_to_feature(b1, "attT1", att1, "att1")
                    cross_attention_values(b1, 1)
                    out_project(b1, "wo1", att_T, w_o1, "attT1_sb")
                if x:
                    out_project(b0, "wo2", xT2, w_o2, "attT2_sb")
                if s:
                    project_k2(b1, 0, 0)
                    pe.wait_ge(*nth(b1, "x1", TB - 1))
                    token_to_feature(b1, "x1T", x1)
                    k2_job(b1, 0, 0)
                    pe.wait_ge(*nth(b1, "x1T_sb", DC - 1))
                    project_q2(b1, 0, 0, "x1T_sb")
                    project_q2(b1, 0, 1, "x1T_sb")
                    q2_job(b1, 0, 0)
                    q2_job(b1, 0, 1)
                    project_q2(b1, 0, 2)
                    project_k2(b1, 0, 1)
                    project_q2(b1, 0, 3)
                    q2_job(b1, 0, 2)
                    project_k2(b1, 0, 2)
                    k2_job(b1, 0, 1)
                    q2_job(b1, 0, 3)
                    project_k2(b1, 0, 3)
                    k2_job(b1, 0, 2)
                    k2_job(b1, 0, 3)
                    cross_attention_values(b1, 2)
                    cross_attention_values(b1, 3)
                for m in range(CUT):
                    def between():
                        if x and m in (2, 3):
                            feed_forward(b0, 2 * (m - 2) + 1)
                        if s:
                            if m == 3:
                                untranspose(b1, ("o2T", 0), QUADS1)
                            if m:
                                q2_job(b1, 1, m - 1)
                            project_k2(b1, 1, m)

                    def after():
                        if s:
                            if m:
                                k2_job(b1, 1, m - 1)
                            project_q2(b1, 1, m)
                        if x and m == 0:
                            pe.wait_ge(*nth(b0, "x2", TB - 1))
                            token_to_feature(b0, "x2T", x2)
                        if x and m == 1:
                            score_row(b0)
                        if x and m in (1, 2):
                            feed_forward(b0, 2 * (m - 1))
                    cross_step(b1 if s else None, m, between, after)
                if s:
                    q2_job(b1, 1, TB - 1)
                    k2_job(b1, 1, TB - 1)

            run(pe, body)
            pe.wait_ge(sem["flag_sum"], 3)
            mm(psO[0][0:1, 0:1], bad[:], ones1[:], start=True, stop=True).then_inc(sem["flag_pe"], 1)

            def transpose32(b, a, n):
                for name, h0 in (("qT" + n, 0), ("kT" + n, H)):
                    claim(b, (name, 0, a))
                    transpose_blocks(b, (name, 0, a), [flat(wk[:, h0 + 4 * c:h0 + 4 * c + 4, :]) for c in range(NC4)],
                                     ident[:])

            def exact_values(i, c, r, s, vals):
                pe.wait_ge(*nth_in_round(i, s + "_a"))
                for kb in range(TB):
                    ins = nc.tensor.transpose(psS[0][:, BANK + kb * P:BANK + (kb + 1) * P], probs[:, kb * P:(kb + 1) * P],
                                              ident[:])
                ins.then_inc(sem[s + "_T"], 1)
                pe.wait_ge(*nth_in_round(i, s + "_aT"))
                for kb in range(TB):
                    ins = mm(psO[0][:, 0:DH], probs_T[:, kb * P:(kb + 1) * P],
                             vals[:].rearrange("p a h w -> p (a h w)")[:, bass.ds(c * (4 * VW) + (kb * H + r) * VW, DH)],
                             start=(kb == 0), stop=(kb == TB - 1))
                ins.then_inc(sem[s + "_pv"], 1)

            def self_round(i, c, qb, r):
                rows = slice(32 * r, 32 * r + 32)
                pe.wait_ge(*nth_in_round(i, "s_out", -1))
                mm(psS[0][:, 0:S], q_cur[rows, :], k_cur[rows, 0, :], start=True, stop=True
                   ).then_inc(sem["s_scores"], 1)
                exact_values(i, c, r, "s", vals1)

            def cross_round(i, c, qb, r):
                rows = slice(32 * r, 32 * r + 32)
                pe.wait_ge(*nth_in_round(i, "c_out", -1))
                for j in range(2):
                    ins = mm(psS[j][:, 0:S], q_cur[rows, :], k_cur[rows, j, :], start=True, stop=True)
                ins.then_inc(sem["c_scores"], 1)
                exact_values(i, c, r, "c", vals2)

            def again(it):
                b = it.b1
                for a in range(TB):
                    amplitudes(b, a)
                    self_attention_values(b, a)
                for a in range(TB):
                    phases(b, a)
                for a in range(TB):
                    pe.wait_ge(*nth(b, "wk_cos", a))
                    pe.wait_ge(*nth(b, "wk_sin", a))
                    transpose32(b, a, "1")
                pe.wait_ge(*nth(b, "k1_stacked", TB - 1))
                pe.wait_ge(*nth(b, "v1_sb", TB - 1))
                rounds(pe, b, nothing, lambda bq, c, qb: pe.wait_ge(sem["s_q"], bq + 1), self_round)
                pe.wait_ge(sem["s_out"], b.reg * (H * TB) + H * TB)
                token_to_feature(b, "attT1", att1)
                out_project(b, "wo1", att_T, w_o1, "attT1_sb")
                pe.wait_ge(*nth(b, "x1", TB - 1))
                token_to_feature(b, "x1T", x1)
                pe.wait_ge(*nth(b, "ctx_in"))
                for a in range(TB):
                    project_block(b, ("k2", 0, a), ctxT, a, w_k2, 2 * D)
                    project_block(b, ("v2", a), ctxT, a, w_v2, D)
                    project_block(b, ("q2", 0, a), xT2, a, w_q2, 2 * D)
                    pe.wait_ge(*nth(b, "q2_split", a))
                    transpose32(b, a, "2")
                pe.wait_ge(*nth(b, "k2_stacked", 2 * TB - 1))
                rounds(pe, b, nothing, lambda bq, c, qb: pe.wait_ge(sem["c_q"], bq + 1), cross_round)
                pe.wait_ge(*nth(b, "att2"))
                token_to_feature(b, "attT2", att2)
                out_project(b, "wo2", xT2, w_o2, "attT2_sb")
                pe.wait_ge(*nth(b, "x2", TB - 1))
                token_to_feature(b, "x2T", x2)
                score_row(b)
                for a in range(TB):
                    feed_forward(b, a)

            if_needed(pe, again)


def kernel(x, ctx_1024, mask_Bx16xSxS2_ff0, L0_attn_Wq_amp, L0_attn_Wk_amp, L0_attn_Wq_phi, L0_attn_Wk_phi, L0_attn_Wv,
           L0_attn_Wo, L0_attn_score_log_scale, L0_xattn_W_q, L0_xattn_W_k, L0_xattn_W_v, L0_xattn_W_o,
           L0_xattn_lambda_q1, L0_xattn_lambda_k1, L0_xattn_lambda_q2, L0_xattn_lambda_k2, L0_xattn_rms_scale,
           L0_ffn_w_router, L0_ffn_w_block):
    import concourse.bacc as bacc
    from concourse.bass_utils import run_bass_kernel_spmd

    def tr(a):
        a = np.asarray(a)
        return np.ascontiguousarray(np.swapaxes(a, -1, -2))

    def plain(a):
        return np.ascontiguousarray(np.asarray(a))

    half_rows = np.zeros((P, 2), np.float32)
    for p in range(P):
        half_rows[p, (p % F) // DH] = 1.0
    arrays = dict(
        x=plain(x), xT=tr(x), ctxT=tr(ctx_1024), mask=plain(mask_Bx16xSxS2_ff0),
        WqaT=tr(L0_attn_Wq_amp), WkaT=tr(L0_attn_Wk_amp), WqpT=tr(L0_attn_Wq_phi), WkpT=tr(L0_attn_Wk_phi),
        WvT=tr(L0_attn_Wv), WoT=tr(L0_attn_Wo), log_scale=plain(L0_attn_score_log_scale),
        xW_q=plain(L0_xattn_W_q), xW_k=plain(L0_xattn_W_k), xW_v=plain(L0_xattn_W_v), xW_o=plain(L0_xattn_W_o),
        lam4=np.stack([np.asarray(a).reshape(-1) for a in (L0_xattn_lambda_q1, L0_xattn_lambda_k1,
                                                           L0_xattn_lambda_q2, L0_xattn_lambda_k2)]),
        rms_tiled=np.tile(np.asarray(L0_xattn_rms_scale), P // DH).reshape(P, 1),
        half_rows=half_rows, w_router=plain(L0_ffn_w_router), w_block=plain(L0_ffn_w_block))
    nc = bacc.Bacc("TRN2", target_bir_lowering=False, num_devices=1)
    tensors = {n: nc.dram_tensor(f"{n}_dram", a.shape, mybir.dt.from_np(a.dtype), kind="ExternalInput").ap()
               for n, a in arrays.items()}
    tensors["out"] = nc.dram_tensor("out_dram", (B, S, D), mybir.dt.float32, kind="ExternalOutput").ap()
    build(nc, tensors)
    r = run_bass_kernel_spmd(nc, [{f"{n}_dram": a for n, a in arrays.items()}], core_ids=[0])
    return r.results[0]["out_dram"]
```
